# Optimizing a Trainium2 kernel written in Bass

```python
import numpy as np
import jax
import jax.numpy as jnp

def _softmax(x, axis=-1):
    return jax.nn.softmax(x, axis=axis)

def _gelu(x):
    return jax.nn.gelu(x, approximate=True)

def _silu(x):
    return jax.nn.silu(x)

def _sigmoid(x):
    return jax.nn.sigmoid(x)

def _layernorm(x, axis=-1, eps=1e-05):
    m = jnp.mean(x, axis=axis, keepdims=True)
    v = jnp.var(x, axis=axis, keepdims=True)
    return (x - m) / jnp.sqrt(v + eps)

def _scatter_add(tgt, idx, src, axis=0):
    return tgt.at[idx].add(src)

def _segment_sum(src, seg, n):
    return jax.ops.segment_sum(src, seg, n)
kernel_name = 'mk_seq_preln_d1_jaxref_r8_27af44'

def setup_inputs(seed: int=0):
    np.random.seed(seed)
    _w = jnp.asarray

    def _L0_attn_setup():
        import jax, jax.numpy as jnp
        import numpy as np
        D_MODEL = 128
        D_STATE = 16
        DT_RANK = 64
        BATCH = 4
        SEQ = 512

        def _selective_scan(x, delta, A, B, C):
            b, s, d = x.shape
            n = A.shape[1]
            h0 = jnp.zeros((b, d, n), dtype=x.dtype)

            def step(h, inp):
                x_t, dt_t, B_t, C_t = inp
                dA = jnp.exp(dt_t[:, :, None] * A[None, :, :])
                dB = dt_t[:, :, None] * B_t[:, None, :]
                h = h * dA + x_t[:, :, None] * dB
                y_t = jnp.einsum('bdn,bn->bd', h, C_t)
                return (h, y_t)
            xs = (jnp.swapaxes(x, 0, 1), jnp.swapaxes(delta, 0, 1), jnp.swapaxes(B, 0, 1), jnp.swapaxes(C, 0, 1))
            _, ys = jax.lax.scan(step, h0, xs)
            return jnp.swapaxes(ys, 0, 1)
        key = jax.random.key(seed)
        ks = jax.random.split(key, 6)
        x = jax.random.normal(ks[0], (BATCH, SEQ, D_MODEL), dtype=jnp.float32)
        W_xproj = jax.random.normal(ks[1], (DT_RANK + 2 * D_STATE, D_MODEL), dtype=jnp.float32) * (1.0 / np.sqrt(D_MODEL))
        W_dt = jax.random.normal(ks[2], (D_MODEL, DT_RANK), dtype=jnp.float32) * (1.0 / np.sqrt(DT_RANK))
        b_dt = jax.random.normal(ks[3], (D_MODEL,), dtype=jnp.float32) * 0.01
        A_log = jax.random.normal(ks[4], (D_MODEL, D_STATE), dtype=jnp.float32)
        D = jax.random.normal(ks[5], (D_MODEL,), dtype=jnp.float32)
        return {'x': x, 'W_xproj': W_xproj, 'W_dt': W_dt, 'b_dt': b_dt, 'A_log': A_log, 'D': D}
    _L0_attn_in = _L0_attn_setup()

    def _L0_ffn_setup():
        import jax, jax.numpy as jnp
        import numpy as np
        import math
        DMODEL = 128
        DFF = 512
        NUM_EXPERTS = 8
        TOPK = 2
        CAP_FACTOR = 1.25
        EPS = 1.1920929e-07

        def _trunc_normal(key, shape, fan_in, scale=1.0):
            std = scale * (1.0 / fan_in) ** 0.5
            return jax.random.truncated_normal(key, -2.0, 2.0, shape, jnp.float32) * std
        key = jax.random.key(seed)
        ks = jax.random.split(key, 5)
        return {'x': jax.random.normal(ks[0], (2, 256, DMODEL), jnp.float32), 'router_weight': _trunc_normal(ks[1], (NUM_EXPERTS, DMODEL), DMODEL), 'ff_pre_act_weight': _trunc_normal(ks[2], (NUM_EXPERTS, DFF, DMODEL), DMODEL), 'gate_weight': _trunc_normal(ks[3], (NUM_EXPERTS, DFF, DMODEL), DMODEL), 'ff_post_act_weight': _trunc_normal(ks[4], (NUM_EXPERTS, DMODEL, DFF), DFF)}
    _L0_ffn_in = _L0_ffn_setup()
    _d = {'L0_attn_x': _L0_attn_in['x'], 'L0_attn_W_xproj': _L0_attn_in['W_xproj'], 'L0_attn_W_dt': _L0_attn_in['W_dt'], 'L0_attn_b_dt': _L0_attn_in['b_dt'], 'L0_attn_A_log': _L0_attn_in['A_log'], 'L0_attn_D': _L0_attn_in['D'], 'L0_ffn_router_weight': _L0_ffn_in['router_weight'], 'L0_ffn_ff_pre_act_weight': _L0_ffn_in['ff_pre_act_weight'], 'L0_ffn_gate_weight': _L0_ffn_in['gate_weight'], 'L0_ffn_ff_post_act_weight': _L0_ffn_in['ff_post_act_weight']}
    _x0 = _d['L0_attn_x']
    _d['L0_attn_x'] = jax.random.normal(jax.random.fold_in(jax.random.key(seed), 1), (8, 256, 128), dtype=_x0.dtype)
    del _x0
    return _d

def reference(L0_attn_x, L0_attn_W_xproj, L0_attn_W_dt, L0_attn_b_dt, L0_attn_A_log, L0_attn_D, L0_ffn_router_weight, L0_ffn_ff_pre_act_weight, L0_ffn_gate_weight, L0_ffn_ff_post_act_weight):

    def _L0_attn_ref(x, W_xproj, W_dt, b_dt, A_log, D):
        import jax, jax.numpy as jnp
        import numpy as np
        D_MODEL = 128
        D_STATE = 16
        DT_RANK = 64
        BATCH = 4
        SEQ = 512

        def _selective_scan(x, delta, A, B, C):
            b, s, d = x.shape
            n = A.shape[1]
            h0 = jnp.zeros((b, d, n), dtype=x.dtype)

            def step(h, inp):
                x_t, dt_t, B_t, C_t = inp
                dA = jnp.exp(dt_t[:, :, None] * A[None, :, :])
                dB = dt_t[:, :, None] * B_t[:, None, :]
                h = h * dA + x_t[:, :, None] * dB
                y_t = jnp.einsum('bdn,bn->bd', h, C_t)
                return (h, y_t)
            xs = (jnp.swapaxes(x, 0, 1), jnp.swapaxes(delta, 0, 1), jnp.swapaxes(B, 0, 1), jnp.swapaxes(C, 0, 1))
            _, ys = jax.lax.scan(step, h0, xs)
            return jnp.swapaxes(ys, 0, 1)
        xp = jnp.einsum('bsd,pd->bsp', x, W_xproj)
        delta = jax.nn.softplus(jnp.einsum('bsr,dr->bsd', xp[..., :DT_RANK], W_dt) + b_dt)
        B = xp[..., DT_RANK:DT_RANK + D_STATE]
        C = xp[..., DT_RANK + D_STATE:]
        A = -jnp.exp(A_log)
        y = _selective_scan(x, delta, A, B, C)
        return y + x * D[None, None, :]

    def _L0_ffn_ref(x, router_weight, ff_pre_act_weight, gate_weight, ff_post_act_weight):
        import jax, jax.numpy as jnp
        import numpy as np
        import math
        DMODEL = 128
        DFF = 512
        NUM_EXPERTS = 8
        TOPK = 2
        CAP_FACTOR = 1.25
        EPS = 1.1920929e-07

        def _trunc_normal(key, shape, fan_in, scale=1.0):
            std = scale * (1.0 / fan_in) ** 0.5
            return jax.random.truncated_normal(key, -2.0, 2.0, shape, jnp.float32) * std
        orig_shape = x.shape
        h = x.reshape(-1, DMODEL)
        T = h.shape[0]
        logits = jnp.einsum('th,eh->te', h, router_weight)
        probs = jax.nn.softmax(logits.astype(jnp.float32), axis=-1)
        topk_probs, selected = jax.lax.top_k(probs, TOPK)
        topk_probs = topk_probs / jnp.maximum(topk_probs.sum(-1, keepdims=True), EPS)
        flat_tokens = jnp.repeat(jnp.arange(T), TOPK)
        flat_experts = selected.reshape(-1)
        flat_weights = topk_probs.reshape(-1)
        A = T * TOPK
        capacity = max(1, math.ceil(CAP_FACTOR * A / NUM_EXPERTS))
        weight_order = jnp.argsort(-flat_weights, stable=True)
        grouped_order = jnp.argsort(flat_experts[weight_order], stable=True)
        sort_order = weight_order[grouped_order]
        se = flat_experts[sort_order]
        st = flat_tokens[sort_order]
        sw = flat_weights[sort_order]
        counts = jnp.bincount(se, length=NUM_EXPERTS)
        offsets = jnp.cumsum(counts) - counts
        slot = jnp.arange(A) - offsets[se]
        keep = slot < capacity
        sw = jnp.where(keep, sw, 0.0)
        token_wsum = jnp.zeros(T, jnp.float32).at[st].add(sw)
        kept_w = sw / jnp.maximum(token_wsum[st], EPS)
        FC = NUM_EXPERTS * capacity
        dispatch = jnp.where(keep, se * capacity + slot, FC)
        expert_inputs = jnp.zeros((FC + 1, DMODEL), x.dtype).at[dispatch].set(h[st])
        expert_inputs = expert_inputs[:FC].reshape(NUM_EXPERTS, capacity, DMODEL)
        pre = jnp.einsum('ech,edh->ecd', expert_inputs, ff_pre_act_weight)
        gate = jnp.einsum('ech,edh->ecd', expert_inputs, gate_weight)
        expert_out = jnp.einsum('ecd,ehd->ech', pre * jax.nn.silu(gate), ff_post_act_weight)
        eo_flat = jnp.concatenate([expert_out.reshape(FC, DMODEL), jnp.zeros((1, DMODEL), x.dtype)], axis=0)
        updates = eo_flat[dispatch] * kept_w.astype(x.dtype)[:, None]
        out = jnp.zeros((T, DMODEL), x.dtype).at[st].add(updates)
        return out.reshape(orig_shape)
    x = L0_attn_x
    x = x + _L0_attn_ref(_layernorm(x, axis=-1), L0_attn_W_xproj, L0_attn_W_dt, L0_attn_b_dt, L0_attn_A_log, L0_attn_D)
    x = x + _L0_ffn_ref(_layernorm(x, axis=-1), L0_ffn_router_weight, L0_ffn_ff_pre_act_weight, L0_ffn_gate_weight, L0_ffn_ff_post_act_weight)
    return x

_drawn_inputs = setup_inputs


def setup_inputs(seed=0):
    import zlib

    import numpy as np

    out = dict(_drawn_inputs(seed))
    spreads = {}
    factors = {'L0_attn_b_dt': 8.0}
    for name, (base, spread) in spreads.items():
        noise = np.random.default_rng([zlib.crc32(name.encode()), seed]).standard_normal(out[name].shape)
        drawn = base * np.exp(spread * noise) if base else spread * noise
        out[name] = jnp.asarray(drawn.astype(out[name].dtype))
    for name, factor in factors.items():
        out[name] = (out[name] * factor).astype(out[name].dtype)
    return out
```

```python
from contextlib import ExitStack

import numpy as np

import concourse.bass as bass
from concourse import mybir

F32 = mybir.dt.float32
F32R = mybir.dt.float32r
BF16 = mybir.dt.bfloat16
I32 = mybir.dt.int32
ALU = mybir.AluOpType
ACT = mybir.ActivationFunctionType
AX = mybir.AxisListType

P = 128
BATCH, SEQ, D = 8, 256, 128
T = BATCH * SEQ
NT = T // P
NS = 16
GD = P // NS
NG = D // GD
RANK = 64
CH = 512
NC = T // CH
TPC = CH // P
BPC = CH // SEQ
UG = 2
UPC = NG // UG
RING = 4
LAG = 4

E = 8
DFF = 512
FC = DFF // P
CAP = 640
NQ = CAP // P
HALF = CAP // 2
EPS_LN = 1e-05
EPS_W = 1.1920929e-07
NROUND = 8
SHIFT = [26 - 4 * r for r in range(NROUND - 1)] + [0]

CONST = [("ident", P), ("ones", P), ("tri", P), ("blk", P), ("iota", P), ("wred", P + D - GD), ("dup", RANK),
         ("selcol", E), ("desc", NT * E), ("smask", E * NT), ("jval", E * NT), ("q5", NQ), ("pval", 1),
         ("spare", 1)]
COFF, _o = {}, 0
for _n, _w in CONST:
    COFF[_n] = (_o, _w)
    _o += _w
CW = _o


def shape_constants():
    p = np.arange(P)
    c = {
        "ident": np.eye(P),
        "ones": np.ones((P, P)),
        "tri": p[:, None] <= p[None, :],
        "blk": (p[:, None] // 16 == p[None, :] // 16) & (p[:, None] % 16 > 0),
        "iota": np.broadcast_to(p[None, :] + 1, (P, P)),
        "wred": (np.arange(P + D - GD)[None, :] == (D - GD) + p[:, None] % GD),
        "dup": p[:, None] % RANK == np.arange(RANK)[None, :],
        "selcol": p[:, None] == 16 * np.arange(E)[None, :],
        "desc": np.broadcast_to(E - np.arange(NT * E) % E, (P, NT * E)),
        "smask": np.broadcast_to(np.arange(E * NT) % NT > 0, (P, E * NT)),
        "jval": np.broadcast_to(P * (np.arange(E * NT) % NT), (P, E * NT)),
        "q5": np.broadcast_to(np.arange(NQ), (P, NQ)),
        "pval": p[:, None] + 1,
        "spare": T + p[:, None],
    }
    return np.concatenate([np.asarray(c[n], np.float32) for n, _ in CONST], axis=1)


def search_bits():
    j = (np.arange(P) % 16)[:, None]
    cols = [j << s for s in SHIFT[:-1]] + [np.where(j < 4, j, 0x40000000)]
    return np.concatenate(cols, axis=1).astype(np.int32)


def build(nc, x, wx, wdt, bdt, alog, dskip, wr, w1, wg, w2, consts, jbits, out, rows):
    with ExitStack() as ctx:
        def sb(name, shape, dt=F32):
            return ctx.enter_context(nc.sbuf_tensor(name, shape, dt))

        def sem(name):
            return ctx.enter_context(nc.semaphore(name))

        psum = ctx.enter_context(nc.psum_tensor("psum", [P, 8, CH], F32))

        cst = sb("cst", [P, CW])

        def cc(name):
            o, w = COFF[name]
            return cst[:, o:o + w]

        ident = cc("ident")
        jb = sb("jb", [P, NROUND], I32)
        wx_s = sb("wx_s", [P, RANK + 2 * NS])
        wdt_s = sb("wdt_s", [RANK, D])
        small = sb("small", [P, 2 + NG + E])
        bdt_s, dsk_s = small[:, 0:1], small[:, 1:2]
        alog_s, wr_s = small[:, 2:2 + NG], small[:, 2 + NG:2 + NG + E]
        nega = sb("nega", [P, NG])
        wred = cc("wred")
        sel_r = sb("sel_r", [P, P // GD // 2, NS, GD], F32R)
        wbc = sb("wbc", [P, 2, NS, GD])
        ones_b = sb("ones_b", [P, P], BF16)
        tri_b = sb("tri_b", [P, P], BF16)
        blk_b = sb("blk_b", [P, P], BF16)
        iota_b = sb("iota_b", [P, P], BF16)

        xt = sb("xt", [P, NT, D])
        xn = sb("xn", [P, NT, D])
        xnT = sb("xnT", [P, T])
        bbc = sb("bbc", [P, T])
        cbc = sb("cbc", [P, T])
        pre_a = sb("pre_a", [P, 2, CH])
        pre_b = sb("pre_b", [P, 2, CH])
        pre_c = sb("pre_c", [P, 2, CH])
        hi_d = sb("hi_d", [P, 2, CH], F32R)
        lo_d = sb("lo_d", [P, 2, CH], F32R)
        hi_x = sb("hi_x", [P, 2, CH], F32R)
        lo_x = sb("lo_x", [P, 2, CH], F32R)
        qd = sb("qd", [P, 2, T], F32R)
        qx = sb("qx", [P, 2, T], F32R)
        stat = sb("stat", [P, NT, 6])
        mv = sb("mv", [P, NT, 2])
        ve = sb("ve", [P, NT])
        lnv = sb("lnv", [P, NT])
        r0 = sb("r0", [P, NT])
        rt = sb("rt", [P, NT])
        rstd = sb("rstd", [P, NT])
        stat2 = sb("stat2", [P, TPC, 6])
        mv2 = sb("mv2", [P, TPC, 2])
        sm2 = sb("sm2", [P, 6, TPC])
        ring = sb("ring", [P, 4 * RING * UG * CH])
        da, uu, hh, hc = (ring[:, k * RING * UG * CH:(k + 1) * RING * UG * CH].rearrange(
            "p (r u n) -> p r u n", r=RING, u=UG) for k in range(4))
        xp_s = ring[0:RANK, 2 * RING * UG * CH:2 * RING * UG * CH + T]
        wmx = xnT[:].rearrange("p (j e r) -> p j e r", e=E, r=16)
        taken = [0]

        def later(*shape):
            n = int(np.prod(shape))
            o = taken[0]
            taken[0] += n
            assert taken[0] <= 4 * RING * UG * CH
            names = "abc"[:len(shape)]
            return ring[:, o:o + n].rearrange(f"p ({' '.join(names)}) -> p {' '.join(names)}",
                                              **dict(zip(names, shape)))
        y2 = sb("y2", [P, CH])
        x2T = sb("x2T", [P, CH])

        lg = sb("lg", [P, NT, E])
        rb = sb("rb", [P, 12, NT * E])
        r16 = sb("r16", [P, 10, NT])
        wm = sb("wm", [P, NT, E])
        cnt = sb("cnt", [P, NROUND])
        ind = sb("ind", [P, NROUND], BF16)
        base = sb("base", [P, NROUND + 1], I32)
        thr = sb("thr", [P, NROUND], I32)
        digs = sb("digs", [P, NROUND], I32)
        taud = sb("taud", [P, E])
        gt_b = sb("gt_b", [P, E, NT], BF16)
        eq_b = sb("eq_b", [P, E, NT], BF16)
        kp_b = sb("kp_b", [P, E, NT], BF16)
        lim = sb("lim", [P, 2, E])
        qq = sb("qq", [P, E * NT])
        r1 = sb("r1", [P, E * NT])
        vals = sb("vals", [P, 5, E * NT], BF16)

        w1_s = sb("w1_s", [P, 2, DFF])
        wg_s = sb("wg_s", [P, 2, DFF])
        w2_s = sb("w2_s", [P, 2, FC, D])
        oh = later(NT, P // 2).bitcast(BF16)
        q1 = sb("q1", [P, NT, NQ], BF16)
        rq = sb("rq", [P, 5, NT, NQ], BF16)
        tab = sb("tab", [P, E, 5 * NQ])
        tg = sb("tg", [P, 2, NQ])
        tk = sb("tk", [P, 4, NQ])
        gid = sb("gid", [P, 2, NQ], I32)
        sid = sb("sid", [P, 2, NQ], I32)
        kw = sb("kw", [P, 2, NQ])
        gx = later(2, NQ, D)
        xe = later(2, CAP)
        sg = later(2, HALF)
        hT = later(2, FC, CAP)
        ye = later(2, NQ, D)
        zero = sb("zero", [P, D])

        s_consts = sem("s_consts")
        s_weights = sem("s_weights")
        s_bits = sem("s_bits")
        s_spreaders = sem("s_spreaders")
        s_neg_a = sem("s_neg_a")
        s_pool_consts = sem("s_pool_consts")
        s_passed = sem("s_passed")
        s_dve = sem("s_dve")
        s_act = sem("s_act")
        s_pool = sem("s_pool")
        s_var = sem("s_var")
        s_rough_rstd = sem("s_rough_rstd")
        s_xn = sem("s_xn")
        s_xn_turned = sem("s_xn_turned")
        s_xnT = sem("s_xnT")
        s_xp_product = sem("s_xp_product")
        s_xp = sem("s_xp")
        s_bc_product = sem("s_bc_product")
        s_bc = sem("s_bc")
        s_z = sem("s_z")
        s_abs_z = sem("s_abs_z")
        s_log = sem("s_log")
        s_delta = sem("s_delta")
        s_high = sem("s_high")
        s_low = sem("s_low")
        s_delta_spread = sem("s_delta_spread")
        s_dx_spread = sem("s_dx_spread")
        s_decay = sem("s_decay")
        s_input = sem("s_input")
        s_state = sem("s_state")
        s_product = sem("s_product")
        s_summed = sem("s_summed")
        s_y = sem("s_y")
        s_y_turned = sem("s_y_turned")
        s_x2 = sem("s_x2")
        s_rough2 = sem("s_rough2")
        s_rstd2 = sem("s_rstd2")
        s_xn2 = sem("s_xn2")
        s_xn2_turned = sem("s_xn2_turned")
        s_xn2T = sem("s_xn2T")
        s_logits_product = sem("s_logits_product")
        s_logits = sem("s_logits")
        s_rows_stored = sem("s_rows_stored")
        s_out_stored = sem("s_out_stored")
        s_router = sem("s_router")
        s_exp = sem("s_exp")
        s_copied_dve = sem("s_copied_dve")
        s_copied_act = sem("s_copied_act")
        s_weights_turned = sem("s_weights_turned")
        s_indicator = sem("s_indicator")
        s_digit = sem("s_digit")
        s_tau_rows = sem("s_tau_rows")
        s_tau = sem("s_tau")
        s_above = sem("s_above")
        s_counted = sem("s_counted")
        s_keep = sem("s_keep")
        s_keep_counted = sem("s_keep_counted")
        s_one_hot = sem("s_one_hot")
        s_table = sem("s_table")
        s_gather_ids = sem("s_gather_ids")
        s_scatter_ids = sem("s_scatter_ids")
        s_rows_turned = sem("s_rows_turned")
        s_xe = sem("s_xe")
        s_up = sem("s_up")
        s_silu = sem("s_silu")
        s_hidden = sem("s_hidden")
        s_down = sem("s_down")
        s_weighed = sem("s_weighed")
        s_scattered = sem("s_scattered")
        s_x = [sem(f"s_x_chunk{c}") for c in range(NC)]
        s_stack = [sem(f"s_stack{c}") for c in range(NC)]
        s_expert_weights = [sem(f"s_expert_weights{b}") for b in range(2)]
        s_gathered = [[sem(f"s_gathered{b}{q}") for q in range(NQ)] for b in range(2)]

        blk = ctx.enter_context(nc.Block())
        xv = x.rearrange("(c j p) d -> c p j d", j=TPC, p=P)
        outv = out[0:T, :].rearrange("(c j p) d -> c p j d", j=TPC, p=P)
        rowv = rows.rearrange("(c j p) d -> c p j d", j=TPC, p=P)

        def bank(k, w=CH):
            return psum[:, k, 0:w]

        SPREAD_D, SPREAD_X, YB, TB, RB = 0, 2, 4, 5, 6

        def above_zero(value):
            return not isinstance(value, int) or value > 0

        def plain(eng):
            eng.sem_inc(s_passed, 1)

        class Chain:

            def __init__(self, eng, own):
                self.eng, self.own, self.n, self.base = eng, own, 0, 0

            def mark(self, ins):
                self.n += 1
                ins.then_inc(self.own, 1)

            def after(self):
                self.eng.wait_ge(self.own, self.base + self.n)

            def link(self, ins):
                self.mark(ins)
                self.after()

        @blk.sync
        def _(sp):
            nc.sync.dma_start(xt[:, 0:TPC, :], xv[0]).then_inc(s_x[0], 16)
            nc.sync.dma_start(cst[:], consts).then_inc(s_consts, 16)
            nc.sync.dma_start(small[:], dskip).then_inc(s_weights, 16)
            nc.sync.dma_start(wx_s[:], wx).then_inc(s_weights, 16)
            nc.sync.dma_start(wdt_s[:], wdt).then_inc(s_weights, 16)
            for c in range(1, NC):
                nc.sync.dma_start(xt[:, TPC * c:TPC * (c + 1), :], xv[c]).then_inc(s_x[c], 16)
            nc.sync.dma_start(jb[:], jbits).then_inc(s_bits, 16)
            for c in range(NC):
                cs = slice(c * CH, (c + 1) * CH)
                for k, (hi, lo, q) in enumerate(((hi_d, lo_d, qd), (hi_x, lo_x, qx))):
                    sp.wait_ge(s_high, 2 * c + k + 1)
                    sp.wait_ge(s_low, 2 * c + k + 1)
                    for half in range(2):
                        src = slice(64 * half, 64 * half + 64)
                        nc.sync.dma_start(q[0:64, half, cs].bitcast(F32), hi[src, c % 2, :].bitcast(F32)).then_inc(s_stack[c], 16)
                        nc.sync.dma_start(q[64:128, half, cs].bitcast(F32), lo[src, c % 2, :].bitcast(F32)).then_inc(s_stack[c], 16)
            sp.wait_ge(s_pool_consts, 1)
            nc.sync.dma_start(out[T:T + P, :], zero[:]).then_inc(s_out_stored, 16)
            for e in range(2):
                nc.sync.dma_start(w1_s[:, e, :], w1[e]).then_inc(s_expert_weights[e], 16)
                nc.sync.dma_start(wg_s[:, e, :], wg[e]).then_inc(s_expert_weights[e], 16)
                nc.sync.dma_start(w2_s[:, e, :, :], w2[e]).then_inc(s_expert_weights[e], 16)
            with sp.Fori(0, NC) as c:
                sp.wait_ge(s_x2, c + 1)
                nc.sync.dma_start(outv[c], xt[:, bass.ts(c, TPC), :]).then_inc(s_out_stored, 16)
                sp.wait_ge(s_xn2, TPC * c + TPC)
                nc.sync.dma_start(rowv[c], xn[:, 0:TPC, :]).then_inc(s_rows_stored, 16)
            with sp.Fori(0, E // 2 - 1) as i:
                for b in range(2):
                    sp.wait_ge(s_down, 2 * i + (b + 1))
                    nc.sync.dma_start(w1_s[:, b, :], w1[2 * i + (2 + b)]).then_inc(s_expert_weights[b], 16)
                    nc.sync.dma_start(wg_s[:, b, :], wg[2 * i + (2 + b)]).then_inc(s_expert_weights[b], 16)
                    nc.sync.dma_start(w2_s[:, b, :, :], w2[2 * i + (2 + b)]).then_inc(s_expert_weights[b], 16)
            sp.wait_ge(s_out_stored, 16 * (NC + 1))
            sp.wait_ge(s_rows_stored, 16 * NC)
            sp.wait_ge(s_scattered, 16 * E * NQ)

        def newton(dve, ch, v, r, t, o):
            ch.link(nc.vector.tensor_tensor(t, r, r, ALU.mult))
            ch.link(nc.vector.tensor_tensor(t, t, v, ALU.mult))
            ch.link(nc.vector.tensor_scalar(t, t, -0.5, 1.5, ALU.mult, ALU.add))
            return nc.vector.tensor_tensor(o, r, t, ALU.mult)

        @blk.vector
        def _(dve):
            ch = Chain(dve, s_dve)
            v = nc.vector
            for j in range(NT):
                if j % TPC == 0:
                    dve.wait_ge(s_x[j // TPC], 16)
                ch.mark(v.bn_stats(stat[:, j, :], xt[:, j, :]))
            ch.after()
            for j in range(NT):
                ch.mark(v.bn_aggr(mv[:, j, :], stat[:, j, :]))
            ch.after()
            v.tensor_scalar(ve[:], mv[:, :, 1], EPS_LN, None, ALU.add).then_inc(s_var, 1)
            dve.wait_ge(s_var, 1)
            dve.wait_ge(s_rough_rstd, 1)
            ch.link(newton(dve, ch, ve[:], r0[:], rt[:], rstd[:]))
            for j in range(NT):
                v.tensor_scalar(xn[:, j, :], xt[:, j, :], mv[:, j, 0:1], rstd[:, j:j + 1], ALU.subtract,
                                ALU.mult).then_inc(s_xn, 1)
            dve.wait_ge(s_weights, 48)
            for c in range(NC):
                dve.wait_ge(s_abs_z, c + 1)
                if c >= 2:
                    if above_zero(2 * (c - 1)):
                        dve.wait_ge(s_low, 2 * (c - 1))
                    if above_zero(2 * (c - 1)):
                        dve.wait_ge(s_high, 2 * (c - 1))
                ch.link(v.tensor_scalar(pre_b[:, c % 2, :], bank(c), bdt_s, 0.0, ALU.add, ALU.max))
                dve.wait_ge(s_log, c + 1)
                v.tensor_tensor(pre_b[:, c % 2, :], pre_b[:, c % 2, :], pre_a[:, c % 2, :], ALU.add).then_inc(s_delta, 1)
                dve.wait_ge(s_delta, 2 * c + 1)
                dve.wait_ge(s_xnT, c + 1)
                v.tensor_tensor(pre_c[:, c % 2, :], pre_b[:, c % 2, :], xnT[:, c * CH:(c + 1) * CH],
                                ALU.mult).then_inc(s_delta, 1)
            dve.wait_ge(s_bc, 2 * NC)

            def u_step(c, vv):
                for k in range(UG):
                    n, m = c * UPC + vv, c * NG + (UG * vv + k)
                    dve.wait_ge(s_dx_spread, m + 1)
                    if k == 0 and above_zero(n - (RING - 1)):
                        dve.wait_ge(s_state, n - (RING - 1))
                    v.tensor_tensor(uu[:, vv % RING, k, :], bank(SPREAD_X + k), bbc[:, bass.ts(c, CH)],
                                    ALU.mult).then_inc(s_input, 1)

            def scan_step(c, vv):
                n, s = c * UPC + vv, vv % RING
                dve.wait_ge(s_input, n * UG + UG)
                dve.wait_ge(s_decay, n * UG + UG)
                if above_zero(n - (RING - 1)):
                    dve.wait_ge(s_product, n - (RING - 1))
                v.tensor_tensor_scan(hh[:, s].rearrange("p a b -> p (a b)"), da[:, s].rearrange("p a b -> p (a b)"),
                                     uu[:, s].rearrange("p a b -> p (a b)"), 0.0, ALU.mult, ALU.add).then_inc(s_state, 1)

            def post(c, step):
                if step == 0:
                    dve.wait_ge(s_summed, c * UPC + UPC)
                    v.scalar_tensor_tensor(y2[:], xnT[:, bass.ts(c, CH)], dsk_s, bank(YB), ALU.mult,
                                           ALU.add).then_inc(s_y, 1)
                elif step == 1:
                    dve.wait_ge(s_y_turned, c + 1)
                    ch.link(v.tensor_tensor(xt[:, bass.ts(c, TPC), :], xt[:, bass.ts(c, TPC), :],
                                            bank(TB).rearrange("p (j d) -> p j d", d=D), ALU.add))
                    plain(dve)
                    for j in range(TPC):
                        ch.mark(v.bn_stats(stat2[:, j, :], xt[:, TPC * c + j, :]))
                    ch.after()
                    plain(dve)
                    for j in range(TPC):
                        ch.mark(v.bn_aggr(mv2[:, j, :], stat2[:, j, :]))
                    ch.after()
                    v.tensor_scalar(sm2[:, 0, :], mv2[:, :, 1], EPS_LN, None, ALU.add).then_inc(s_x2, 1)
                elif step == 2:
                    dve.wait_ge(s_rough2, c + 1)
                    ch.link(newton(dve, ch, sm2[:, 0, :], sm2[:, 2, :], sm2[:, 3, :], sm2[:, 4, :]))
                    v.scalar_tensor_tensor(sm2[:, 5, :], mv2[:, :, 0], -1.0, sm2[:, 4, :], ALU.mult,
                                           ALU.mult).then_inc(s_rstd2, 1)

            def chunk(c, first):
                for vv in range(UPC):
                    u_step(c, vv)
                    if vv:
                        scan_step(c, vv - 1)
                    elif not first:
                        scan_step(c - 1, UPC - 1)
                    if not first and vv >= LAG:
                        post(c - 1, vv - LAG)

            chunk(0, True)
            old = ch.base + ch.n
            PER = 1 + 2 * TPC + 4
            with dve.Fori(1, NC) as c:
                ch.base, ch.n = old + (c - 1) * PER, 0
                chunk(c, False)
                assert ch.n == PER, ch.n
            ch.base, ch.n = old + (NC - 1) * PER, 0
            scan_step(NC - 1, UPC - 1)
            for step in range(3):
                post(NC - 1, step)

            R = [rb[:, k, :].rearrange("p (j e) -> p j e", e=E) for k in range(12)]

            def w16(k):
                return r16[:, k, :]

            def over(a):
                return a.unsqueeze(2).to_broadcast([P, NT, E])

            desc = cc("desc").rearrange("p (j e) -> p j e", e=E)
            dve.wait_ge(s_logits, NC)
            ch.link(v.tensor_reduce(w16(0), lg[:], AX.X, ALU.max))
            v.tensor_tensor(R[0], lg[:], over(w16(0)), ALU.subtract).then_inc(s_router, 1)
            dve.wait_ge(s_exp, 1)
            ch.link(v.tensor_reduce(w16(1), R[1], AX.X, ALU.add))
            ch.link(v.reciprocal(w16(2), w16(1)))
            ch.link(v.tensor_tensor(R[2], R[1], over(w16(2)), ALU.mult))

            def first_largest(src, top, tmp, tmp16, mask):
                ch.link(v.tensor_reduce(top, src, AX.X, ALU.max))
                ch.link(v.tensor_tensor(tmp, src, over(top), ALU.is_equal))
                ch.link(v.tensor_tensor(tmp, tmp, desc, ALU.mult))
                ch.link(v.tensor_reduce(tmp16, tmp, AX.X, ALU.max))
                ch.link(v.tensor_tensor(mask, tmp, over(tmp16), ALU.is_equal))

            first_largest(R[2], w16(3), R[3], w16(4), R[4])
            ch.link(v.scalar_tensor_tensor(R[5], R[4], -2.0, R[2], ALU.mult, ALU.add))
            first_largest(R[5], w16(5), R[3], w16(4), R[6])
            ch.link(v.tensor_tensor(w16(6), w16(3), w16(5), ALU.add))
            ch.link(v.tensor_scalar(w16(6), w16(6), EPS_W, None, ALU.max))
            ch.link(v.reciprocal(w16(7), w16(6)))
            ch.mark(v.tensor_tensor(w16(8), w16(3), w16(7), ALU.mult))
            ch.link(v.tensor_tensor(w16(9), w16(5), w16(7), ALU.mult))
            ch.mark(v.tensor_tensor(R[7], R[4], over(w16(8)), ALU.mult))
            ch.link(v.tensor_tensor(R[8], R[6], over(w16(9)), ALU.mult))
            ch.mark(v.tensor_tensor(R[9], R[4], R[6], ALU.add))
            ch.link(v.tensor_tensor(R[8], R[7], R[8], ALU.add))
            v.scalar_tensor_tensor(wm[:], R[9], -1.0, R[8], ALU.add, ALU.add).then_inc(s_router, 1)
            dve.wait_ge(s_router, 2)
            for k in (0, 2):
                js = slice(4 * k, 4 * k + 4)
                v.tensor_copy(wmx[:, js], wm[:, js].unsqueeze(3).to_broadcast([P, 4, E, 16])).then_inc(s_copied_dve, 1)

            dve.wait_ge(s_weights_turned, 1)
            junk = bbc[:]
            allw = psum[:, 0:4, :].rearrange("p b n -> p (b n)")
            dve.wait_ge(s_pool_consts, 2)
            dve.wait_ge(s_bits, 16)
            for r in range(NROUND):
                edge = jb[:, 0:1] if r == 0 else thr[:, r:r + 1]
                ch.link(v.tensor_scalar(junk, allw, edge.bitcast(F32), None, ALU.is_ge, ALU.add,
                                        accum_out=cnt[:, r:r + 1]))
                v.tensor_scalar(ind[:, r:r + 1], cnt[:, r:r + 1], float(CAP), None, ALU.is_ge).then_inc(s_indicator, 1)
                dve.wait_ge(s_digit, r + 1)
                ch.link(v.tensor_scalar(digs[:, r:r + 1], psum[:, 4, r:r + 1], float(1 << SHIFT[r]), None, ALU.mult))
                ch.link(v.tensor_tensor(base[:, r + 1:r + 2], digs[:, r:r + 1], base[:, r:r + 1], ALU.bitwise_or))
                if r + 1 < NROUND:
                    ch.link(v.tensor_tensor(thr[:, r + 1:r + 2], base[:, r + 1:r + 2], jb[:, r + 1:r + 2], ALU.bitwise_or))
            v.tensor_scalar(taud[:], cc("selcol"), base[:, NROUND:].bitcast(F32), None, ALU.mult).then_inc(s_tau_rows, 1)

            wv = wm[:].rearrange("p j e -> p e j")
            dve.wait_ge(s_tau, 1)
            tau = psum[:, 4, 32:32 + E].unsqueeze(2).to_broadcast([P, E, NT])
            v.tensor_tensor(gt_b[:], wv, tau, ALU.is_gt).then_inc(s_above, 1)
            v.tensor_tensor(eq_b[:], wv, tau, ALU.is_equal).then_inc(s_above, 1)

            def ej(a):
                return a.rearrange("p (e j) -> p e j", j=NT)

            def running(tot, within, a, b, o):
                ch.link(v.tensor_tensor_scan(rb[:, a, :], cc("smask"), tot, 0.0, ALU.mult, ALU.add))
                ch.link(v.tensor_tensor(rb[:, b, :], rb[:, a, :], tot, ALU.subtract))
                ch.link(v.tensor_tensor(rb[:, o, :], rb[:, b, :], within, ALU.add))

            dve.wait_ge(s_counted, 1)
            ch.link(v.tensor_reduce(lim[:, 0, :], ej(bank(5, P)), AX.X, ALU.add))
            ch.link(v.tensor_scalar(lim[:, 1, :], lim[:, 0, :], -1.0, float(CAP), ALU.mult, ALU.add))
            running(bank(6, P), bank(7, P), 0, 1, 2)
            ch.link(v.tensor_tensor(ej(rb[:, 3, :]), ej(rb[:, 2, :]), lim[:, 1, :].unsqueeze(2).to_broadcast([P, E, NT]),
                                    ALU.is_le))
            ch.link(v.tensor_tensor(ej(rb[:, 4, :]), ej(rb[:, 3, :]), eq_b[:], ALU.mult))
            v.tensor_tensor(kp_b[:], ej(rb[:, 4, :]), gt_b[:], ALU.add).then_inc(s_keep, 1)
            dve.wait_ge(s_keep, 1)
            ch.link(v.tensor_tensor(ej(rb[:, 5, :]), kp_b[:], wv, ALU.mult))
            ch.link(v.tensor_reduce(w16(0), ej(rb[:, 5, :]).rearrange("p e j -> p j e"), AX.X, ALU.add))
            ch.link(v.tensor_scalar(w16(0), w16(0), EPS_W, None, ALU.max))
            ch.link(v.reciprocal(w16(1), w16(0)))
            ch.link(v.tensor_tensor(ej(rb[:, 6, :]), ej(rb[:, 5, :]), r16[:, 1:2, :].to_broadcast([P, E, NT]), ALU.mult))
            ch.link(v.tensor_copy(vals[:, 2, :], rb[:, 6, :]))
            ch.link(v.tensor_tensor(rb[:, 7, :], rb[:, 6, :], vals[:, 2, :], ALU.subtract))
            ch.link(v.tensor_copy(vals[:, 3, :], rb[:, 7, :]))
            ch.link(v.tensor_tensor(vals[:, 4, :], rb[:, 7, :], vals[:, 3, :], ALU.subtract))
            dve.wait_ge(s_keep_counted, 1)
            running(bank(6, P), bank(7, P), 0, 1, 2)
            ch.link(v.tensor_tensor(ej(rb[:, 8, :]), ej(rb[:, 2, :]), kp_b[:], ALU.mult))
            ch.link(v.tensor_scalar(qq[:], rb[:, 8, :], float(P), None, ALU.is_gt))
            for k in range(2, NQ):
                ch.link(v.scalar_tensor_tensor(qq[:], rb[:, 8, :], float(k * P), qq[:], ALU.is_gt, ALU.add))
            ch.link(v.scalar_tensor_tensor(r1[:], qq[:], -float(P), rb[:, 8, :], ALU.mult, ALU.add))

            def one_hot(e, j):
                return v.tensor_scalar(oh[:, j, :], iota_b[:], r1[:, bass.ds(e * NT + j, 1)], None, ALU.is_equal)

            def columns(e):
                ch.link(v.tensor_tensor(q1[:], qq[:, bass.ts(e, NT)].unsqueeze(2).to_broadcast([P, NT, NQ]),
                                        cc("q5").rearrange("p (o q) -> p o q", o=1).to_broadcast([P, NT, NQ]), ALU.is_equal))
                for k in range(5):
                    last = v.tensor_tensor(rq[:, k], q1[:], vals[:, k, bass.ts(e, NT)].unsqueeze(2).to_broadcast([P, NT, NQ]),
                                           ALU.mult)
                last.then_inc(s_one_hot, 1)

            def gather_rows(e, b):
                dve.wait_ge(s_table, e + 1)
                if above_zero(2 * (e - 1)):
                    dve.wait_ge(s_rows_turned, 2 * (e - 1))
                tb = tab[:, bass.ds(e, 1), :].rearrange("p o n -> p (o n)")
                ch.link(v.tensor_copy(tb, psum[:, 7, 0:5 * NQ]))
                ch.mark(v.tensor_scalar(tg[:, 0, :], tb[:, 0:NQ], 0.0, None, ALU.is_gt))
                ch.link(v.tensor_tensor(tg[:, 1, :], tb[:, 0:NQ], tb[:, NQ:2 * NQ], ALU.add))
                v.tensor_tensor(gid[:, b, :], tg[:, 1, :], tg[:, 0, :], ALU.subtract).then_inc(s_gather_ids, 1)

            def scatter_rows(e, b):
                if above_zero(NQ * (e - 1)):
                    dve.wait_ge(s_weighed, NQ * (e - 1))
                if above_zero(16 * NQ * (e - 1)):
                    dve.wait_ge(s_scattered, 16 * NQ * (e - 1))
                tb = tab[:, bass.ds(e, 1), :].rearrange("p o n -> p (o n)")
                ch.mark(v.tensor_scalar(tk[:, 0, :], tb[:, 0:NQ], 0.0, None, ALU.is_gt))
                ch.mark(v.tensor_tensor(tk[:, 1, :], tb[:, 0:NQ], tb[:, NQ:2 * NQ], ALU.add))
                ch.link(v.tensor_tensor(tk[:, 3, :], tb[:, 2 * NQ:3 * NQ], tb[:, 3 * NQ:4 * NQ], ALU.add))
                ch.mark(v.tensor_tensor(kw[:, b, :], tb[:, 4 * NQ:5 * NQ], tk[:, 3, :], ALU.add))
                ch.link(v.scalar_tensor_tensor(tk[:, 2, :], tk[:, 0, :], cc("spare"), tk[:, 0, :], ALU.mult, ALU.add))
                ch.link(v.tensor_tensor(tk[:, 2, :], tk[:, 1, :], tk[:, 2, :], ALU.subtract))
                v.tensor_scalar(sid[:, b, :], tk[:, 2, :], cc("spare"), None, ALU.add).then_inc(s_scatter_ids, 1)

            def expert(e, b, more):
                scatter_rows(e, b)
                if more:
                    dve.wait_ge(s_table, e + 2)
                for un in range(2 * FC):
                    half, f = un // FC, un % FC
                    dve.wait_ge(s_silu, e * (2 * FC) + (un + 1))
                    if un == 0:
                        if above_zero(e - 1):
                            dve.wait_ge(s_down, e - 1)
                    v.tensor_tensor(hT[:, b, f, half * HALF:(half + 1) * HALF], psum[:, un % 2, 0:HALF],
                                    sg[:, un % 2, :], ALU.mult).then_inc(s_hidden, 1)
                    if more and un < FC:
                        for j in range(un * NT // FC, (un + 1) * NT // FC):
                            one_hot(e + 2, j)
                    elif more and un == FC:
                        columns(e + 2)
                if more:
                    gather_rows(e + 2, b)

            ch.after()
            for e in range(2):
                if above_zero(e):
                    dve.wait_ge(s_table, e)
                for j in range(NT):
                    one_hot(e, j)
                columns(e)
                gather_rows(e, e)
            expert(0, 0, True)
            expert(1, 1, True)
            old = ch.base + ch.n
            PER = 2 * (6 + 1 + 3)
            with dve.Fori(1, E // 2 - 1) as i:
                ch.base, ch.n = old + (i - 1) * PER, 0
                for b in range(2):
                    expert(2 * i + b, b, True)
                assert ch.n == PER, ch.n
            ch.base, ch.n = old + (E // 2 - 2) * PER, 0
            expert(E - 2, 0, False)
            expert(E - 1, 1, False)

        @blk.scalar
        def _(act):
            a = nc.scalar
            ch = Chain(act, s_act)
            act.wait_ge(s_consts, 16)
            a.activation(sel_r[:], cc("dup").rearrange("p (g o d) -> p g o d", o=1, d=GD).to_broadcast(
                [P, P // GD // 2, NS, GD]), ACT.Copy).then_inc(s_spreaders, 1)
            act.wait_ge(s_weights, 48)
            a.activation(nega[:], alog_s, ACT.Exp).then_inc(s_neg_a, 1)
            for k in range(2):
                a.activation(wbc[:, k], wx_s[:, RANK + NS * k:RANK + NS * (k + 1)].unsqueeze(2).to_broadcast([P, NS, GD]),
                             ACT.Copy).then_inc(s_spreaders, 1)
            act.wait_ge(s_var, 1)
            ch.link(a.activation(lnv[:], ve[:], ACT.Ln))
            a.activation(r0[:], lnv[:], ACT.Exp, scale=-0.5).then_inc(s_rough_rstd, 1)
            for c in range(NC):
                act.wait_ge(s_xn_turned, c + 1)
                a.activation(xnT[:, c * CH:(c + 1) * CH], bank(c), ACT.Copy).then_inc(s_xnT, 1)
            for c in range(NC):
                cs = slice(c * CH, (c + 1) * CH)
                act.wait_ge(s_xp_product, c + 1)
                a.activation(xp_s[:, cs], psum[0:RANK, 4 + c % 2, :], ACT.Copy).then_inc(s_xp, 1)
                act.wait_ge(s_z, c + 1)
                if c >= 2:
                    if above_zero(2 * (c - 2) + 1):
                        act.wait_ge(s_delta, 2 * (c - 2) + 1)
                a.activation(pre_a[:, c % 2, :], bank(c), ACT.Abs, bias=bdt_s).then_inc(s_abs_z, 1)
                act.wait_ge(s_abs_z, c + 1)
                ch.link(a.activation(pre_a[:, c % 2, :], pre_a[:, c % 2, :], ACT.Exp, scale=-1.0))
                a.activation(pre_a[:, c % 2, :], pre_a[:, c % 2, :], ACT.Ln, bias=1.0).then_inc(s_log, 1)
                for k, (dst, src) in enumerate(((hi_d, pre_b), (hi_x, pre_c))):
                    act.wait_ge(s_delta, 2 * c + 1 + k)
                    if c >= 2:
                        act.wait_ge(s_stack[c - 2], 16 * 8)
                    a.activation(dst[:, c % 2, :], src[:, c % 2, :], ACT.Copy).then_inc(s_high, 1)
                for k, dst in enumerate((bbc, cbc)):
                    act.wait_ge(s_bc_product, 2 * c + k + 1)
                    a.activation(dst[:, cs], bank(6 + k), ACT.Copy).then_inc(s_bc, 1)
            act.wait_ge(s_neg_a, 2)
            act.wait_ge(s_pool_consts, 2)

            def decay(c, vv):
                for k in range(UG):
                    n, m = c * UPC + vv, c * NG + (UG * vv + k)
                    g = UG * vv + k
                    act.wait_ge(s_delta_spread, m + 1)
                    if k == 0 and above_zero(n - (RING - 1)):
                        act.wait_ge(s_state, n - (RING - 1))
                    src = bank(SPREAD_D + k).rearrange("p (b s) -> p b s", s=SEQ)
                    dst = da[:, vv % RING, k, :].rearrange("p (b s) -> p b s", s=SEQ)
                    a.activation(dst[:, :, 1:], src[:, :, 1:], ACT.Exp, scale=nega[:, g:g + 1]).then_inc(s_decay, 1)

            def post(c, step):
                if step == 1:
                    act.wait_ge(s_x2, c + 1)
                    ch.link(a.activation(sm2[:, 1, :], sm2[:, 0, :], ACT.Ln))
                    a.activation(sm2[:, 2, :], sm2[:, 1, :], ACT.Exp, scale=-0.5).then_inc(s_rough2, 1)
                elif step == 2:
                    act.wait_ge(s_rstd2, c + 1)
                    if above_zero(16 * c):
                        act.wait_ge(s_rows_stored, 16 * c)
                    if above_zero(c):
                        act.wait_ge(s_xn2_turned, c)
                    for j in range(TPC):
                        a.activation(xn[:, j, :], xt[:, TPC * c + j, :], ACT.Identity, bias=sm2[:, 5, j:j + 1],
                                     scale=sm2[:, 4, j:j + 1]).then_inc(s_xn2, 1)
                elif step == 3:
                    act.wait_ge(s_xn2_turned, c + 1)
                    a.activation(x2T[:], bank(TB), ACT.Copy).then_inc(s_xn2T, 1)
                    act.wait_ge(s_logits_product, c + 1)
                    a.activation(lg[:, bass.ts(c, TPC), :], psum[:, RB, 0:TPC * E].rearrange("p (j e) -> p j e", e=E),
                                 ACT.Copy).then_inc(s_logits, 1)

            def chunk(c, first):
                for vv in range(UPC):
                    decay(c, vv)
                    if not first and vv >= LAG:
                        post(c - 1, vv - LAG)

            chunk(0, True)
            old = ch.base + ch.n
            with act.Fori(1, NC) as c:
                ch.base, ch.n = old + (c - 1), 0
                chunk(c, False)
            ch.base, ch.n = old + NC - 1, 0
            for step in range(4):
                post(NC - 1, step)
            act.wait_ge(s_router, 1)
            a.activation(rb[:, 1, :], rb[:, 0, :], ACT.Exp).then_inc(s_exp, 1)

            act.wait_ge(s_router, 2)
            for k in (1, 3):
                js = slice(4 * k, 4 * k + 4)
                a.activation(wmx[:, js], wm[:, js].unsqueeze(3).to_broadcast([P, 4, E, 16]), ACT.Copy).then_inc(s_copied_act, 1)

            def spread_tokens(e, b):
                if above_zero((e - 1) * 2 * FC):
                    act.wait_ge(s_up, (e - 1) * 2 * FC)
                act.wait_ge(s_rows_turned, 2 * e + 1)
                a.activation(xe[:, b, 0:CH], bank(4), ACT.Copy).then_inc(s_xe, 1)
                act.wait_ge(s_rows_turned, 2 * e + 2)
                a.activation(xe[:, b, CH:CAP], bank(6, CAP - CH), ACT.Copy).then_inc(s_xe, 1)

            def gates(e, b):
                for un in range(2 * FC):
                    g = e * (2 * FC) + un
                    act.wait_ge(s_up, g + 1)
                    if above_zero(g - 1):
                        act.wait_ge(s_hidden, g - 1)
                    a.activation(sg[:, un % 2, :], psum[:, 2 + un % 2, 0:HALF], ACT.Silu).then_inc(s_silu, 1)

            def weigh(e, b):
                act.wait_ge(s_down, e + 1)
                if above_zero(16 * NQ * (e - 1)):
                    act.wait_ge(s_scattered, 16 * NQ * (e - 1))
                for q in range(NQ):
                    a.activation(ye[:, b, q, :], psum[:, 5 + q // 4, (q % 4) * P:(q % 4 + 1) * P], ACT.Copy,
                                 scale=kw[:, b, q:q + 1]).then_inc(s_weighed, 1)

            def expert(e, b, more=True):
                gates(e, b)
                if more:
                    spread_tokens(e + 1, 1 - b)
                weigh(e, b)

            spread_tokens(0, 0)
            expert(0, 0)
            expert(1, 1)
            with act.Fori(1, E // 2 - 1) as i:
                for b in range(2):
                    expert(2 * i + b, b)
            expert(E - 2, 0)
            expert(E - 1, 1, False)

        @blk.gpsimd
        def _(pool):
            g = nc.gpsimd
            g.memset(zero[:], 0.0).then_inc(s_pool_consts, 1)
            g.memset(da.rearrange("p r u (b s) -> p (r u b) s", s=SEQ)[:, :, 0:1], 0.0).then_inc(s_pool, 1)
            g.memset(base[:, 0:1], 0).then_inc(s_pool, 1)
            pool.wait_ge(s_pool, 2)
            pool.wait_ge(s_consts, 16)
            for dst, src in ((ones_b, "ones"), (tri_b, "tri"), (blk_b, "blk"), (iota_b, "iota")):
                g.tensor_copy(dst[:], cc(src)).then_inc(s_pool, 1)
            g.tensor_tensor(vals[:, 0, :], cc("ones")[:, 0:E * NT], cc("pval").to_broadcast([P, E * NT]),
                            ALU.mult).then_inc(s_pool, 1)
            g.tensor_copy(vals[:, 1, :], cc("jval")).then_inc(s_pool_consts, 1)
            pool.wait_ge(s_neg_a, 1)
            g.tensor_scalar(nega[:], nega[:], -1.0, 0.0, ALU.mult, ALU.add).then_inc(s_neg_a, 1)
            for c in range(NC):
                for k, (dst, full, hi) in enumerate(((lo_d, pre_b, hi_d), (lo_x, pre_c, hi_x))):
                    pool.wait_ge(s_high, 2 * c + k + 1)
                    if c >= 2:
                        pool.wait_ge(s_stack[c - 2], 16 * 8)
                    g.tensor_tensor(dst[:, c % 2, :], full[:, c % 2, :], hi[:, c % 2, :].bitcast(F32),
                                    ALU.subtract).then_inc(s_low, 1)

            def product(c, vv):
                n, s = c * UPC + vv, vv % RING
                pool.wait_ge(s_state, n + 1)
                if above_zero(n - (RING - 1)):
                    pool.wait_ge(s_summed, n - (RING - 1))
                plain(pool)
                cb = cbc[:, bass.ts(c, CH)].rearrange("p (o n) -> p o n", o=1).to_broadcast([P, UG, CH])
                g.tensor_tensor(hc[:, s], hh[:, s], cb, ALU.mult).then_inc(s_product, 1)

            for vv in range(UPC):
                product(0, vv)
            with pool.Fori(1, NC) as c:
                for vv in range(UPC):
                    product(c, vv)

            def gather_ready(e, b):
                pool.wait_ge(s_gather_ids, e + 1)
                if above_zero(2 * (e - 1)):
                    pool.wait_ge(s_rows_turned, 2 * (e - 1))
                plain(pool)

            def gather(b, q):
                g.indirect_dma_start(out=gx[:, b, q, :], out_offset=None, in_=rows,
                                     in_offset=bass.IndirectOffsetOnAxis(ap=gid[:, b, q:q + 1], axis=0)
                                     ).then_inc(s_gathered[b][q], 16)

            def expert(e, b, more=True):
                pool.wait_ge(s_scatter_ids, e + 1)
                for q in range(NQ):
                    pool.wait_ge(s_weighed, NQ * e + q + 1)
                    if above_zero(16 * (NQ * e + q)):
                        pool.wait_ge(s_scattered, 16 * (NQ * e + q))
                    plain(pool)
                    g.indirect_dma_start(out=out, out_offset=bass.IndirectOffsetOnAxis(ap=sid[:, b, q:q + 1], axis=0),
                                         in_=ye[:, b, q, :], in_offset=None, compute_op=ALU.add
                                         ).then_inc(s_scattered, 16)
                    if more:
                        if q == 0:
                            gather_ready(e + 2, b)
                        gather(b, q)

            pool.wait_ge(s_rows_stored, 16 * NC)
            pool.wait_ge(s_out_stored, 16 * (NC + 1))
            for b in range(2):
                gather_ready(b, b)
                for q in range(NQ):
                    gather(b, q)
            for e in range(2):
                expert(e, e)
            with pool.Fori(1, E // 2 - 1) as i:
                for b in range(2):
                    expert(2 * i + b, b)
            expert(E - 2, 0, False)
            expert(E - 1, 1, False)

        @blk.tensor
        def _(pe):
            t = nc.tensor
            mm = t.matmul
            pe.wait_ge(s_consts, 16)
            for j in range(NT):
                pe.wait_ge(s_xn, j + 1)
                ins = t.transpose(psum[:, j // TPC, (j % TPC) * P:(j % TPC + 1) * P], xn[:, j, :], ident)
                if j % TPC == TPC - 1:
                    ins.then_inc(s_xn_turned, 1)
            pe.wait_ge(s_weights, 48)

            pe.wait_ge(s_spreaders, 3)
            for c in range(NC):
                cs = slice(c * CH, (c + 1) * CH)
                pe.wait_ge(s_xnT, c + 1)
                if c >= 2:
                    if above_zero(c - 1):
                        pe.wait_ge(s_xp, c - 1)
                mm(psum[0:RANK, 4 + c % 2, :], wx_s[:, 0:RANK], xnT[:, cs], start=True, stop=True).then_inc(s_xp_product, 1)
                for k in range(2):
                    if above_zero(2 * (c - 1) + k + 1):
                        pe.wait_ge(s_bc, 2 * (c - 1) + k + 1)
                    mm(bank(6 + k), wbc[:, k].rearrange("p s d -> p (s d)"), xnT[:, cs], start=True, stop=True).then_inc(s_bc_product, 1)
                pe.wait_ge(s_xp, c + 1)
                mm(bank(c), wdt_s[:], xp_s[:, cs], start=True, stop=True).then_inc(s_z, 1)
            pe.wait_ge(s_delta, 2 * NC)
            pe.wait_ge(s_high, 2 * NC)
            pe.wait_ge(s_log, NC)
            pe.wait_ge(s_bc, 2 * NC)

            def spread(c, vv):
                for k in range(UG):
                    grp, m = UG * vv + k, c * NG + (UG * vv + k)
                    half = grp // 8
                    sel = sel_r[:, grp % 8].rearrange("p s d -> p (s d)")
                    if above_zero(m - 1):
                        pe.wait_ge(s_decay, m - 1)
                    mm(bank(SPREAD_D + k), sel, qd[:, half, bass.ts(c, CH)], start=True, stop=True).then_inc(s_delta_spread, 1)
                    if above_zero(m - 1):
                        pe.wait_ge(s_input, m - 1)
                    mm(bank(SPREAD_X + k), sel, qx[:, half, bass.ts(c, CH)], start=True, stop=True).then_inc(s_dx_spread, 1)

            def reduce(c, vv):
                n, s = c * UPC + vv, vv % RING
                pe.wait_ge(s_product, n + 1)
                if vv == 0:
                    if above_zero(c):
                        pe.wait_ge(s_y, c)
                for k in range(UG):
                    grp = UG * vv + k
                    o = D - GD - GD * grp
                    ins = mm(bank(YB), wred[:, o:o + D], hc[:, s, k, :], start=(grp == 0), stop=(grp == NG - 1))
                ins.then_inc(s_summed, 1)

            def post(c, step):
                if step == 1:
                    pe.wait_ge(s_y, c + 1)
                    if above_zero(c):
                        pe.wait_ge(s_xn2T, c)
                    for j in range(TPC):
                        ins = t.transpose(psum[:, TB, j * P:(j + 1) * P], y2[:, j * P:(j + 1) * P], ident)
                    ins.then_inc(s_y_turned, 1)
                elif step == 3:
                    pe.wait_ge(s_xn2, TPC * c + TPC)
                    for j in range(TPC):
                        ins = t.transpose(psum[:, TB, j * P:(j + 1) * P], xn[:, j, :], ident)
                    ins.then_inc(s_xn2_turned, 1)
                    pe.wait_ge(s_xn2T, c + 1)
                    if above_zero(c):
                        pe.wait_ge(s_logits, c)
                    for j in range(TPC):
                        ins = mm(psum[:, RB, j * E:(j + 1) * E], x2T[:, j * P:(j + 1) * P], wr_s, start=True, stop=True)
                    ins.then_inc(s_logits_product, 1)

            def chunk(c, first):
                for vv in range(UPC):
                    spread(c, vv)
                    if vv >= LAG:
                        if not first:
                            post(c - 1, vv - LAG)
                        reduce(c, vv - LAG)
                    elif not first:
                        reduce(c - 1, UPC - LAG + vv)

            pe.wait_ge(s_stack[0], 16 * 8)
            chunk(0, True)
            for c in range(1, NC):
                pe.wait_ge(s_stack[c], 16 * 8)
            with pe.Fori(1, NC) as c:
                chunk(c, False)
            for vv in range(LAG):
                reduce(NC - 1, UPC - LAG + vv)
            for step in range(4):
                post(NC - 1, step)

            for j in range(NT):
                if j % 4 == 0:
                    pe.wait_ge((s_copied_dve, s_copied_act)[j // 4 % 2], j // 8 + 1)
                ins = t.transpose(psum[:, j // 4, (j % 4) * P:(j % 4 + 1) * P],
                                  wmx[:, j].rearrange("p e r -> p (e r)"), ident)
            ins.then_inc(s_weights_turned, 1)
            for r in range(NROUND):
                pe.wait_ge(s_indicator, r + 1)
                mm(psum[:, 4, r:r + 1], blk_b[:], ind[:, r:r + 1], start=True, stop=True).then_inc(s_digit, 1)
            pe.wait_ge(s_tau_rows, 1)
            mm(psum[:, 4, 32:32 + E], cc("ones"), taud[:], start=True, stop=True).then_inc(s_tau, 1)

            def flat(a):
                return a[:].rearrange("p e j -> p (e j)")

            pe.wait_ge(s_above, 2)
            mm(bank(5, P), ones_b[:], flat(gt_b), start=True, stop=True)
            mm(bank(6, P), ones_b[:], flat(eq_b), start=True, stop=True)
            mm(bank(7, P), tri_b[:], flat(eq_b), start=True, stop=True).then_inc(s_counted, 1)
            pe.wait_ge(s_keep, 1)
            mm(bank(6, P), ones_b[:], flat(kp_b), start=True, stop=True)
            mm(bank(7, P), tri_b[:], flat(kp_b), start=True, stop=True).then_inc(s_keep_counted, 1)

            def table(e):
                pe.wait_ge(s_one_hot, e + 1)
                if above_zero(e):
                    pe.wait_ge(s_gather_ids, e)
                for j in range(NT):
                    ins = mm(psum[:, 7, 0:5 * NQ], oh[:, j, :], rq[:, :, j, :], start=(j == 0), stop=(j == NT - 1))
                ins.then_inc(s_table, 1)

            def turn(e, b, i):
                for q in range(NQ):
                    pe.wait_ge(s_gathered[b][q], 16 * i + 16)
                    if q == 0:
                        if above_zero(2 * e):
                            pe.wait_ge(s_xe, 2 * e)
                    if q == 4:
                        if above_zero(NQ * (e - 1)):
                            pe.wait_ge(s_weighed, NQ * (e - 1))
                    ins = t.transpose(psum[:, 4 + 2 * (q // 4), (q % 4) * P:(q % 4 + 1) * P], gx[:, b, q, :], ident)
                    if q >= 3:
                        ins.then_inc(s_rows_turned, 1)

            def up(e, b, i):
                pe.wait_ge(s_expert_weights[b], 48 * i + 48)
                for un in range(2 * FC):
                    half, f = un // FC, un % FC
                    g = e * (2 * FC) + un
                    pe.wait_ge(s_xe, 2 * e + 1 + half)
                    if above_zero(g - 1):
                        pe.wait_ge(s_silu, g - 1)
                    cs = slice(half * HALF, (half + 1) * HALF)
                    mm(psum[:, 2 + un % 2, 0:HALF], wg_s[:, b, f * P:(f + 1) * P], xe[:, b, cs], start=True, stop=True)
                    if above_zero(g - 1):
                        pe.wait_ge(s_hidden, g - 1)
                    mm(psum[:, un % 2, 0:HALF], w1_s[:, b, f * P:(f + 1) * P], xe[:, b, cs], start=True,
                       stop=True).then_inc(s_up, 1)

            def down(e, b, turned=None):
                pe.wait_ge(s_hidden, (e + 1) * 2 * FC)
                if above_zero(NQ * e):
                    pe.wait_ge(s_weighed, NQ * e)
                for q in range(NQ):
                    if q == 4 and turned is not None:
                        pe.wait_ge(s_xe, turned)
                    for f in range(FC):
                        ins = mm(psum[:, 5 + q // 4, (q % 4) * P:(q % 4 + 1) * P], hT[:, b, f, q * P:(q + 1) * P],
                                 w2_s[:, b, f, :], start=(f == 0), stop=(f == FC - 1))
                ins.then_inc(s_down, 1)

            def expert(i, b, more=True, turn_next=True):
                e = 2 * i + b
                up(e, b, i)
                if more:
                    table(e + 2)
                if turn_next:
                    turn(e + 1, 1 - b, i + b)
                down(e, b, 2 * e + 4 if turn_next else None)

            table(0)
            table(1)
            turn(0, 0, 0)
            expert(0, 0)
            expert(0, 1)
            with pe.Fori(1, E // 2 - 1) as i:
                for b in range(2):
                    expert(i, b)
            expert(E // 2 - 1, 0, False)
            expert(E // 2 - 1, 1, False, False)


def kernel(L0_attn_x, L0_attn_W_xproj, L0_attn_W_dt, L0_attn_b_dt, L0_attn_A_log, L0_attn_D, L0_ffn_router_weight,
           L0_ffn_ff_pre_act_weight, L0_ffn_gate_weight, L0_ffn_ff_post_act_weight):
    import concourse.bacc as bacc
    from concourse.bass_utils import run_bass_kernel_spmd

    def lay(a):
        return np.ascontiguousarray(a)

    x = np.asarray(L0_attn_x)
    alog = np.asarray(L0_attn_A_log).reshape(NG, GD, NS).transpose(2, 1, 0).reshape(P, NG)
    small = np.concatenate([np.asarray(L0_attn_b_dt)[:, None], np.asarray(L0_attn_D)[:, None], alog,
                            np.asarray(L0_ffn_router_weight).T], axis=1)
    arrays = {
        "x": lay(x.reshape(T, D)),
        "wx": lay(np.asarray(L0_attn_W_xproj).T),
        "wdt": lay(np.asarray(L0_attn_W_dt).T),
        "small": lay(small),
        "w1": lay(np.asarray(L0_ffn_ff_pre_act_weight).transpose(0, 2, 1)),
        "wg": lay(np.asarray(L0_ffn_gate_weight).transpose(0, 2, 1)),
        "w2": lay(np.asarray(L0_ffn_ff_post_act_weight).reshape(E, D, FC, P).transpose(0, 3, 2, 1)),
        "consts": shape_constants(),
        "jbits": search_bits(),
    }
    nc = bacc.Bacc("TRN2", target_bir_lowering=False, num_devices=1)
    ap = {k: nc.dram_tensor("in_" + k, a.shape, mybir.dt.from_np(a.dtype), kind="ExternalInput").ap() for k, a in arrays.items()}
    out = nc.dram_tensor("out", [T + P, D], F32, kind="ExternalOutput").ap()
    rows = nc.dram_tensor("rows", [T, D], F32, kind="Internal").ap()
    build(nc, ap["x"], ap["wx"], ap["wdt"], None, None, ap["small"], None, ap["w1"], ap["wg"], ap["w2"], ap["consts"],
          ap["jbits"], out, rows)
    r = run_bass_kernel_spmd(nc, [{"in_" + k: a for k, a in arrays.items()}], core_ids=[0])
    return r.results[0]["out"][:T].reshape(BATCH, SEQ, D)
```

```python
from contextlib import ExitStack

import numpy as np

import concourse.bass as bass
from concourse import mybir

F32 = mybir.dt.float32
F32R = mybir.dt.float32r
BF16 = mybir.dt.bfloat16
I32 = mybir.dt.int32
ALU = mybir.AluOpType
ACT = mybir.ActivationFunctionType
AX = mybir.AxisListType

P = 128
BATCH, SEQ, D = 8, 256, 128
T = BATCH * SEQ
NT = T // P
NS = 16
GD = P // NS
NG = D // GD
RANK = 64
CH = 512
NC = T // CH
TPC = CH // P
BPC = CH // SEQ
UG = 2
UPC = NG // UG
RING = 4
SPLIT = 3
LAG = 3

E = 8
DFF = 512
FC = DFF // P
CAP = 640
NQ = CAP // P
HALF = CAP // 2
EPS_LN = 1e-05
EPS_W = 1.1920929e-07
NROUND = 8
SHIFT = [26 - 4 * r for r in range(NROUND - 1)] + [0]

CONST = [("ident", P), ("dup", RANK), ("wred", P + D - GD), ("ones", P), ("tri", P), ("blk", P), ("iota", P),
         ("selcol", E), ("desc", NT * E), ("smask", E * NT), ("jval", E * NT), ("q5", NQ), ("pval", 1),
         ("spare", NQ)]
COFF, _o = {}, 0
for _n, _w in CONST:
    COFF[_n] = (_o, _w)
    _o += _w
CW = _o
CW_EARLY = P + RANK


def shape_constants():
    p = np.arange(P)
    c = {
        "ident": np.eye(P),
        "ones": np.ones((P, P)),
        "tri": p[:, None] <= p[None, :],
        "blk": (p[:, None] // 16 == p[None, :] // 16) & (p[:, None] % 16 > 0),
        "iota": np.broadcast_to(p[None, :] + 1, (P, P)),
        "wred": (np.arange(P + D - GD)[None, :] == (D - GD) + p[:, None] % GD),
        "dup": p[:, None] % RANK == np.arange(RANK)[None, :],
        "selcol": p[:, None] == 16 * np.arange(E)[None, :],
        "desc": np.broadcast_to(E - np.arange(NT * E) % E, (P, NT * E)),
        "smask": np.broadcast_to(np.arange(E * NT) % NT > 0, (P, E * NT)),
        "jval": np.broadcast_to(P * (np.arange(E * NT) % NT), (P, E * NT)),
        "q5": np.broadcast_to(np.arange(NQ), (P, NQ)),
        "pval": p[:, None] + 1,
        "spare": T + P * np.arange(NQ)[None, :] + p[:, None],
    }
    return np.concatenate([np.asarray(c[n], np.float32) for n, _ in CONST], axis=1)


def search_bits():
    j = (np.arange(P) % 16)[:, None]
    cols = [j << s for s in SHIFT[:-1]] + [np.where(j < 4, j, 0x40000000)]
    return np.concatenate(cols, axis=1).astype(np.int32)


def build(nc, x, wx, wdt, vectors, dskip, w1, wg, w2, consts, jbits, out, rows):
    with ExitStack() as ctx:
        def sb(name, shape, dt=F32):
            return ctx.enter_context(nc.sbuf_tensor(name, shape, dt))

        def sem(name):
            return ctx.enter_context(nc.semaphore(name))

        psum = ctx.enter_context(nc.psum_tensor("psum", [P, 8, CH], F32))

        cst = sb("cst", [P, CW])

        def cc(name):
            o, w = COFF[name]
            return cst[:, o:o + w]

        ident = cc("ident")
        jb = sb("jb", [P, NROUND], I32)
        wx_s = sb("wx_s", [P, RANK + 2 * NS])
        wdt_s = sb("wdt_s", [RANK, D])
        small = sb("small", [P, 1 + NG + E])
        bdt_s, alog_s, wr_s = small[:, 0:1], small[:, 1:1 + NG], small[:, 1 + NG:1 + NG + E]
        nega = sb("nega", [P, NG])
        wred = cc("wred")
        sel_r = sb("sel_r", [P, P // GD // 2, NS, GD], F32R)
        wbc = sb("wbc", [P, 2, NS, GD])
        ones_b = sb("ones_b", [P, P], BF16)
        tri_b = sb("tri_b", [P, P], BF16)
        blk_b = sb("blk_b", [P, P], BF16)
        iota_b = sb("iota_b", [P, P], BF16)

        xt = sb("xt", [P, NT, D])
        xn = sb("xn", [P, NT, D])
        xnT = sb("xnT", [P, T])
        bbc = sb("bbc", [P, T])
        cbc = sb("cbc", [P, T])
        parts = sb("parts", [P, SPLIT, 2, 2, CH], F32R)
        drow = sb("drow", [P, D])
        stack = sb("stack", [P, 2, 2, T], F32R)
        stat = sb("stat", [P, NT, 6])
        mv = sb("mv", [P, NT, 2])
        ve = sb("ve", [P, NT])
        r0 = sb("r0", [P, NT])
        rt = sb("rt", [P, NT])
        rstd = sb("rstd", [P, NT])
        stat2 = sb("stat2", [P, TPC, 6])
        mv2 = sb("mv2", [P, TPC, 2])
        sm2 = sb("sm2", [P, 6, TPC])
        ring = sb("ring", [P, 4 * RING * UG * CH])
        da, uu, hh, hc = (ring[:, k * RING * UG * CH:(k + 1) * RING * UG * CH].rearrange(
            "p (r u n) -> p r u n", r=RING, u=UG) for k in range(4))
        xp_s = ring[0:RANK, 2 * RING * UG * CH:2 * RING * UG * CH + T]
        pre_a, pre_b, pre_c = uu[:, :, 0], hc[:, :, 0], hc[:, :, 1]
        wmx = xnT[:].rearrange("p (j e r) -> p j e r", e=E, r=16)
        taken = [0]

        def later(*shape):
            n = int(np.prod(shape))
            o = taken[0]
            taken[0] += n
            assert taken[0] <= 4 * RING * UG * CH
            names = "abc"[:len(shape)]
            return ring[:, o:o + n].rearrange(f"p ({' '.join(names)}) -> p {' '.join(names)}",
                                              **dict(zip(names, shape)))
        y2 = sb("y2", [P, CH])
        x2T = sb("x2T", [P, CH])

        lg = sb("lg", [P, NT, E])
        rb = sb("rb", [P, 12, NT * E])
        r16 = sb("r16", [P, 10, NT])
        wm = sb("wm", [P, NT, E])
        fullest = sb("fullest", [P, 1], I32)
        cnt = sb("cnt", [P, NROUND])
        ind = sb("ind", [P, NROUND], BF16)
        base = sb("base", [P, NROUND + 1], I32)
        thr = sb("thr", [P, NROUND], I32)
        digs = sb("digs", [P, NROUND], I32)
        taud = sb("taud", [P, E])
        gt_b = sb("gt_b", [P, E, NT], BF16)
        eq_b = sb("eq_b", [P, E, NT], BF16)
        kp_b = sb("kp_b", [P, E, NT], BF16)
        lim = sb("lim", [P, 2, E])
        qq = sb("qq", [P, E * NT])
        r1 = sb("r1", [P, E * NT])
        vals = sb("vals", [P, 5, E * NT], BF16)

        w1_s = sb("w1_s", [P, 2, DFF])
        wg_s = sb("wg_s", [P, 2, DFF])
        w2_s = sb("w2_s", [P, 2, FC, D])
        oh = later(NT, P // 2).bitcast(BF16)
        q1 = sb("q1", [P, NT, NQ], BF16)
        rq = sb("rq", [P, 5, NT, NQ], BF16)
        tab = sb("tab", [P, E, 5 * NQ])
        tg = sb("tg", [P, 2, NQ])
        tk = sb("tk", [P, 4, NQ])
        gid = sb("gid", [P, 2, NQ], I32)
        sid = sb("sid", [P, 2, NQ], I32)
        kw = sb("kw", [P, 2, NQ])
        gx = later(2, NQ, D)
        xe = later(2, CAP)
        sg = later(2, HALF)
        hT = later(2, FC, CAP)
        ye = later(2, NQ, D)
        zero = sb("zero", [P, D])

        s_consts = sem("s_consts")
        s_late_consts = sem("s_late_consts")
        s_skip = sem("s_skip")
        s_weights = sem("s_weights")
        s_wx = sem("s_wx")
        s_wdt = sem("s_wdt")
        s_bits = sem("s_bits")
        s_spreaders = sem("s_spreaders")
        s_neg_a = sem("s_neg_a")
        s_pool_consts = sem("s_pool_consts")
        s_passed = sem("s_passed")
        s_dve = sem("s_dve")
        s_act = sem("s_act")
        s_pool = sem("s_pool")
        s_residual = sem("s_residual")
        s_xn = sem("s_xn")
        s_xn_turned = sem("s_xn_turned")
        s_xnT = sem("s_xnT")
        s_xp_product = sem("s_xp_product")
        s_xp = sem("s_xp")
        s_bc_product = sem("s_bc_product")
        s_b = sem("s_b")
        s_c = sem("s_c")
        s_z = sem("s_z")
        s_abs_z = sem("s_abs_z")
        s_log = sem("s_log")
        s_delta = sem("s_delta")
        s_high = sem("s_high")
        s_low = sem("s_low")
        s_delta_spread = sem("s_delta_spread")
        s_dx_spread = sem("s_dx_spread")
        s_decay = sem("s_decay")
        s_input = sem("s_input")
        s_state = sem("s_state")
        s_product = sem("s_product")
        s_summed = sem("s_summed")
        s_y = sem("s_y")
        s_y_turned = sem("s_y_turned")
        s_x2 = sem("s_x2")
        s_rough2 = sem("s_rough2")
        s_rstd2 = sem("s_rstd2")
        s_xn2 = sem("s_xn2")
        s_xn2_turned = sem("s_xn2_turned")
        s_xn2T = sem("s_xn2T")
        s_logits_product = sem("s_logits_product")
        s_logits = sem("s_logits")
        s_rows_stored = sem("s_rows_stored")
        s_out_stored = sem("s_out_stored")
        s_router = sem("s_router")
        s_exp = sem("s_exp")
        s_chosen = sem("s_chosen")
        s_chosen_counted = sem("s_chosen_counted")
        s_fullest = sem("s_fullest")
        s_search = sem("s_search")
        s_copied_dve = sem("s_copied_dve")
        s_copied_act = sem("s_copied_act")
        s_weights_turned = sem("s_weights_turned")
        s_indicator = sem("s_indicator")
        s_digit = sem("s_digit")
        s_tau_rows = sem("s_tau_rows")
        s_tau = sem("s_tau")
        s_above = sem("s_above")
        s_counted = sem("s_counted")
        s_keep = sem("s_keep")
        s_keep_counted = sem("s_keep_counted")
        s_one_hot = sem("s_one_hot")
        s_table = sem("s_table")
        s_gather_ids = sem("s_gather_ids")
        s_scatter_ids = sem("s_scatter_ids")
        s_rows_turned = sem("s_rows_turned")
        s_xe = sem("s_xe")
        s_up = sem("s_up")
        s_silu = sem("s_silu")
        s_hidden = sem("s_hidden")
        s_down = sem("s_down")
        s_weighed = sem("s_weighed")
        s_scattered = sem("s_scattered")
        s_x = [sem(f"s_x_chunk{c}") for c in range(NC)]
        s_stack = [sem(f"s_stack{c}") for c in range(NC)]
        s_expert_weights = [sem(f"s_expert_weights{b}") for b in range(2)]
        s_gathered = [[sem(f"s_gathered{b}{q}") for q in range(NQ)] for b in range(2)]

        blk = ctx.enter_context(nc.Block())
        xv = x.rearrange("(c j p) d -> c p j d", j=TPC, p=P)
        outv = out[0:T, :].rearrange("(c j p) d -> c p j d", j=TPC, p=P)
        rowv = rows.rearrange("(c j p) d -> c p j d", j=TPC, p=P)

        def bank(k, w=CH):
            return psum[:, k, 0:w]

        SPREAD_D, SPREAD_X, YB, TB, RB = 0, 2, 4, 5, 6

        def above_zero(value):
            return not isinstance(value, int) or value > 0

        def plain(eng):
            eng.sem_inc(s_passed, 1)

        class Chain:

            def __init__(self, eng, own):
                self.eng, self.own, self.n, self.base = eng, own, 0, 0

            def mark(self, ins):
                self.n += 1
                ins.then_inc(self.own, 1)
                return self.n

            def until(self, n):
                self.eng.wait_ge(self.own, self.base + n)

            def after(self):
                self.eng.wait_ge(self.own, self.base + self.n)

            def link(self, ins):
                self.mark(ins)
                self.after()

        @blk.sync
        def _(sp):
            for c in range(NC):
                nc.sync.dma_start(xt[:, TPC * c:TPC * (c + 1), :], xv[c]).then_inc(s_x[c], 16)
            nc.sync.dma_start(drow[:], dskip).then_inc(s_skip, 16)
            nc.sync.dma_start(cst[:, CW_EARLY:], consts[:, CW_EARLY:]).then_inc(s_late_consts, 16)
            nc.sync.dma_start(jb[:], jbits).then_inc(s_bits, 16)
            for c in range(NC):
                cs = slice(c * CH, (c + 1) * CH)
                for part, ready in enumerate((s_high, s_low)):
                    sp.wait_ge(ready, 2 * c + 2)
                    rows_to = slice(64 * part, 64 * part + 64)
                    for half in range(2):
                        rows_from = slice(64 * half, 64 * half + 64)
                        nc.sync.dma_start(stack[rows_to, half, :, cs].bitcast(F32),
                                          parts[rows_from, c % SPLIT, part].bitcast(F32)).then_inc(s_stack[c], 16)
            sp.wait_ge(s_pool_consts, 1)
            nc.sync.dma_start(out[T:T + CAP, :].rearrange("(q p) d -> p q d", p=P),
                              zero[:].rearrange("p (o d) -> p o d", o=1).to_broadcast([P, NQ, D])).then_inc(s_out_stored, 16)
            for e in range(2):
                nc.sync.dma_start(w1_s[:, e, :], w1[e]).then_inc(s_expert_weights[e], 16)
                nc.sync.dma_start(wg_s[:, e, :], wg[e]).then_inc(s_expert_weights[e], 16)
                nc.sync.dma_start(w2_s[:, e, :, :], w2[e]).then_inc(s_expert_weights[e], 16)
            with sp.Fori(0, NC) as c:
                sp.wait_ge(s_x2, c + 1)
                nc.sync.dma_start(outv[c], xt[:, bass.ts(c, TPC), :]).then_inc(s_out_stored, 16)
                sp.wait_ge(s_xn2, TPC * c + TPC)
                nc.sync.dma_start(rowv[c], xn[:, 0:TPC, :]).then_inc(s_rows_stored, 16)
            with sp.Fori(0, E // 2 - 1) as i:
                for b in range(2):
                    sp.wait_ge(s_down, 2 * i + (b + 1))
                    nc.sync.dma_start(w1_s[:, b, :], w1[2 * i + (2 + b)]).then_inc(s_expert_weights[b], 16)
                    nc.sync.dma_start(wg_s[:, b, :], wg[2 * i + (2 + b)]).then_inc(s_expert_weights[b], 16)
                    nc.sync.dma_start(w2_s[:, b, :, :], w2[2 * i + (2 + b)]).then_inc(s_expert_weights[b], 16)
            sp.wait_ge(s_out_stored, 16 * (NC + 1))
            sp.wait_ge(s_rows_stored, 16 * NC)
            sp.wait_ge(s_scattered, 16 * E * NQ)

        @blk.vector
        def _(dve):
            ch = Chain(dve, s_dve)
            v = nc.vector
            for j in range(NT):
                if j % TPC == 0:
                    dve.wait_ge(s_x[j // TPC], 16)
                ch.mark(v.bn_stats(stat[:, j, :], xt[:, j, :]))
            ch.after()
            for j in range(NT):
                ch.mark(v.bn_aggr(mv[:, j, :], stat[:, j, :]))
            ch.after()
            ch.link(v.tensor_scalar(ve[:], mv[:, :, 1], EPS_LN, None, ALU.add))
            ch.link(v.tensor_scalar(r0[:].bitcast(I32), ve[:].bitcast(I32), 1, None, ALU.logical_shift_right))
            ch.link(v.tensor_scalar(rstd[:].bitcast(I32), r0[:].bitcast(I32), -1.0, float(0x5f3759df), ALU.mult, ALU.add))
            for _ in range(3):
                ch.link(v.tensor_tensor(rt[:], rstd[:], rstd[:], ALU.mult))
                ch.link(v.scalar_tensor_tensor(rt[:], rt[:], -0.5, ve[:], ALU.mult, ALU.mult))
                ch.link(v.scalar_tensor_tensor(rstd[:], rt[:], 1.5, rstd[:], ALU.add, ALU.mult))
            for j in range(NT):
                v.tensor_scalar(xn[:, j, :], xt[:, j, :], mv[:, j, 0:1], rstd[:, j:j + 1], ALU.subtract,
                                ALU.mult).then_inc(s_xn, 1)

            def rank_rows(c):
                dve.wait_ge(s_xp_product, c + 1)
                v.tensor_copy(xp_s[:, c * CH:(c + 1) * CH], psum[0:RANK, 4 + c, :]).then_inc(s_xp, 1)

            def positive(c):
                dve.wait_ge(s_abs_z, c + 1)
                ch.mark(v.tensor_scalar(pre_b[:, c], bank(c), bdt_s, 0.0, ALU.add, ALU.max))

            def delta(c):
                dve.wait_ge(s_log, c + 1)
                v.tensor_tensor(pre_b[:, c], pre_b[:, c], pre_a[:, c], ALU.add).then_inc(s_delta, 1)
                dve.wait_ge(s_delta, 2 * c + 1)
                v.tensor_tensor(pre_c[:, c], pre_b[:, c], xnT[:, c * CH:(c + 1) * CH], ALU.mult).then_inc(s_delta, 1)

            def b_rows(c):
                dve.wait_ge(s_bc_product, 2 * c + 1)
                v.tensor_copy(bbc[:, c * CH:(c + 1) * CH], bank(4 + 2 * c % 4)).then_inc(s_b, 1)

            for c in range(NC):
                rank_rows(c)
            dve.wait_ge(s_weights, 16)
            for c in range(NC):
                positive(c)
            ch.after()
            dve.wait_ge(s_xnT, NC)
            delta(0)
            b_rows(0)
            for k, full in enumerate((pre_b, pre_c)):
                dve.wait_ge(s_high, k + 1)
                v.tensor_tensor(parts[:, 0, 1, k], full[:, 0], parts[:, 0, 0, k].bitcast(F32),
                                ALU.subtract).then_inc(s_low, 1)
            dve.wait_ge(s_b, 1)

            def u_step(c, vv):
                for k in range(UG):
                    n, m = c * UPC + vv, c * NG + (UG * vv + k)
                    dve.wait_ge(s_dx_spread, m + 1)
                    if k == 0 and above_zero(n - (RING - 1)):
                        dve.wait_ge(s_state, n - (RING - 1))
                    v.tensor_tensor(uu[:, vv % RING, k, :], bank(SPREAD_X + k), bbc[:, bass.ts(c, CH)],
                                    ALU.mult).then_inc(s_input, 1)

            def scan_step(c, vv):
                n, s = c * UPC + vv, vv % RING
                dve.wait_ge(s_input, n * UG + UG)
                dve.wait_ge(s_decay, n * UG + UG)
                if above_zero(n - (RING - 1)):
                    dve.wait_ge(s_product, n - (RING - 1))
                v.tensor_tensor_scan(hh[:, s].rearrange("p a b -> p (a b)"), da[:, s].rearrange("p a b -> p (a b)"),
                                     uu[:, s].rearrange("p a b -> p (a b)"), 0.0, ALU.mult, ALU.add).then_inc(s_state, 1)

            def post(c, step):
                if step == 0:
                    dve.wait_ge(s_y_turned, c + 1)
                    ch.link(v.tensor_tensor(xt[:, bass.ts(c, TPC), :], xt[:, bass.ts(c, TPC), :],
                                            bank(TB).rearrange("p (j d) -> p j d", d=D), ALU.add))
                    plain(dve)
                    for j in range(TPC):
                        ch.mark(v.bn_stats(stat2[:, j, :], xt[:, TPC * c + j, :]))
                elif step == 1:
                    ch.after()
                    plain(dve)
                    for j in range(TPC):
                        ch.mark(v.bn_aggr(mv2[:, j, :], stat2[:, j, :]))
                elif step == 2:
                    ch.after()
                    v.tensor_scalar(sm2[:, 0, :], mv2[:, :, 1], EPS_LN, None, ALU.add).then_inc(s_x2, 1)
                elif step == 3:
                    dve.wait_ge(s_rough2, c + 1)
                    ch.link(v.tensor_tensor(sm2[:, 3, :], sm2[:, 2, :], sm2[:, 2, :], ALU.mult))
                    ch.link(v.scalar_tensor_tensor(sm2[:, 3, :], sm2[:, 3, :], -0.5, sm2[:, 0, :], ALU.mult, ALU.mult))
                    ch.link(v.scalar_tensor_tensor(sm2[:, 4, :], sm2[:, 3, :], 1.5, sm2[:, 2, :], ALU.add, ALU.mult))
                    v.scalar_tensor_tensor(sm2[:, 5, :], mv2[:, :, 0], -1.0, sm2[:, 4, :], ALU.mult,
                                           ALU.mult).then_inc(s_rstd2, 1)

            def chunk(c, first):
                for vv in range(UPC):
                    if not first and vv == LAG + 1:
                        post(c - 1, 1)
                    if first and vv < NC:
                        dve.wait_ge(s_delta, 2 * vv + 1)
                    u_step(c, vv)
                    if first and vv + 1 < NC:
                        delta(vv + 1)
                        b_rows(vv + 1)
                        dve.wait_ge(s_b, vv + 2)
                    if not first and vv == LAG + 1:
                        post(c - 1, 2)
                    if vv:
                        scan_step(c, vv - 1)
                    elif not first:
                        scan_step(c - 1, UPC - 1)
                    if not first and vv == LAG:
                        post(c - 1, 0)
                    if not first and vv == LAG + 2:
                        post(c - 1, 3)

            dve.wait_ge(s_residual, NC)
            chunk(0, True)
            old = ch.base + ch.n
            PER = 1 + 2 * TPC + 3
            with dve.Fori(1, NC) as c:
                ch.base, ch.n = old + (c - 1) * PER, 0
                chunk(c, False)
                assert ch.n == PER, ch.n
            ch.base, ch.n = old + (NC - 1) * PER, 0
            scan_step(NC - 1, UPC - 1)
            for step in range(4):
                post(NC - 1, step)

            R = [rb[:, k, :].rearrange("p (j e) -> p j e", e=E) for k in range(12)]

            def w16(k):
                return r16[:, k, :]

            def over(a):
                return a.unsqueeze(2).to_broadcast([P, NT, E])

            desc = cc("desc").rearrange("p (j e) -> p j e", e=E)
            dve.wait_ge(s_late_consts, 16)
            dve.wait_ge(s_logits, NC)
            ch.link(v.tensor_reduce(w16(0), lg[:], AX.X, ALU.max))
            v.tensor_tensor(R[0], lg[:], over(w16(0)), ALU.subtract).then_inc(s_router, 1)
            dve.wait_ge(s_exp, 1)
            ch.link(v.tensor_reduce(w16(1), R[1], AX.X, ALU.add))
            ch.link(v.reciprocal(w16(2), w16(1)))
            ch.link(v.tensor_tensor(R[2], R[1], over(w16(2)), ALU.mult))

            def first_largest(src, top, tmp, tmp16, mask):
                ch.link(v.tensor_reduce(top, src, AX.X, ALU.max))
                ch.link(v.tensor_tensor(tmp, src, over(top), ALU.is_equal))
                ch.link(v.tensor_tensor(tmp, tmp, desc, ALU.mult))
                ch.link(v.tensor_reduce(tmp16, tmp, AX.X, ALU.max))
                ch.link(v.tensor_tensor(mask, tmp, over(tmp16), ALU.is_equal))

            first_largest(R[2], w16(3), R[3], w16(4), R[4])
            ch.link(v.scalar_tensor_tensor(R[5], R[4], -2.0, R[2], ALU.mult, ALU.add))
            first_largest(R[5], w16(5), R[3], w16(4), R[6])
            v.tensor_tensor(kp_b[:], R[4].rearrange("p j e -> p e j"), R[6].rearrange("p j e -> p e j"),
                            ALU.add).then_inc(s_chosen, 1)
            ch.link(v.tensor_tensor(w16(6), w16(3), w16(5), ALU.add))
            ch.link(v.tensor_scalar(w16(6), w16(6), EPS_W, None, ALU.max))
            ch.link(v.reciprocal(w16(7), w16(6)))
            ch.mark(v.tensor_tensor(w16(8), w16(3), w16(7), ALU.mult))
            ch.link(v.tensor_tensor(w16(9), w16(5), w16(7), ALU.mult))
            ch.mark(v.tensor_tensor(R[7], R[4], over(w16(8)), ALU.mult))
            ch.link(v.tensor_tensor(R[8], R[6], over(w16(9)), ALU.mult))

            def ej(a):
                return a.rearrange("p (e j) -> p e j", j=NT)

            dve.wait_ge(s_chosen_counted, 1)
            ch.mark(v.tensor_tensor(R[9], R[4], R[6], ALU.add))
            ch.link(v.tensor_reduce(lim[:, 0, :], ej(bank(6, P)), AX.X, ALU.add))
            ch.mark(v.tensor_tensor(R[8], R[7], R[8], ALU.add))
            v.tensor_reduce(fullest[:], lim[:, 0, :], AX.X, ALU.max).then_inc(s_fullest, 1)
            ch.after()
            v.scalar_tensor_tensor(wm[:], R[9], -1.0, R[8], ALU.add, ALU.add).then_inc(s_router, 1)
            dve.wait_ge(s_router, 2)
            wv = wm[:].rearrange("p j e -> p e j")

            def running(chain, tot, within, a, b, o):
                chain.link(v.tensor_tensor_scan(rb[:, a, :], cc("smask"), tot, 0.0, ALU.mult, ALU.add))
                chain.link(v.tensor_tensor(rb[:, b, :], rb[:, a, :], tot, ALU.subtract))
                chain.link(v.tensor_tensor(rb[:, o, :], rb[:, b, :], within, ALU.add))

            dve.wait_ge(s_fullest, 1)
            with dve.If(dve.value_load(fullest[0:1, 0:1]) > CAP):
                cs = Chain(dve, s_search)
                for k in (0, 2):
                    js = slice(4 * k, 4 * k + 4)
                    v.tensor_copy(wmx[:, js], wm[:, js].unsqueeze(3).to_broadcast([P, 4, E, 16])).then_inc(s_copied_dve, 1)
                dve.wait_ge(s_weights_turned, 1)
                junk = bbc[:]
                allw = psum[:, 0:4, :].rearrange("p b n -> p (b n)")
                dve.wait_ge(s_bits, 16)
                for r in range(NROUND):
                    edge = jb[:, 0:1] if r == 0 else thr[:, r:r + 1]
                    cs.link(v.tensor_scalar(junk, allw, edge.bitcast(F32), None, ALU.is_ge, ALU.add,
                                            accum_out=cnt[:, r:r + 1]))
                    v.tensor_scalar(ind[:, r:r + 1], cnt[:, r:r + 1], float(CAP), None, ALU.is_ge).then_inc(s_indicator, 1)
                    dve.wait_ge(s_digit, r + 1)
                    cs.link(v.tensor_scalar(digs[:, r:r + 1], psum[:, 4, r:r + 1], float(1 << SHIFT[r]), None, ALU.mult))
                    cs.link(v.tensor_tensor(base[:, r + 1:r + 2], digs[:, r:r + 1], base[:, r:r + 1], ALU.bitwise_or))
                    if r + 1 < NROUND:
                        cs.link(v.tensor_tensor(thr[:, r + 1:r + 2], base[:, r + 1:r + 2], jb[:, r + 1:r + 2], ALU.bitwise_or))
                v.tensor_scalar(taud[:], cc("selcol"), base[:, NROUND:].bitcast(F32), None, ALU.mult).then_inc(s_tau_rows, 1)
                dve.wait_ge(s_tau, 1)
                tau = psum[:, 4, 32:32 + E].unsqueeze(2).to_broadcast([P, E, NT])
                v.tensor_tensor(gt_b[:], wv, tau, ALU.is_gt).then_inc(s_above, 1)
                v.tensor_tensor(eq_b[:], wv, tau, ALU.is_equal).then_inc(s_above, 1)
                dve.wait_ge(s_counted, 1)
                cs.link(v.tensor_reduce(lim[:, 0, :], ej(bank(5, P)), AX.X, ALU.add))
                cs.link(v.tensor_scalar(lim[:, 1, :], lim[:, 0, :], -1.0, float(CAP), ALU.mult, ALU.add))
                running(cs, bank(6, P), bank(7, P), 0, 1, 2)
                cs.link(v.tensor_tensor(ej(rb[:, 3, :]), ej(rb[:, 2, :]), lim[:, 1, :].unsqueeze(2).to_broadcast([P, E, NT]),
                                        ALU.is_le))
                cs.link(v.tensor_tensor(ej(rb[:, 4, :]), ej(rb[:, 3, :]), eq_b[:], ALU.mult))
                v.tensor_tensor(kp_b[:], ej(rb[:, 4, :]), gt_b[:], ALU.add).then_inc(s_keep, 1)
                dve.wait_ge(s_keep, 1)
                dve.wait_ge(s_keep_counted, 1)

            slot = ch.mark(v.tensor_tensor_scan(rb[:, 0, :], cc("smask"), bank(6, P), 0.0, ALU.mult, ALU.add))
            share = ch.mark(v.tensor_tensor(ej(rb[:, 5, :]), kp_b[:], wv, ALU.mult))
            ch.until(slot)
            slot = ch.mark(v.tensor_tensor(rb[:, 1, :], rb[:, 0, :], bank(6, P), ALU.subtract))
            ch.until(share)
            share = ch.mark(v.tensor_reduce(w16(0), ej(rb[:, 5, :]).rearrange("p e j -> p j e"), AX.X, ALU.add))
            ch.until(slot)
            slot = ch.mark(v.tensor_tensor(rb[:, 2, :], rb[:, 1, :], bank(7, P), ALU.add))
            ch.until(share)
            share = ch.mark(v.tensor_scalar(w16(0), w16(0), EPS_W, None, ALU.max))
            ch.until(slot)
            slot = ch.mark(v.tensor_tensor(ej(rb[:, 8, :]), ej(rb[:, 2, :]), kp_b[:], ALU.mult))
            ch.until(share)
            share = ch.mark(v.reciprocal(w16(1), w16(0)))
            ch.until(slot)
            slot = ch.mark(v.tensor_scalar(qq[:], rb[:, 8, :], float(P), None, ALU.is_gt))
            ch.until(share)
            share = ch.mark(v.tensor_tensor(ej(rb[:, 6, :]), ej(rb[:, 5, :]), r16[:, 1:2, :].to_broadcast([P, E, NT]),
                                            ALU.mult))
            ch.until(slot)
            slot = ch.mark(v.scalar_tensor_tensor(qq[:], rb[:, 8, :], float(2 * P), qq[:], ALU.is_gt, ALU.add))
            ch.until(share)
            share = ch.mark(v.tensor_copy(vals[:, 2, :], rb[:, 6, :]))
            ch.until(slot)
            slot = ch.mark(v.scalar_tensor_tensor(qq[:], rb[:, 8, :], float(3 * P), qq[:], ALU.is_gt, ALU.add))
            ch.until(share)
            share = ch.mark(v.tensor_tensor(rb[:, 7, :], rb[:, 6, :], vals[:, 2, :], ALU.subtract))
            ch.until(slot)
            slot = ch.mark(v.scalar_tensor_tensor(qq[:], rb[:, 8, :], float(4 * P), qq[:], ALU.is_gt, ALU.add))
            ch.until(share)
            share = ch.mark(v.tensor_copy(vals[:, 3, :], rb[:, 7, :]))
            ch.until(slot)
            slot = ch.mark(v.scalar_tensor_tensor(r1[:], qq[:], -float(P), rb[:, 8, :], ALU.mult, ALU.add))
            ch.until(share)
            ch.mark(v.tensor_tensor(vals[:, 4, :], rb[:, 7, :], vals[:, 3, :], ALU.subtract))
            assert NQ == 5

            def one_hot(e, j):
                return v.tensor_scalar(oh[:, j, :], iota_b[:], r1[:, bass.ds(e * NT + j, 1)], None, ALU.is_equal)

            def columns(e):
                ch.link(v.tensor_tensor(q1[:], qq[:, bass.ts(e, NT)].unsqueeze(2).to_broadcast([P, NT, NQ]),
                                        cc("q5").rearrange("p (o q) -> p o q", o=1).to_broadcast([P, NT, NQ]), ALU.is_equal))
                for k in range(5):
                    last = v.tensor_tensor(rq[:, k], q1[:], vals[:, k, bass.ts(e, NT)].unsqueeze(2).to_broadcast([P, NT, NQ]),
                                           ALU.mult)
                last.then_inc(s_one_hot, 1)

            def gather_rows(e, b):
                dve.wait_ge(s_table, e + 1)
                if above_zero(2 * (e - 1)):
                    dve.wait_ge(s_rows_turned, 2 * (e - 1))
                tb = tab[:, bass.ds(e, 1), :].rearrange("p o n -> p (o n)")
                ch.link(v.tensor_copy(tb, psum[:, 7, 0:5 * NQ]))
                ch.mark(v.tensor_scalar(tg[:, 0, :], tb[:, 0:NQ], 0.0, None, ALU.is_gt))
                ch.link(v.tensor_tensor(tg[:, 1, :], tb[:, 0:NQ], tb[:, NQ:2 * NQ], ALU.add))
                v.tensor_tensor(gid[:, b, :], tg[:, 1, :], tg[:, 0, :], ALU.subtract).then_inc(s_gather_ids, 1)

            def scatter_rows(e, b):
                if above_zero(NQ * (e - 1)):
                    dve.wait_ge(s_weighed, NQ * (e - 1))
                if above_zero(16 * NQ * (e - 1)):
                    dve.wait_ge(s_scattered, 16 * NQ * (e - 1))
                tb = tab[:, bass.ds(e, 1), :].rearrange("p o n -> p (o n)")
                ch.mark(v.tensor_scalar(tk[:, 0, :], tb[:, 0:NQ], 0.0, None, ALU.is_gt))
                ch.mark(v.tensor_tensor(tk[:, 1, :], tb[:, 0:NQ], tb[:, NQ:2 * NQ], ALU.add))
                ch.link(v.tensor_tensor(tk[:, 3, :], tb[:, 2 * NQ:3 * NQ], tb[:, 3 * NQ:4 * NQ], ALU.add))
                ch.mark(v.tensor_tensor(kw[:, b, :], tb[:, 4 * NQ:5 * NQ], tk[:, 3, :], ALU.add))
                ch.link(v.scalar_tensor_tensor(tk[:, 2, :], cc("spare"), 1.0, tk[:, 0, :], ALU.add, ALU.mult))
                ch.link(v.tensor_tensor(tk[:, 2, :], tk[:, 1, :], tk[:, 2, :], ALU.subtract))
                v.tensor_tensor(sid[:, b, :], tk[:, 2, :], cc("spare"), ALU.add).then_inc(s_scatter_ids, 1)

            def expert(e, b, more):
                scatter_rows(e, b)
                if more:
                    dve.wait_ge(s_table, e + 2)
                for un in range(2 * FC):
                    half, f = un // FC, un % FC
                    dve.wait_ge(s_silu, e * (2 * FC) + (un + 1))
                    if un == 0:
                        if above_zero(e - 1):
                            dve.wait_ge(s_down, e - 1)
                    v.tensor_tensor(hT[:, b, f, half * HALF:(half + 1) * HALF], psum[:, un % 2, 0:HALF],
                                    sg[:, un % 2, :], ALU.mult).then_inc(s_hidden, 1)
                    if more and un < FC:
                        for j in range(un * NT // FC, (un + 1) * NT // FC):
                            one_hot(e + 2, j)
                    elif more and un == FC:
                        columns(e + 2)
                if more:
                    gather_rows(e + 2, b)

            ch.after()
            dve.wait_ge(s_pool_consts, 3 + 6)
            for e in range(2):
                if above_zero(e):
                    dve.wait_ge(s_table, e)
                for j in range(NT):
                    one_hot(e, j)
                columns(e)
                gather_rows(e, e)
            expert(0, 0, True)
            expert(1, 1, True)
            old = ch.base + ch.n
            PER = 2 * (6 + 1 + 3)
            with dve.Fori(1, E // 2 - 1) as i:
                ch.base, ch.n = old + (i - 1) * PER, 0
                for b in range(2):
                    expert(2 * i + b, b, True)
                assert ch.n == PER, ch.n
            ch.base, ch.n = old + (E // 2 - 2) * PER, 0
            expert(E - 2, 0, False)
            expert(E - 1, 1, False)

        @blk.scalar
        def _(act):
            a = nc.scalar
            ch = Chain(act, s_act)
            nc.scalar.dma_start(cst[:, 0:CW_EARLY], consts[:, 0:CW_EARLY]).then_inc(s_consts, 16)
            nc.scalar.dma_start(wx_s[:], wx).then_inc(s_wx, 16)
            nc.scalar.dma_start(wdt_s[:], wdt).then_inc(s_wdt, 16)
            nc.scalar.dma_start(small[:], vectors).then_inc(s_weights, 16)
            act.wait_ge(s_wx, 16)
            for k in range(2):
                a.activation(wbc[:, k], wx_s[:, RANK + NS * k:RANK + NS * (k + 1)].unsqueeze(2).to_broadcast([P, NS, GD]),
                             ACT.Copy).then_inc(s_spreaders, 1)
            act.wait_ge(s_consts, 16)
            a.activation(sel_r[:], cc("dup").rearrange("p (g o d) -> p g o d", o=1, d=GD).to_broadcast(
                [P, P // GD // 2, NS, GD]), ACT.Copy).then_inc(s_spreaders, 1)
            act.wait_ge(s_weights, 16)
            a.activation(nega[:], alog_s, ACT.Exp).then_inc(s_neg_a, 1)
            for c in range(NC):
                act.wait_ge(s_xn_turned, c + 1)
                a.activation(xnT[:, c * CH:(c + 1) * CH], bank(c), ACT.Copy).then_inc(s_xnT, 1)
            for c in range(NC):
                act.wait_ge(s_z, c + 1)
                a.activation(pre_a[:, c], bank(c), ACT.Abs, bias=bdt_s).then_inc(s_abs_z, 1)
                act.wait_ge(s_abs_z, c + 1)
                ch.mark(a.activation(pre_a[:, c], pre_a[:, c], ACT.Exp, scale=-1.0))
            ch.after()
            for c in range(NC):
                a.activation(pre_a[:, c], pre_a[:, c], ACT.Ln, bias=1.0).then_inc(s_log, 1)

            def high_and_c(c):
                for k, src in enumerate((pre_b, pre_c)):
                    act.wait_ge(s_delta, 2 * c + 1 + k)
                    if c >= SPLIT:
                        act.wait_ge(s_stack[c - SPLIT], 16 * 4)
                    a.activation(parts[:, c % SPLIT, 0, k], src[:, c], ACT.Copy).then_inc(s_high, 1)
                act.wait_ge(s_bc_product, 2 * c + 2)
                a.activation(cbc[:, c * CH:(c + 1) * CH], bank(5 + 2 * c % 4), ACT.Copy).then_inc(s_c, 1)

            high_and_c(0)
            act.wait_ge(s_neg_a, 2)
            act.wait_ge(s_pool_consts, 2)

            def decay(c, vv):
                for k in range(UG):
                    n, m = c * UPC + vv, c * NG + (UG * vv + k)
                    g = UG * vv + k
                    act.wait_ge(s_delta_spread, m + 1)
                    if k == 0 and above_zero(n - (RING - 1)):
                        act.wait_ge(s_state, n - (RING - 1))
                    src = bank(SPREAD_D + k).rearrange("p (b s) -> p b s", s=SEQ)
                    dst = da[:, vv % RING, k, :].rearrange("p (b s) -> p b s", s=SEQ)
                    a.activation(dst[:, :, 1:], src[:, :, 1:], ACT.Exp, scale=nega[:, g:g + 1]).then_inc(s_decay, 1)

            def post(c, step):
                if step == 0:
                    act.wait_ge(s_summed, c * UPC + UPC)
                    if above_zero(c):
                        act.wait_ge(s_y_turned, c)
                    a.activation(y2[:], bank(YB), ACT.Copy).then_inc(s_y, 1)
                elif step == 1:
                    act.wait_ge(s_x2, c + 1)
                    ch.link(a.activation(sm2[:, 1, :], sm2[:, 0, :], ACT.Ln))
                    a.activation(sm2[:, 2, :], sm2[:, 1, :], ACT.Exp, scale=-0.5).then_inc(s_rough2, 1)
                elif step == 2:
                    act.wait_ge(s_rstd2, c + 1)
                    if above_zero(16 * c):
                        act.wait_ge(s_rows_stored, 16 * c)
                    if above_zero(c):
                        act.wait_ge(s_xn2_turned, c)
                    for j in range(TPC):
                        a.activation(xn[:, j, :], xt[:, TPC * c + j, :], ACT.Identity, bias=sm2[:, 5, j:j + 1],
                                     scale=sm2[:, 4, j:j + 1]).then_inc(s_xn2, 1)
                elif step == 3:
                    act.wait_ge(s_xn2_turned, c + 1)
                    a.activation(x2T[:], bank(TB), ACT.Copy).then_inc(s_xn2T, 1)
                    act.wait_ge(s_logits_product, c + 1)
                    a.activation(lg[:, bass.ts(c, TPC), :], psum[:, RB, 0:TPC * E].rearrange("p (j e) -> p j e", e=E),
                                 ACT.Copy).then_inc(s_logits, 1)

            def chunk(c, first):
                for vv in range(UPC):
                    if not first and vv == LAG:
                        post(c - 1, 0)
                    decay(c, vv)
                    if first and vv + 1 < NC:
                        high_and_c(vv + 1)
                    if not first and vv > LAG + 1:
                        post(c - 1, vv - LAG - 1)

            chunk(0, True)
            old = ch.base + ch.n
            with act.Fori(1, NC) as c:
                ch.base, ch.n = old + (c - 1), 0
                chunk(c, False)
            ch.base, ch.n = old + NC - 1, 0
            for step in range(4):
                post(NC - 1, step)
            act.wait_ge(s_router, 1)
            a.activation(rb[:, 1, :], rb[:, 0, :], ACT.Exp).then_inc(s_exp, 1)

            act.wait_ge(s_fullest, 1)
            with act.If(act.value_load(fullest[0:1, 0:1]) > CAP):
                act.wait_ge(s_router, 2)
                for k in (1, 3):
                    js = slice(4 * k, 4 * k + 4)
                    a.activation(wmx[:, js], wm[:, js].unsqueeze(3).to_broadcast([P, 4, E, 16]),
                                 ACT.Copy).then_inc(s_copied_act, 1)

            def spread_tokens(e, b):
                if above_zero((e - 1) * 2 * FC):
                    act.wait_ge(s_up, (e - 1) * 2 * FC)
                act.wait_ge(s_rows_turned, 2 * e + 1)
                a.activation(xe[:, b, 0:CH], bank(4), ACT.Copy).then_inc(s_xe, 1)
                act.wait_ge(s_rows_turned, 2 * e + 2)
                a.activation(xe[:, b, CH:CAP], bank(6, CAP - CH), ACT.Copy).then_inc(s_xe, 1)

            def gates(e, b):
                for un in range(2 * FC):
                    g = e * (2 * FC) + un
                    act.wait_ge(s_up, g + 1)
                    if above_zero(g - 1):
                        act.wait_ge(s_hidden, g - 1)
                    a.activation(sg[:, un % 2, :], psum[:, 2 + un % 2, 0:HALF], ACT.Silu).then_inc(s_silu, 1)

            def weigh(e, b):
                act.wait_ge(s_down, e + 1)
                if above_zero(16 * NQ * (e - 1)):
                    act.wait_ge(s_scattered, 16 * NQ * (e - 1))
                for q in range(NQ):
                    a.activation(ye[:, b, q, :], psum[:, 5 + q // 4, (q % 4) * P:(q % 4 + 1) * P], ACT.Copy,
                                 scale=kw[:, b, q:q + 1]).then_inc(s_weighed, 1)

            def expert(e, b, more=True):
                gates(e, b)
                if more:
                    spread_tokens(e + 1, 1 - b)
                weigh(e, b)

            spread_tokens(0, 0)
            expert(0, 0)
            expert(1, 1)
            with act.Fori(1, E // 2 - 1) as i:
                for b in range(2):
                    expert(2 * i + b, b)
            expert(E - 2, 0)
            expert(E - 1, 1, False)

        @blk.gpsimd
        def _(pool):
            g = nc.gpsimd
            ch = Chain(pool, s_pool)
            g.memset(zero[:], 0.0).then_inc(s_pool_consts, 1)
            g.memset(da.rearrange("p r u (b s) -> p (r u b) s", s=SEQ)[:, :, 0:1], 0.0).then_inc(s_pool_consts, 1)
            g.memset(base[:, 0:1], 0).then_inc(s_pool_consts, 1)
            pool.wait_ge(s_neg_a, 1)
            g.tensor_scalar(nega[:], nega[:], -1.0, 0.0, ALU.mult, ALU.add).then_inc(s_neg_a, 1)
            pool.wait_ge(s_skip, 16)
            skip = drow[:].rearrange("p (o d) -> p o d", o=1).to_broadcast([P, TPC, D])
            for c in range(NC):
                js = slice(TPC * c, TPC * (c + 1))
                pool.wait_ge(s_xn, TPC * (c + 1))
                term = (y2, x2T)[c % 2][:].rearrange("p (j d) -> p j d", d=D)
                ch.link(g.tensor_tensor(term, xn[:, js, :], skip, ALU.mult))
                g.tensor_tensor(xt[:, js, :], xt[:, js, :], term, ALU.add).then_inc(s_residual, 1)

            def low(c):
                for k, full in enumerate((pre_b, pre_c)):
                    pool.wait_ge(s_high, 2 * c + k + 1)
                    if c >= SPLIT:
                        pool.wait_ge(s_stack[c - SPLIT], 16 * 4)
                    g.tensor_tensor(parts[:, c % SPLIT, 1, k], full[:, c], parts[:, c % SPLIT, 0, k].bitcast(F32),
                                    ALU.subtract).then_inc(s_low, 1)

            def product(c, vv):
                n, s = c * UPC + vv, vv % RING
                pool.wait_ge(s_state, n + 1)
                if above_zero(n - (RING - 1)):
                    pool.wait_ge(s_summed, n - (RING - 1))
                plain(pool)
                cb = cbc[:, bass.ts(c, CH)].rearrange("p (o n) -> p o n", o=1).to_broadcast([P, UG, CH])
                g.tensor_tensor(hc[:, s], hh[:, s], cb, ALU.mult).then_inc(s_product, 1)

            pool.wait_ge(s_low, 2)
            for vv in range(UPC):
                if vv + 1 < NC:
                    low(vv + 1)
                if vv == 0:
                    pool.wait_ge(s_c, 1)
                if vv < NC:
                    pool.wait_ge(s_low, 2 * vv + 2)
                product(0, vv)
            pool.wait_ge(s_c, NC)
            with pool.Fori(1, NC) as c:
                for vv in range(UPC):
                    product(c, vv)

            pool.wait_ge(s_late_consts, 16)
            for dst, src in ((ones_b, "ones"), (tri_b, "tri"), (blk_b, "blk"), (iota_b, "iota")):
                g.tensor_copy(dst[:], cc(src)).then_inc(s_pool_consts, 1)
            g.tensor_tensor(vals[:, 0, :], cc("ones")[:, 0:E * NT], cc("pval").to_broadcast([P, E * NT]),
                            ALU.mult).then_inc(s_pool_consts, 1)
            g.tensor_copy(vals[:, 1, :], cc("jval")).then_inc(s_pool_consts, 1)

            def gather_ready(e, b):
                pool.wait_ge(s_gather_ids, e + 1)
                if above_zero(2 * (e - 1)):
                    pool.wait_ge(s_rows_turned, 2 * (e - 1))
                plain(pool)

            def gather(b, q):
                g.indirect_dma_start(out=gx[:, b, q, :], out_offset=None, in_=rows,
                                     in_offset=bass.IndirectOffsetOnAxis(ap=gid[:, b, q:q + 1], axis=0)
                                     ).then_inc(s_gathered[b][q], 16)

            def expert(e, b, more=True):
                if more:
                    gather_ready(e + 2, b)
                    for q in range(NQ):
                        gather(b, q)
                pool.wait_ge(s_scatter_ids, e + 1)
                for q in range(NQ):
                    pool.wait_ge(s_weighed, NQ * e + q + 1)
                    if q == 0 and above_zero(16 * NQ * e):
                        pool.wait_ge(s_scattered, 16 * NQ * e)
                    plain(pool)
                    g.indirect_dma_start(out=out, out_offset=bass.IndirectOffsetOnAxis(ap=sid[:, b, q:q + 1], axis=0),
                                         in_=ye[:, b, q, :], in_offset=None, compute_op=ALU.add
                                         ).then_inc(s_scattered, 16)

            pool.wait_ge(s_rows_stored, 16 * NC)
            pool.wait_ge(s_out_stored, 16 * (NC + 1))
            for b in range(2):
                gather_ready(b, b)
                for q in range(NQ):
                    gather(b, q)
            for e in range(2):
                expert(e, e)
            with pool.Fori(1, E // 2 - 1) as i:
                for b in range(2):
                    expert(2 * i + b, b)
            expert(E - 2, 0, False)
            expert(E - 1, 1, False)

        @blk.tensor
        def _(pe):
            t = nc.tensor
            mm = t.matmul
            pe.wait_ge(s_consts, 16)
            for j in range(NT):
                pe.wait_ge(s_xn, j + 1)
                ins = t.transpose(psum[:, j // TPC, (j % TPC) * P:(j % TPC + 1) * P], xn[:, j, :], ident)
                if j % TPC == TPC - 1:
                    ins.then_inc(s_xn_turned, 1)
            pe.wait_ge(s_wx, 16)
            pe.wait_ge(s_wdt, 16)

            def outer(c):
                pe.wait_ge(s_xp, c + 1)
                mm(bank(c), wdt_s[:], xp_s[:, c * CH:(c + 1) * CH], start=True, stop=True).then_inc(s_z, 1)

            for c in range(NC):
                pe.wait_ge(s_xnT, c + 1)
                mm(psum[0:RANK, 4 + c, :], wx_s[:, 0:RANK], xnT[:, c * CH:(c + 1) * CH], start=True,
                   stop=True).then_inc(s_xp_product, 1)
                if c:
                    outer(c - 1)
            outer(NC - 1)
            pe.wait_ge(s_spreaders, 3)
            def bc_rows(c):
                for k in range(2):
                    if c >= 2:
                        pe.wait_ge((s_b, s_c)[k], c - 1)
                    mm(bank(4 + (2 * c + k) % 4), wbc[:, k].rearrange("p s d -> p (s d)"), xnT[:, c * CH:(c + 1) * CH],
                       start=True, stop=True).then_inc(s_bc_product, 1)

            for c in range(2):
                bc_rows(c)
            pe.wait_ge(s_abs_z, NC)
            pe.wait_ge(s_log, NC)
            pe.wait_ge(s_delta, 2)
            pe.wait_ge(s_late_consts, 16)

            def spread(c, vv):
                for k in range(UG):
                    grp, m = UG * vv + k, c * NG + (UG * vv + k)
                    half = grp // 8
                    sel = sel_r[:, grp % 8].rearrange("p s d -> p (s d)")
                    if above_zero(m - 1):
                        pe.wait_ge(s_decay, m - 1)
                    mm(bank(SPREAD_D + k), sel, stack[:, half, 0, bass.ts(c, CH)], start=True, stop=True).then_inc(s_delta_spread, 1)
                    if above_zero(m - 1):
                        pe.wait_ge(s_input, m - 1)
                    mm(bank(SPREAD_X + k), sel, stack[:, half, 1, bass.ts(c, CH)], start=True, stop=True).then_inc(s_dx_spread, 1)

            def reduce(c, vv):
                n, s = c * UPC + vv, vv % RING
                pe.wait_ge(s_product, n + 1)
                if vv == 0:
                    if above_zero(c):
                        pe.wait_ge(s_y, c)
                    else:
                        pe.wait_ge(s_b, NC)
                        pe.wait_ge(s_c, NC)
                for k in range(UG):
                    grp = UG * vv + k
                    o = D - GD - GD * grp
                    ins = mm(bank(YB), wred[:, o:o + D], hc[:, s, k, :], start=(grp == 0), stop=(grp == NG - 1))
                ins.then_inc(s_summed, 1)

            def post(c, step):
                if step == 0:
                    pe.wait_ge(s_y, c + 1)
                    if above_zero(c):
                        pe.wait_ge(s_xn2T, c)
                    for j in range(TPC):
                        ins = t.transpose(psum[:, TB, j * P:(j + 1) * P], y2[:, j * P:(j + 1) * P], ident)
                    ins.then_inc(s_y_turned, 1)
                elif step == 1:
                    pe.wait_ge(s_xn2, TPC * c + TPC)
                    for j in range(TPC):
                        ins = t.transpose(psum[:, TB, j * P:(j + 1) * P], xn[:, j, :], ident)
                    ins.then_inc(s_xn2_turned, 1)
                elif step == 2:
                    pe.wait_ge(s_xn2T, c + 1)
                    if above_zero(c):
                        pe.wait_ge(s_logits, c)
                    for j in range(TPC):
                        ins = mm(psum[:, RB, j * E:(j + 1) * E], x2T[:, j * P:(j + 1) * P], wr_s, start=True, stop=True)
                    ins.then_inc(s_logits_product, 1)

            def chunk(c, first):
                for vv in range(UPC):
                    spread(c, vv)
                    if first and vv + 2 < NC:
                        bc_rows(vv + 2)
                    if not first and vv == LAG:
                        post(c - 1, 0)
                    if not first and vv == UPC - 1:
                        post(c - 1, 1)
                    if vv >= LAG:
                        reduce(c, vv - LAG)
                        if not first and vv == UPC - 1:
                            post(c - 1, 2)
                    elif not first:
                        reduce(c - 1, UPC - LAG + vv)

            pe.wait_ge(s_stack[0], 16 * 4)
            chunk(0, True)
            for c in range(1, NC):
                pe.wait_ge(s_stack[c], 16 * 4)
            with pe.Fori(1, NC) as c:
                chunk(c, False)
            for vv in range(LAG):
                reduce(NC - 1, UPC - LAG + vv)
            for step in range(3):
                post(NC - 1, step)

            def flat(a):
                return a[:].rearrange("p e j -> p (e j)")

            pe.wait_ge(s_pool_consts, 3 + 6)
            pe.wait_ge(s_logits, NC)
            pe.wait_ge(s_chosen, 1)
            mm(bank(6, P), ones_b[:], flat(kp_b), start=True, stop=True)
            mm(bank(7, P), tri_b[:], flat(kp_b), start=True, stop=True).then_inc(s_chosen_counted, 1)

            pe.wait_ge(s_fullest, 1)
            with pe.If(pe.value_load(fullest[0:1, 0:1]) > CAP):
                for j in range(NT):
                    if j % 4 == 0:
                        pe.wait_ge((s_copied_dve, s_copied_act)[j // 4 % 2], j // 8 + 1)
                    ins = t.transpose(psum[:, j // 4, (j % 4) * P:(j % 4 + 1) * P],
                                      wmx[:, j].rearrange("p e r -> p (e r)"), ident)
                ins.then_inc(s_weights_turned, 1)
                for r in range(NROUND):
                    pe.wait_ge(s_indicator, r + 1)
                    mm(psum[:, 4, r:r + 1], blk_b[:], ind[:, r:r + 1], start=True, stop=True).then_inc(s_digit, 1)
                pe.wait_ge(s_tau_rows, 1)
                mm(psum[:, 4, 32:32 + E], cc("ones"), taud[:], start=True, stop=True).then_inc(s_tau, 1)
                pe.wait_ge(s_above, 2)
                mm(bank(5, P), ones_b[:], flat(gt_b), start=True, stop=True)
                mm(bank(6, P), ones_b[:], flat(eq_b), start=True, stop=True)
                mm(bank(7, P), tri_b[:], flat(eq_b), start=True, stop=True).then_inc(s_counted, 1)
                pe.wait_ge(s_keep, 1)
                mm(bank(6, P), ones_b[:], flat(kp_b), start=True, stop=True)
                mm(bank(7, P), tri_b[:], flat(kp_b), start=True, stop=True).then_inc(s_keep_counted, 1)

            def table(e):
                pe.wait_ge(s_one_hot, e + 1)
                if above_zero(e):
                    pe.wait_ge(s_gather_ids, e)
                for j in range(NT):
                    ins = mm(psum[:, 7, 0:5 * NQ], oh[:, j, :], rq[:, :, j, :], start=(j == 0), stop=(j == NT - 1))
                ins.then_inc(s_table, 1)

            def turn(e, b, i):
                for q in range(NQ):
                    pe.wait_ge(s_gathered[b][q], 16 * i + 16)
                    if q == 0:
                        if above_zero(2 * e):
                            pe.wait_ge(s_xe, 2 * e)
                    if q == 4:
                        if above_zero(NQ * (e - 1)):
                            pe.wait_ge(s_weighed, NQ * (e - 1))
                    ins = t.transpose(psum[:, 4 + 2 * (q // 4), (q % 4) * P:(q % 4 + 1) * P], gx[:, b, q, :], ident)
                    if q >= 3:
                        ins.then_inc(s_rows_turned, 1)

            def up(e, b, i):
                pe.wait_ge(s_expert_weights[b], 48 * i + 48)
                for un in range(2 * FC):
                    half, f = un // FC, un % FC
                    g = e * (2 * FC) + un
                    pe.wait_ge(s_xe, 2 * e + 1 + half)
                    if above_zero(g - 1):
                        pe.wait_ge(s_silu, g - 1)
                    cs = slice(half * HALF, (half + 1) * HALF)
                    mm(psum[:, 2 + un % 2, 0:HALF], wg_s[:, b, f * P:(f + 1) * P], xe[:, b, cs], start=True, stop=True)
                    if above_zero(g - 1):
                        pe.wait_ge(s_hidden, g - 1)
                    mm(psum[:, un % 2, 0:HALF], w1_s[:, b, f * P:(f + 1) * P], xe[:, b, cs], start=True,
                       stop=True).then_inc(s_up, 1)

            def down(e, b, turned=None):
                pe.wait_ge(s_hidden, (e + 1) * 2 * FC)
                if above_zero(NQ * e):
                    pe.wait_ge(s_weighed, NQ * e)
                for q in range(NQ):
                    if q == 4 and turned is not None:
                        pe.wait_ge(s_xe, turned)
                    for f in range(FC):
                        ins = mm(psum[:, 5 + q // 4, (q % 4) * P:(q % 4 + 1) * P], hT[:, b, f, q * P:(q + 1) * P],
                                 w2_s[:, b, f, :], start=(f == 0), stop=(f == FC - 1))
                ins.then_inc(s_down, 1)

            def expert(i, b, more=True, turn_next=True):
                e = 2 * i + b
                up(e, b, i)
                if more:
                    table(e + 2)
                if turn_next:
                    turn(e + 1, 1 - b, i + b)
                down(e, b, 2 * e + 4 if turn_next else None)

            table(0)
            table(1)
            turn(0, 0, 0)
            expert(0, 0)
            expert(0, 1)
            with pe.Fori(1, E // 2 - 1) as i:
                for b in range(2):
                    expert(i, b)
            expert(E // 2 - 1, 0, False)
            expert(E // 2 - 1, 1, False, False)


def kernel(L0_attn_x, L0_attn_W_xproj, L0_attn_W_dt, L0_attn_b_dt, L0_attn_A_log, L0_attn_D, L0_ffn_router_weight,
           L0_ffn_ff_pre_act_weight, L0_ffn_gate_weight, L0_ffn_ff_post_act_weight):
    import concourse.bacc as bacc
    from concourse.bass_utils import run_bass_kernel_spmd

    def lay(a):
        return np.ascontiguousarray(a)

    x = np.asarray(L0_attn_x)
    alog = np.asarray(L0_attn_A_log).reshape(NG, GD, NS).transpose(2, 1, 0).reshape(P, NG)
    small = np.concatenate([np.asarray(L0_attn_b_dt)[:, None], alog,
                            np.asarray(L0_ffn_router_weight).T], axis=1)
    arrays = {
        "x": lay(x.reshape(T, D)),
        "wx": lay(np.asarray(L0_attn_W_xproj).T),
        "wdt": lay(np.asarray(L0_attn_W_dt).T),
        "small": lay(small),
        "dskip": lay(np.broadcast_to(np.asarray(L0_attn_D), (P, D))),
        "w1": lay(np.asarray(L0_ffn_ff_pre_act_weight).transpose(0, 2, 1)),
        "wg": lay(np.asarray(L0_ffn_gate_weight).transpose(0, 2, 1)),
        "w2": lay(np.asarray(L0_ffn_ff_post_act_weight).reshape(E, D, FC, P).transpose(0, 3, 2, 1)),
        "consts": shape_constants(),
        "jbits": search_bits(),
    }
    nc = bacc.Bacc("TRN2", target_bir_lowering=False, num_devices=1)
    ap = {k: nc.dram_tensor("in_" + k, a.shape, mybir.dt.from_np(a.dtype), kind="ExternalInput").ap() for k, a in arrays.items()}
    out = nc.dram_tensor("out", [T + CAP, D], F32, kind="ExternalOutput").ap()
    rows = nc.dram_tensor("rows", [T, D], F32, kind="Internal").ap()
    build(nc, ap["x"], ap["wx"], ap["wdt"], ap["small"], ap["dskip"], ap["w1"], ap["wg"], ap["w2"], ap["consts"],
          ap["jbits"], out, rows)
    r = run_bass_kernel_spmd(nc, [{"in_" + k: a for k, a in arrays.items()}], core_ids=[0])
    return r.results[0]["out"][:T].reshape(BATCH, SEQ, D)
```

```python
from contextlib import ExitStack

import numpy as np

import concourse.bass as bass
from concourse import mybir

F32 = mybir.dt.float32
F32R = mybir.dt.float32r
BF16 = mybir.dt.bfloat16
I32 = mybir.dt.int32
ALU = mybir.AluOpType
ACT = mybir.ActivationFunctionType
AX = mybir.AxisListType

P = 128
BATCH, SEQ, D = 8, 256, 128
T = BATCH * SEQ
NT = T // P
NS = 16
GD = P // NS
NG = D // GD
RANK = 64
CH = 512
NC = T // CH
TPC = CH // P
UG = 2
UPC = NG // UG
RING = 4
SPLIT = 3
DIRECT = 2
STACKED = 16 * 4
WARM = dict(rows=33, turned=6, rank=8, parts=38, rows2=46, slots=30, columns=34, gathered=4)
LAG = 3

E = 8
DFF = 512
FC = DFF // P
CAP = 640
NQ = CAP // P
QA = 3
HALF = CAP // 2
EPS_LN = 1e-05
EPS_W = 1.1920929e-07
NROUND = 8
SHIFT = [26 - 4 * r for r in range(NROUND - 1)] + [0]

CONST = [("ident", P), ("dup", RANK), ("wred", P + D - GD), ("ones", P), ("tri", P), ("blk", P), ("iota", P),
         ("selcol", E), ("desc", NT * E), ("smask", E * NT), ("jval", E * NT), ("q5", NQ), ("pval", 1),
         ("spare1", NQ)]
COFF, _o = {}, 0
for _n, _w in CONST:
    COFF[_n] = (_o, _w)
    _o += _w
CW = _o
CW_EARLY = P + RANK


def shape_constants():
    p = np.arange(P)
    c = {
        "ident": np.eye(P),
        "ones": np.ones((P, P)),
        "tri": p[:, None] <= p[None, :],
        "blk": (p[:, None] // 16 == p[None, :] // 16) & (p[:, None] % 16 > 0),
        "iota": np.broadcast_to(p[None, :] + 1, (P, P)),
        "wred": (np.arange(P + D - GD)[None, :] == (D - GD) + p[:, None] % GD),
        "dup": p[:, None] % RANK == np.arange(RANK)[None, :],
        "selcol": p[:, None] == 16 * np.arange(E)[None, :],
        "desc": np.broadcast_to(E - np.arange(NT * E) % E, (P, NT * E)),
        "smask": np.broadcast_to(np.arange(E * NT) % NT > 0, (P, E * NT)),
        "jval": np.broadcast_to(P * (np.arange(E * NT) % NT), (P, E * NT)),
        "q5": np.broadcast_to(np.arange(NQ), (P, NQ)),
        "pval": p[:, None] + 1,
        "spare1": T + P * np.arange(NQ)[None, :] + p[:, None] + 1,
    }
    return np.concatenate([np.asarray(c[n], np.float32) for n, _ in CONST], axis=1)


def search_bits():
    j = (np.arange(P) % 16)[:, None]
    cols = [j << s for s in SHIFT[:-1]] + [np.where(j < 4, j, 0x40000000)]
    return np.concatenate(cols, axis=1).astype(np.int32)


def build(nc, x, wx, wdt, vectors, dskip, w1, wg, w2, consts, jbits, out, rows):
    with ExitStack() as ctx:
        def sb(name, shape, dt=F32):
            return ctx.enter_context(nc.sbuf_tensor(name, shape, dt))

        def sem(name):
            return ctx.enter_context(nc.semaphore(name))

        psum = ctx.enter_context(nc.psum_tensor("psum", [P, 8, CH], F32))

        cst = sb("cst", [P, CW])

        def cc(name):
            o, w = COFF[name]
            return cst[:, o:o + w]

        ident = cc("ident")
        jb = sb("jb", [P, NROUND], I32)
        wx_s = sb("wx_s", [P, RANK + 2 * NS])
        wdt_s = sb("wdt_s", [RANK, D])
        small = sb("small", [P, 1 + NG + E])
        bdt_s, alog_s, wr_s = small[:, 0:1], small[:, 1:1 + NG], small[:, 1 + NG:1 + NG + E]
        nega = sb("nega", [P, NG])
        wred = cc("wred")
        sel_r = sb("sel_r", [P, P // GD // 2, NS, GD], F32R)
        wbc = sb("wbc", [P, 2, NS, GD])
        ones_b = sb("ones_b", [P, P], BF16)
        tri_b = sb("tri_b", [P, P], BF16)
        blk_b = sb("blk_b", [P, P], BF16)
        iota_b = sb("iota_b", [P, P], BF16)

        xt = sb("xt", [P, NT, D])
        xn = sb("xn", [P, NT, D])
        xnT = sb("xnT", [P, T])
        bbc = sb("bbc", [P, T])
        cbc = sb("cbc", [P, T])
        parts = sb("parts", [P, SPLIT, 2, 2, CH], F32R)
        drow = sb("drow", [P, D])
        stack = sb("stack", [P, 2, 2, T], F32R)
        stat = sb("stat", [P, NT, 6])
        mv = sb("mv", [P, NT, 2])
        ve = sb("ve", [P, NT])
        r0 = sb("r0", [P, NT])
        rt = sb("rt", [P, NT])
        rstd = sb("rstd", [P, NT])
        stat2 = sb("stat2", [P, TPC, 6])
        mv2 = sb("mv2", [P, TPC, 2])
        sm2 = sb("sm2", [P, 6, TPC])
        ring = sb("ring", [P, 4 * RING * UG * CH])
        da, uu, hh, hc = (ring[:, k * RING * UG * CH:(k + 1) * RING * UG * CH].rearrange(
            "p (r u n) -> p r u n", r=RING, u=UG) for k in range(4))
        wmx = xnT[:].rearrange("p (j e r) -> p j e r", e=E, r=16)
        taken = [0]

        def later(*shape):
            n = int(np.prod(shape))
            o = taken[0]
            taken[0] += n
            assert taken[0] <= 4 * RING * UG * CH
            names = "abc"[:len(shape)]
            return ring[:, o:o + n].rearrange(f"p ({' '.join(names)}) -> p {' '.join(names)}",
                                              **dict(zip(names, shape)))
        y2 = sb("y2", [P, CH])
        x2T = sb("x2T", [P, CH])

        lg = sb("lg", [P, NT, E])
        rb = sb("rb", [P, 10, NT * E])
        r16 = sb("r16", [P, 10, NT])
        wm = sb("wm", [P, NT, E])
        fullest = sb("fullest", [P, 1], I32)
        cnt = sb("cnt", [P, NROUND])
        ind = sb("ind", [P, NROUND], BF16)
        base = sb("base", [P, NROUND + 1], I32)
        thr = sb("thr", [P, NROUND], I32)
        digs = sb("digs", [P, NROUND], I32)
        taud = sb("taud", [P, E])
        gt_b = sb("gt_b", [P, E, NT], BF16)
        eq_b = sb("eq_b", [P, E, NT], BF16)
        kp_b = sb("kp_b", [P, E, NT], BF16)
        lim = sb("lim", [P, 2, E])
        qq = sb("qq", [P, E * NT])
        r1 = sb("r1", [P, E * NT])
        vals = sb("vals", [P, 5, E * NT], BF16)

        win_s = sb("win_s", [P, 2, 2, DFF])
        w2_s = sb("w2_s", [P, 2, FC, D])
        win_rows = win_s[:].rearrange("p b k f -> p (b k) f")
        w2_rows = w2_s[:].rearrange("p b f d -> p b (f d)")
        pre_a = [uu[:, 0, 0]] + [xn[:, TPC * c:TPC * (c + 1)].rearrange("p j d -> p (j d)")
                                 for c in range(1, NC)]
        pre_b = [hc[:, 0, 0]] + [win_rows[:, c] for c in range(NC - 1)]
        pre_c = [hc[:, 0, 1], win_rows[:, NC - 1]] + [w2_rows[:, c] for c in range(NC - 2)]
        oh = later(NT, P // 2).bitcast(BF16)
        q1 = sb("q1", [P, NT, NQ], BF16)
        rq = sb("rq", [P, 5, NT, NQ], BF16)
        tab = sb("tab", [P, 2, 5 * NQ])
        token = sb("token", [P, 2, NQ])
        tk = sb("tk", [P, 2, NQ])
        gid = sb("gid", [P, 2, NQ], I32)
        sid = sb("sid", [P, 2, NQ], I32)
        kw = sb("kw", [P, 2, NQ])
        gx = later(2, NQ, D)
        stack_flat = stack[:].rearrange("p h k t -> p (h k t)")
        win_p = stack_flat[:, 0:8 * DFF].rearrange("p (b i k f) -> p b i k f", b=2, i=2, k=2)
        xe_p = stack_flat[:, 8 * DFF:8 * DFF + 4 * CAP].rearrange("p (b i n) -> p b i n", b=2, i=2)
        sg = later(2, HALF)
        hT = later(2, FC, CAP)
        ye = later(2, NQ, D)
        zero = sb("zero", [P, D])

        s_consts = sem("s_consts")
        s_late_consts = sem("s_late_consts")
        s_skip = sem("s_skip")
        s_weights = sem("s_weights")
        s_wx = sem("s_wx")
        s_wdt = sem("s_wdt")
        s_bits = sem("s_bits")
        s_spreaders = sem("s_spreaders")
        s_neg_a = sem("s_neg_a")
        s_pool_consts = sem("s_pool_consts")
        s_passed = sem("s_passed")
        s_dve = sem("s_dve")
        s_act = sem("s_act")
        s_pool = sem("s_pool")
        s_residual = sem("s_residual")
        s_xn = sem("s_xn")
        s_xn_turned = sem("s_xn_turned")
        s_xnT = sem("s_xnT")
        s_xp_product = sem("s_xp_product")
        s_xp = sem("s_xp")
        s_bc_product = sem("s_bc_product")
        s_b = sem("s_b")
        s_c = sem("s_c")
        s_z = sem("s_z")
        s_positive = sem("s_positive")
        s_abs_z = sem("s_abs_z")
        s_log = sem("s_log")
        s_delta = sem("s_delta")
        s_high = sem("s_high")
        s_low = sem("s_low")
        s_delta_spread = sem("s_delta_spread")
        s_dx_spread = sem("s_dx_spread")
        s_decay = sem("s_decay")
        s_input = sem("s_input")
        s_state = sem("s_state")
        s_product = sem("s_product")
        s_summed = sem("s_summed")
        s_y = sem("s_y")
        s_y_turned = sem("s_y_turned")
        s_x2 = sem("s_x2")
        s_rough2 = sem("s_rough2")
        s_rstd2 = sem("s_rstd2")
        s_xn2 = sem("s_xn2")
        s_xn2_turned = sem("s_xn2_turned")
        s_xn2T = sem("s_xn2T")
        s_last_xn2 = sem("s_last_xn2")
        s_last_xn2_turned = sem("s_last_xn2_turned")
        s_last_xn2T = sem("s_last_xn2T")
        s_logits_product = sem("s_logits_product")
        s_logits = sem("s_logits")
        s_rows_stored = sem("s_rows_stored")
        s_out_stored = sem("s_out_stored")
        s_router = sem("s_router")
        s_exp = sem("s_exp")
        s_chosen = sem("s_chosen")
        s_chosen_counted = sem("s_chosen_counted")
        s_fullest = sem("s_fullest")
        s_search = sem("s_search")
        s_copied_dve = sem("s_copied_dve")
        s_copied_act = sem("s_copied_act")
        s_weights_turned = sem("s_weights_turned")
        s_indicator = sem("s_indicator")
        s_digit = sem("s_digit")
        s_tau_rows = sem("s_tau_rows")
        s_tau = sem("s_tau")
        s_above = sem("s_above")
        s_counted = sem("s_counted")
        s_keep = sem("s_keep")
        s_keep_counted = sem("s_keep_counted")
        s_columns = sem("s_columns")
        s_first_one_hot = sem("s_first_one_hot")
        s_table = sem("s_table")
        s_gather_ids = sem("s_gather_ids")
        s_scatter_ids = sem("s_scatter_ids")
        s_rows_turned = sem("s_rows_turned")
        s_xe = sem("s_xe")
        s_xe_low = sem("s_xe_low")
        s_in_high = sem("s_in_high")
        s_in_low = sem("s_in_low")
        s_down_tile = sem("s_down_tile")
        s_up = sem("s_up")
        s_silu = sem("s_silu")
        s_hidden = sem("s_hidden")
        s_down = sem("s_down")
        s_weighed = sem("s_weighed")
        s_scattered = sem("s_scattered")
        s_x = [sem(f"s_x_chunk{c}") for c in range(NC)]
        s_stack = sem("s_stack")
        s_in_weights = [sem(f"s_in_weights{b}") for b in range(2)]
        s_out_weights = [sem(f"s_out_weights{b}") for b in range(2)]
        s_gathered = [[sem(f"s_gathered{b}{q}") for q in range(NQ)] for b in range(2)]

        blk = ctx.enter_context(nc.Block())
        xv = x.rearrange("(c j p) d -> c p j d", j=TPC, p=P)
        outv = out[0:T, :].rearrange("(c j p) d -> c p j d", j=TPC, p=P)
        rowv = rows.rearrange("(c j p) d -> c p j d", j=TPC, p=P)

        def bank(k, w=CH):
            return psum[:, k, 0:w]

        SPREAD_D, SPREAD_X, YB, TB, RB = 0, 2, 4, 5, 6
        TURNED, XPB, ZB, BB, CB = (0, 4, 4, 4), (5, 5, 5, 5), (7, 6, 7, 6), (6, 7, 7, 7), (5, 5, 5, 5)
        LAST_BANK = (5, 6, 7, 4, 0)

        def above_zero(value):
            return not isinstance(value, int) or value > 0

        def plain(eng):
            eng.sem_inc(s_passed, 1)

        class Chain:

            def __init__(self, eng, own):
                self.eng, self.own, self.n, self.base = eng, own, 0, 0

            def mark(self, ins):
                self.n += 1
                ins.then_inc(self.own, 1)
                return self.n

            def until(self, n):
                self.eng.wait_ge(self.own, self.base + n)

            def after(self):
                self.eng.wait_ge(self.own, self.base + self.n)

            def link(self, ins):
                self.mark(ins)
                self.after()

        @blk.sync
        def _(sp):
            for c in range(NC):
                nc.sync.dma_start(xt[:, TPC * c:TPC * (c + 1), :], xv[c]).then_inc(s_x[c], 16)
            nc.sync.dma_start(drow[:], dskip).then_inc(s_skip, 16)
            nc.sync.dma_start(cst[:, CW_EARLY:], consts[:, CW_EARLY:]).then_inc(s_late_consts, 16)
            nc.sync.dma_start(jb[:], jbits).then_inc(s_bits, 16)
            for c in range(NC):
                cs = slice(c * CH, (c + 1) * CH)
                if c:
                    sp.wait_ge(s_stack, STACKED * c)
                for part, ready in enumerate((s_high, s_low)):
                    sp.wait_ge(ready, 2 * c + 2)
                    rows_to = slice(64 * part, 64 * part + 64)
                    for half in range(2):
                        rows_from = slice(64 * half, 64 * half + 64)
                        nc.sync.dma_start(stack[rows_to, half, :, cs].bitcast(F32),
                                          parts[rows_from, c % SPLIT, part].bitcast(F32)).then_inc(s_stack, 16)
            sp.wait_ge(s_pool_consts, 1)
            nc.sync.dma_start(out[T:T + CAP, :].rearrange("(q p) d -> p q d", p=P),
                              zero[:].rearrange("p (o d) -> p o d", o=1).to_broadcast([P, NQ, D])).then_inc(s_out_stored, 16)
            for e in range(2):
                nc.sync.dma_start(win_s[:, e, 0, :], wg[e]).then_inc(s_in_weights[e], 16)
                nc.sync.dma_start(win_s[:, e, 1, :], w1[e]).then_inc(s_in_weights[e], 16)
                nc.sync.dma_start(w2_s[:, e, :, :], w2[e]).then_inc(s_out_weights[e], 16)
            with sp.Fori(0, NC - 1) as c:
                sp.wait_ge(s_x2, c + 1)
                nc.sync.dma_start(outv[c], xt[:, bass.ts(c, TPC), :]).then_inc(s_out_stored, 16)
                sp.wait_ge(s_xn2, TPC * c + TPC)
                nc.sync.dma_start(rowv[c], xn[:, 0:TPC, :]).then_inc(s_rows_stored, 16)
            sp.wait_ge(s_x2, NC)
            nc.sync.dma_start(outv[NC - 1], xt[:, TPC * (NC - 1):, :]).then_inc(s_out_stored, 16)
            sp.wait_ge(s_xn2, TPC * (NC - 1) + 1)
            sp.wait_ge(s_last_xn2, TPC - 1)
            nc.sync.dma_start(rowv[NC - 1], xn[:, 0:TPC, :]).then_inc(s_rows_stored, 16)
            with sp.Fori(0, E // 2 - 1) as i:
                for b in range(2):
                    sp.wait_ge(s_in_low, 4 * i + (2 * b + 2))
                    nc.sync.dma_start(win_s[:, b, 0, :], wg[2 * i + (2 + b)]).then_inc(s_in_weights[b], 16)
                    nc.sync.dma_start(win_s[:, b, 1, :], w1[2 * i + (2 + b)]).then_inc(s_in_weights[b], 16)
                    sp.wait_ge(s_down, 2 * i + (b + 1))
                    nc.sync.dma_start(w2_s[:, b, :, :], w2[2 * i + (2 + b)]).then_inc(s_out_weights[b], 16)
            sp.wait_ge(s_out_stored, 16 * (NC + 1))
            sp.wait_ge(s_rows_stored, 16 * NC)
            sp.wait_ge(s_scattered, 16 * E * NQ)

        @blk.vector
        def _(dve):
            ch = Chain(dve, s_dve)
            v = nc.vector
            def row_stats(j):
                ch.mark(v.bn_stats(stat[:, j, :], xt[:, j, :]))

            def row_rstd(js, between=()):
                between = list(between)

                def link(ins):
                    n = ch.mark(ins)
                    if between:
                        j = between.pop(0)
                        if j % TPC == 0:
                            dve.wait_ge(s_x[j // TPC], 16)
                        row_stats(j)
                    ch.until(n)

                for j in range(js.start, js.stop):
                    ch.mark(v.bn_aggr(mv[:, j, :], stat[:, j, :]))
                ch.after()
                link(v.tensor_scalar(ve[:, js], mv[:, js, 1], EPS_LN, None, ALU.add))
                link(v.tensor_scalar(r0[:, js].bitcast(I32), ve[:, js].bitcast(I32), 1, None, ALU.logical_shift_right))
                link(v.tensor_scalar(rstd[:, js].bitcast(I32), r0[:, js].bitcast(I32), -1.0, float(0x5f3759df), ALU.mult,
                                     ALU.add))
                for _ in range(3):
                    link(v.tensor_tensor(rt[:, js], rstd[:, js], rstd[:, js], ALU.mult))
                    link(v.scalar_tensor_tensor(rt[:, js], rt[:, js], -0.5, ve[:, js], ALU.mult, ALU.mult))
                    link(v.scalar_tensor_tensor(rstd[:, js], rt[:, js], 1.5, rstd[:, js], ALU.add, ALU.mult))
                assert len(between) == 0

            def normalise(j):
                v.tensor_scalar(xn[:, j, :], xt[:, j, :], mv[:, j, 0:1], rstd[:, j:j + 1], ALU.subtract,
                                ALU.mult).then_inc(s_xn, 1)

            def positive(c):
                dve.wait_ge(s_abs_z, c + 1)
                v.tensor_scalar(pre_b[c], bank(ZB[c]), bdt_s, 0.0, ALU.add, ALU.max).then_inc(s_positive, 1)

            def delta(c):
                dve.wait_ge(s_log, c + 1)
                dve.wait_ge(s_positive, c + 1)
                v.tensor_tensor(pre_b[c], pre_b[c], pre_a[c], ALU.add).then_inc(s_delta, 1)
                dve.wait_ge(s_xnT, c + 1)
                dve.wait_ge(s_delta, 2 * c + 1)
                v.tensor_tensor(pre_c[c], pre_b[c], xnT[:, c * CH:(c + 1) * CH], ALU.mult).then_inc(s_delta, 1)

            def b_rows(c):
                dve.wait_ge(s_bc_product, 2 * c + 1)
                v.tensor_copy(bbc[:, c * CH:(c + 1) * CH], bank(BB[c])).then_inc(s_b, 1)

            dve.wait_ge(s_x[0], 16)
            for j in range(TPC):
                row_stats(j)
            ch.after()
            row_rstd(slice(0, TPC), range(TPC, NT))
            for j in range(TPC):
                normalise(j)
            ch.after()
            row_rstd(slice(TPC, NT))
            for j in range(TPC, 3 * TPC):
                normalise(j)
            dve.wait_ge(s_weights, 16)
            positive(0)
            b_rows(0)
            delta(0)
            for k, full in enumerate((pre_b, pre_c)):
                dve.wait_ge(s_high, k + 1)
                v.tensor_tensor(parts[:, 0, 1, k], full[0], parts[:, 0, 0, k].bitcast(F32),
                                ALU.subtract).then_inc(s_low, 1)
            for j in range(3 * TPC, NT):
                normalise(j)
            dve.wait_ge(s_b, 1)

            def u_step(c, vv):
                for k in range(UG):
                    n, m = c * UPC + vv, c * NG + (UG * vv + k)
                    dve.wait_ge(s_dx_spread, m + 1)
                    if k == 0 and above_zero(n - (RING - 1)):
                        dve.wait_ge(s_state, n - (RING - 1))
                    v.tensor_tensor(uu[:, vv % RING, k, :], bank(SPREAD_X + k), bbc[:, bass.ts(c, CH)],
                                    ALU.mult).then_inc(s_input, 1)

            def scan_step(c, vv):
                n, s = c * UPC + vv, vv % RING
                dve.wait_ge(s_input, n * UG + UG)
                dve.wait_ge(s_decay, n * UG + UG)
                if above_zero(n - (RING - 1)):
                    dve.wait_ge(s_product, n - (RING - 1))
                v.tensor_tensor_scan(hh[:, s].rearrange("p a b -> p (a b)"), da[:, s].rearrange("p a b -> p (a b)"),
                                     uu[:, s].rearrange("p a b -> p (a b)"), 0.0, ALU.mult, ALU.add).then_inc(s_state, 1)

            def post(c, step):
                if step == 0:
                    dve.wait_ge(s_y_turned, c + 1)
                    ch.link(v.tensor_tensor(xt[:, bass.ts(c, TPC), :], xt[:, bass.ts(c, TPC), :],
                                            bank(TB).rearrange("p (j d) -> p j d", d=D), ALU.add))
                    plain(dve)
                    for j in range(TPC):
                        ch.mark(v.bn_stats(stat2[:, j, :], xt[:, TPC * c + j, :]))
                elif step == 1:
                    ch.after()
                    plain(dve)
                    for j in range(TPC):
                        ch.mark(v.bn_aggr(mv2[:, j, :], stat2[:, j, :]))
                elif step == 2:
                    ch.after()
                    v.tensor_scalar(sm2[:, 0, :], mv2[:, :, 1], EPS_LN, None, ALU.add).then_inc(s_x2, 1)
                elif step == 3:
                    dve.wait_ge(s_rough2, c + 1)
                    ch.link(v.tensor_tensor(sm2[:, 3, :], sm2[:, 2, :], sm2[:, 2, :], ALU.mult))
                    ch.link(v.scalar_tensor_tensor(sm2[:, 3, :], sm2[:, 3, :], -0.5, sm2[:, 0, :], ALU.mult, ALU.mult))
                    ch.link(v.scalar_tensor_tensor(sm2[:, 4, :], sm2[:, 3, :], 1.5, sm2[:, 2, :], ALU.add, ALU.mult))
                    v.scalar_tensor_tensor(sm2[:, 5, :], mv2[:, :, 0], -1.0, sm2[:, 4, :], ALU.mult,
                                           ALU.mult).then_inc(s_rstd2, 1)

            def chunk(c, first):
                for vv in range(UPC):
                    if not first and vv == LAG + 1:
                        post(c - 1, 1)
                    if first and vv == 0:
                        dve.wait_ge(s_delta, 1)
                    u_step(c, vv)
                    if first and 2 <= vv < NC + 1:
                        positive(vv - 1)
                    if first and NC <= vv < 2 * NC - 1:
                        b_rows(vv - NC + 1)
                        delta(vv - NC + 1)
                        dve.wait_ge(s_b, vv - NC + 2)
                    if not first and vv == LAG + 1:
                        post(c - 1, 2)
                    if vv:
                        scan_step(c, vv - 1)
                    elif not first:
                        scan_step(c - 1, UPC - 1)
                    if not first and vv == LAG:
                        post(c - 1, 0)
                    if not first and vv == LAG + 2:
                        post(c - 1, 3)

            chunk(0, True)
            dve.wait_ge(s_residual, NC)
            old = ch.base + ch.n
            PER = 1 + 2 * TPC + 3
            with dve.Fori(1, NC) as c:
                ch.base, ch.n = old + (c - 1) * PER, 0
                chunk(c, False)
                assert ch.n == PER, ch.n
            ch.base, ch.n = old + (NC - 1) * PER, 0
            scan_step(NC - 1, UPC - 1)

            R = [rb[:, k, :].rearrange("p (j e) -> p j e", e=E) for k in range(10)]

            def w16(k):
                return r16[:, k, :]

            def over(a):
                return a.unsqueeze(2).to_broadcast([P, a.shape[1], E])

            desc = cc("desc").rearrange("p (j e) -> p j e", e=E)

            def first_largest(js, src, top, tmp, tmp16, mask):
                ch.link(v.tensor_reduce(top[:, js], src[:, js], AX.X, ALU.max))
                ch.link(v.tensor_tensor(tmp[:, js], src[:, js], over(top[:, js]), ALU.is_equal))
                ch.link(v.tensor_tensor(tmp[:, js], tmp[:, js], desc[:, js], ALU.mult))
                ch.link(v.tensor_reduce(tmp16[:, js], tmp[:, js], AX.X, ALU.max))
                ch.link(v.tensor_tensor(mask[:, js], tmp[:, js], over(tmp16[:, js]), ALU.is_equal))

            def choose(js, logits, part):
                ch.link(v.tensor_reduce(w16(0)[:, js], logits, AX.X, ALU.max))
                v.tensor_tensor(R[0][:, js], logits, over(w16(0)[:, js]), ALU.subtract).then_inc(s_router, 1)
                dve.wait_ge(s_exp, part + 1)
                ch.link(v.tensor_reduce(w16(1)[:, js], R[1][:, js], AX.X, ALU.add))
                ch.link(v.reciprocal(w16(2)[:, js], w16(1)[:, js]))
                ch.link(v.tensor_tensor(R[2][:, js], R[1][:, js], over(w16(2)[:, js]), ALU.mult))
                first_largest(js, R[2], w16(3), R[3], w16(4), R[4])
                ch.link(v.scalar_tensor_tensor(R[5][:, js], R[4][:, js], -2.0, R[2][:, js], ALU.mult, ALU.add))
                first_largest(js, R[5], w16(5), R[3], w16(4), R[6])
                v.tensor_tensor(kp_b[:, :, js], R[4][:, js].rearrange("p j e -> p e j"),
                                R[6][:, js].rearrange("p j e -> p e j"), ALU.add).then_inc(s_chosen, 1)

            def shares(js):
                ch.mark(v.tensor_tensor(R[9][:, js], R[4][:, js], R[6][:, js], ALU.add))
                ch.link(v.tensor_tensor(w16(6)[:, js], w16(3)[:, js], w16(5)[:, js], ALU.add))
                ch.link(v.tensor_scalar(w16(6)[:, js], w16(6)[:, js], EPS_W, None, ALU.max))
                ch.link(v.reciprocal(w16(7)[:, js], w16(6)[:, js]))
                ch.mark(v.tensor_tensor(w16(8)[:, js], w16(3)[:, js], w16(7)[:, js], ALU.mult))
                ch.link(v.tensor_tensor(w16(9)[:, js], w16(5)[:, js], w16(7)[:, js], ALU.mult))
                ch.mark(v.tensor_tensor(R[7][:, js], R[4][:, js], over(w16(8)[:, js]), ALU.mult))
                ch.link(v.tensor_tensor(R[8][:, js], R[6][:, js], over(w16(9)[:, js]), ALU.mult))
                ch.link(v.tensor_tensor(R[8][:, js], R[7][:, js], R[8][:, js], ALU.add))
                v.scalar_tensor_tensor(wm[:, js], R[9][:, js], -1.0, R[8][:, js], ALU.add, ALU.add).then_inc(s_router, 1)

            before, last = slice(0, NT - TPC), slice(NT - TPC, NT)
            dve.wait_ge(s_late_consts, 16)
            dve.wait_ge(s_logits, NC - 1)
            choose(before, lg[:, before], 0)
            ch.after()

            for h in range(2):
                js = slice(2 * h, 2 * h + 2)
                dve.wait_ge(s_y_turned, NC + h)
                ch.mark(v.tensor_tensor(xt[:, NT - TPC + 2 * h:NT - TPC + 2 * h + 2, :],
                                        xt[:, NT - TPC + 2 * h:NT - TPC + 2 * h + 2, :],
                                        bank(TB + 2 * h, 2 * P).rearrange("p (j d) -> p j d", d=D), ALU.add))
            done = [ch.n - 1, ch.n]
            for j in range(TPC):
                if j % 2 == 0:
                    ch.until(done[j // 2])
                ch.mark(v.bn_stats(stat2[:, j, :], xt[:, NT - TPC + j, :]))
            post(NC - 1, 1)
            post(NC - 1, 2)
            shares(before)
            post(NC - 1, 3)
            dve.wait_ge(s_rows_stored, 16 * (NC - 1))
            dve.wait_ge(s_xn2_turned, NC - 1)
            for j in range(1, TPC):
                v.tensor_scalar(xn[:, j, :], xt[:, NT - TPC + j, :], mv2[:, j, 0:1], sm2[:, 4, j:j + 1], ALU.subtract,
                                ALU.mult).then_inc(s_last_xn2, 1)
            dve.wait_ge(s_logits_product, NC - 1)
            for j in range(1, TPC):
                dve.wait_ge(s_last_xn2_turned, j + (j > 1))
                v.tensor_copy(x2T[:, j * P:(j + 1) * P], bank(j, P)).then_inc(s_last_xn2T, 1)
            dve.wait_ge(s_logits_product, NC)
            choose(last, psum[:, RB, 0:TPC * E].rearrange("p (j e) -> p j e", e=E), 1)
            shares(last)

            def ej(a):
                return a.rearrange("p (e j) -> p e j", j=NT)

            dve.wait_ge(s_chosen_counted, 1)
            ch.link(v.tensor_reduce(lim[:, 0, :], ej(bank(6, P)), AX.X, ALU.add))
            v.tensor_reduce(fullest[:], lim[:, 0, :], AX.X, ALU.max).then_inc(s_fullest, 1)
            dve.wait_ge(s_router, 4)
            wv = wm[:].rearrange("p j e -> p e j")

            def running(chain, tot, within, a, b, o):
                chain.link(v.tensor_tensor_scan(rb[:, a, :], cc("smask"), tot, 0.0, ALU.mult, ALU.add))
                chain.link(v.tensor_tensor(rb[:, b, :], rb[:, a, :], tot, ALU.subtract))
                chain.link(v.tensor_tensor(rb[:, o, :], rb[:, b, :], within, ALU.add))

            dve.wait_ge(s_fullest, 1)
            with dve.If(dve.value_load(fullest[0:1, 0:1]) > CAP):
                cs = Chain(dve, s_search)
                for k in (0, 2):
                    js = slice(4 * k, 4 * k + 4)
                    v.tensor_copy(wmx[:, js], wm[:, js].unsqueeze(3).to_broadcast([P, 4, E, 16])).then_inc(s_copied_dve, 1)
                dve.wait_ge(s_weights_turned, 1)
                junk = bbc[:]
                allw = psum[:, 0:4, :].rearrange("p b n -> p (b n)")
                dve.wait_ge(s_bits, 16)
                for r in range(NROUND):
                    edge = jb[:, 0:1] if r == 0 else thr[:, r:r + 1]
                    cs.link(v.tensor_scalar(junk, allw, edge.bitcast(F32), None, ALU.is_ge, ALU.add,
                                            accum_out=cnt[:, r:r + 1]))
                    v.tensor_scalar(ind[:, r:r + 1], cnt[:, r:r + 1], float(CAP), None, ALU.is_ge).then_inc(s_indicator, 1)
                    dve.wait_ge(s_digit, r + 1)
                    cs.link(v.tensor_scalar(digs[:, r:r + 1], psum[:, 4, r:r + 1], float(1 << SHIFT[r]), None, ALU.mult))
                    cs.link(v.tensor_tensor(base[:, r + 1:r + 2], digs[:, r:r + 1], base[:, r:r + 1], ALU.bitwise_or))
                    if r + 1 < NROUND:
                        cs.link(v.tensor_tensor(thr[:, r + 1:r + 2], base[:, r + 1:r + 2], jb[:, r + 1:r + 2], ALU.bitwise_or))
                v.tensor_scalar(taud[:], cc("selcol"), base[:, NROUND:].bitcast(F32), None, ALU.mult).then_inc(s_tau_rows, 1)
                dve.wait_ge(s_tau, 1)
                tau = psum[:, 4, 32:32 + E].unsqueeze(2).to_broadcast([P, E, NT])
                v.tensor_tensor(gt_b[:], wv, tau, ALU.is_gt).then_inc(s_above, 1)
                v.tensor_tensor(eq_b[:], wv, tau, ALU.is_equal).then_inc(s_above, 1)
                dve.wait_ge(s_counted, 1)
                cs.link(v.tensor_reduce(lim[:, 0, :], ej(bank(5, P)), AX.X, ALU.add))
                cs.link(v.tensor_scalar(lim[:, 1, :], lim[:, 0, :], -1.0, float(CAP), ALU.mult, ALU.add))
                running(cs, bank(6, P), bank(7, P), 0, 1, 2)
                cs.link(v.tensor_tensor(ej(rb[:, 3, :]), ej(rb[:, 2, :]), lim[:, 1, :].unsqueeze(2).to_broadcast([P, E, NT]),
                                        ALU.is_le))
                cs.link(v.tensor_tensor(ej(rb[:, 4, :]), ej(rb[:, 3, :]), eq_b[:], ALU.mult))
                v.tensor_tensor(kp_b[:], ej(rb[:, 4, :]), gt_b[:], ALU.add).then_inc(s_keep, 1)
                dve.wait_ge(s_keep, 1)
                dve.wait_ge(s_keep_counted, 1)

            slot = ch.mark(v.tensor_tensor_scan(rb[:, 0, :], cc("smask"), bank(6, P), 0.0, ALU.mult, ALU.add))
            share = ch.mark(v.tensor_tensor(ej(rb[:, 5, :]), kp_b[:], wv, ALU.mult))
            ch.until(slot)
            slot = ch.mark(v.tensor_tensor(rb[:, 1, :], rb[:, 0, :], bank(6, P), ALU.subtract))
            ch.until(share)
            share = ch.mark(v.tensor_reduce(w16(0), ej(rb[:, 5, :]).rearrange("p e j -> p j e"), AX.X, ALU.add))
            ch.until(slot)
            slot = ch.mark(v.tensor_tensor(rb[:, 2, :], rb[:, 1, :], bank(7, P), ALU.add))
            ch.until(share)
            share = ch.mark(v.tensor_scalar(w16(0), w16(0), EPS_W, None, ALU.max))
            ch.until(slot)
            slot = ch.mark(v.tensor_tensor(ej(rb[:, 8, :]), ej(rb[:, 2, :]), kp_b[:], ALU.mult))
            ch.until(share)
            share = ch.mark(v.reciprocal(w16(1), w16(0)))
            ch.until(slot)
            slot = ch.mark(v.tensor_scalar(qq[:], rb[:, 8, :], float(P), None, ALU.is_gt))
            ch.until(share)
            share = ch.mark(v.tensor_tensor(ej(rb[:, 6, :]), ej(rb[:, 5, :]), r16[:, 1:2, :].to_broadcast([P, E, NT]),
                                            ALU.mult))
            ch.until(slot)
            slot = ch.mark(v.scalar_tensor_tensor(qq[:], rb[:, 8, :], float(2 * P), qq[:], ALU.is_gt, ALU.add))
            ch.until(share)
            share = ch.mark(v.tensor_copy(vals[:, 2, :], rb[:, 6, :]))
            ch.until(slot)
            slot = ch.mark(v.scalar_tensor_tensor(qq[:], rb[:, 8, :], float(3 * P), qq[:], ALU.is_gt, ALU.add))
            ch.until(share)
            share = ch.mark(v.tensor_tensor(rb[:, 7, :], rb[:, 6, :], vals[:, 2, :], ALU.subtract))
            ch.until(slot)
            slot = ch.mark(v.scalar_tensor_tensor(qq[:], rb[:, 8, :], float(4 * P), qq[:], ALU.is_gt, ALU.add))
            ch.until(share)
            share = ch.mark(v.tensor_copy(vals[:, 3, :], rb[:, 7, :]))
            ch.until(slot)
            slot = ch.mark(v.scalar_tensor_tensor(r1[:], qq[:], -float(P), rb[:, 8, :], ALU.mult, ALU.add))
            ch.until(share)
            ch.mark(v.tensor_tensor(vals[:, 4, :], rb[:, 7, :], vals[:, 3, :], ALU.subtract))
            assert NQ == 5

            def one_hot(e, j):
                return v.tensor_scalar(oh[:, j, :], iota_b[:], r1[:, bass.ds(e * NT + j, 1)], None, ALU.is_equal)

            def columns(e):
                ch.link(v.tensor_tensor(q1[:], qq[:, bass.ts(e, NT)].unsqueeze(2).to_broadcast([P, NT, NQ]),
                                        cc("q5").rearrange("p (o q) -> p o q", o=1).to_broadcast([P, NT, NQ]), ALU.is_equal))
                v.tensor_tensor(rq[:], q1[:].unsqueeze(1).to_broadcast([P, 5, NT, NQ]),
                                vals[:, :, bass.ts(e, NT)].unsqueeze(3).to_broadcast([P, 5, NT, NQ]),
                                ALU.mult).then_inc(s_columns, 1)

            def gather_rows(e, b):
                dve.wait_ge(s_table, e + 1)
                if above_zero(2 * (e - 1)):
                    dve.wait_ge(s_rows_turned, 2 * (e - 1))
                ch.link(v.tensor_copy(tab[:, b, :], psum[:, 7, 0:5 * NQ]))
                ch.link(v.tensor_tensor(token[:, b, :], tab[:, b, 0:NQ], tab[:, b, NQ:2 * NQ], ALU.add))
                v.tensor_scalar(gid[:, b, :], token[:, b, :], -1.0, 0.0, ALU.add, ALU.max).then_inc(s_gather_ids, 1)

            def scatter_rows(e, b):
                if above_zero(NQ * (e - 1)):
                    dve.wait_ge(s_weighed, NQ * (e - 1))
                if above_zero(16 * NQ * (e - 1)):
                    dve.wait_ge(s_scattered, 16 * NQ * (e - 1))
                ch.mark(v.scalar_tensor_tensor(tk[:, 0, :], tab[:, b, 0:NQ], 0.0, cc("spare1"), ALU.is_equal, ALU.mult))
                ch.link(v.tensor_tensor(tk[:, 1, :], tab[:, b, 2 * NQ:3 * NQ], tab[:, b, 3 * NQ:4 * NQ], ALU.add))
                v.scalar_tensor_tensor(sid[:, b, :], tk[:, 0, :], -1.0, token[:, b, :], ALU.add, ALU.add).then_inc(s_scatter_ids, 1)
                v.tensor_tensor(kw[:, b, :], tab[:, b, 4 * NQ:5 * NQ], tk[:, 1, :], ALU.add).then_inc(s_scatter_ids, 1)

            def tokens_low(e, b):
                for k, (w, bk, o) in enumerate(((QA * P, 4, 0), (CAP - QA * P, 6, QA * P))):
                    dve.wait_ge(s_xe, 2 * e + k + 1)
                    v.tensor_tensor(xe_p[:, b, 1, o:o + w], bank(bk, w), xe_p[:, b, 0, o:o + w].bitcast(F32),
                                    ALU.subtract).then_inc(s_xe_low, 1)

            def weights_low(e, b, k):
                dve.wait_ge(s_in_high, 2 * e + k + 1)
                v.tensor_tensor(win_p[:, b, 1, k], win_s[:, b, k], win_p[:, b, 0, k].bitcast(F32),
                                ALU.subtract).then_inc(s_in_low, 1)

            def expert(e, b, more, split=True, last=False):
                scatter_rows(e, b)
                if more:
                    dve.wait_ge(s_table, e + 2)
                for un in range(2 * FC):
                    half, f = un // FC, un % FC
                    dve.wait_ge(s_silu, e * (2 * FC) + (un + 1))
                    if un == 0:
                        if above_zero(e - 1):
                            dve.wait_ge(s_down, e - 1)
                    v.tensor_tensor(hT[:, b, f, half * HALF:(half + 1) * HALF], psum[:, un % 2, 0:HALF],
                                    sg[:, un % 2, :], ALU.mult).then_inc(s_hidden, 1)
                    if more:
                        for j in range(un * NT // (2 * FC), (un + 1) * NT // (2 * FC)):
                            one_hot(e + 2, j)
                if more:
                    columns(e + 2)
                if not last:
                    tokens_low(e + 1, 1 - b)
                if split:
                    for k in range(2):
                        weights_low(e + 1, 1 - b, k)
                if more:
                    gather_rows(e + 2, b)

            ch.after()
            dve.wait_ge(s_pool_consts, 3 + 6)
            for e in range(2):
                if above_zero(e):
                    dve.wait_ge(s_table, e)
                if e == 0:
                    columns(0)
                for j in range(NT):
                    ins = one_hot(e, j)
                    if e == 0:
                        ins.then_inc(s_first_one_hot, 1)
                if e:
                    columns(e)
                gather_rows(e, e)
            tokens_low(0, 0)
            expert(0, 0, True, split=False)
            expert(1, 1, True)
            old = ch.base + ch.n
            PER = 2 * (2 + 1 + 2)
            with dve.Fori(1, E // 2 - 1) as i:
                ch.base, ch.n = old + (i - 1) * PER, 0
                for b in range(2):
                    expert(2 * i + b, b, True)
                assert ch.n == PER, ch.n
            ch.base, ch.n = old + (E // 2 - 2) * PER, 0
            expert(E - 2, 0, False)
            expert(E - 1, 1, False, split=False, last=True)

        @blk.scalar
        def _(act):
            a = nc.scalar
            ch = Chain(act, s_act)
            nc.scalar.dma_start(cst[:, 0:CW_EARLY], consts[:, 0:CW_EARLY]).then_inc(s_consts, 16)
            nc.scalar.dma_start(wx_s[:], wx).then_inc(s_wx, 16)
            nc.scalar.dma_start(wdt_s[:], wdt).then_inc(s_wdt, 16)
            nc.scalar.dma_start(small[:], vectors).then_inc(s_weights, 16)
            act.wait_ge(s_wx, 16)
            for k in range(2):
                a.activation(wbc[:, k], wx_s[:, RANK + NS * k:RANK + NS * (k + 1)].unsqueeze(2).to_broadcast([P, NS, GD]),
                             ACT.Copy).then_inc(s_spreaders, 1)
            act.wait_ge(s_consts, 16)
            a.activation(sel_r[:], cc("dup").rearrange("p (g o d) -> p g o d", o=1, d=GD).to_broadcast(
                [P, P // GD // 2, NS, GD]), ACT.Copy).then_inc(s_spreaders, 1)
            act.wait_ge(s_weights, 16)
            a.activation(nega[:], alog_s, ACT.Exp).then_inc(s_neg_a, 1)

            def transposed_rows(c):
                act.wait_ge(s_xn_turned, c + 1)
                a.activation(xnT[:, c * CH:(c + 1) * CH], bank(TURNED[c]), ACT.Copy).then_inc(s_xnT, 1)

            def rank_rows(c):
                act.wait_ge(s_xp_product, c + 1)
                a.activation(pre_b[c][0:RANK], psum[0:RANK, XPB[c], :], ACT.Copy).then_inc(s_xp, 1)

            def exp_z(c):
                if c:
                    act.wait_ge(s_residual, c + 1)
                act.wait_ge(s_z, c + 1)
                a.activation(pre_a[c], bank(ZB[c]), ACT.Abs, bias=bdt_s).then_inc(s_abs_z, 1)
                act.wait_ge(s_abs_z, c + 1)
                ch.mark(a.activation(pre_a[c], pre_a[c], ACT.Exp, scale=-1.0))

            def log_z(c):
                a.activation(pre_a[c], pre_a[c], ACT.Ln, bias=1.0).then_inc(s_log, 1)

            def c_rows(c):
                act.wait_ge(s_bc_product, 2 * c + 2)
                a.activation(cbc[:, c * CH:(c + 1) * CH], bank(CB[c]), ACT.Copy).then_inc(s_c, 1)

            def high(c):
                if c >= SPLIT:
                    act.wait_ge(s_stack, STACKED * (c - SPLIT + 1))
                    act.wait_ge(s_dx_spread, UG * DIRECT)
                for k, src in enumerate((pre_b, pre_c)):
                    act.wait_ge(s_delta, 2 * c + 1 + k)
                    a.activation(parts[:, c % SPLIT, 0, k], src[c], ACT.Copy).then_inc(s_high, 1)

            transposed_rows(0)
            rank_rows(0)
            exp_z(0)
            ch.after()
            log_z(0)
            transposed_rows(1)
            c_rows(0)
            high(0)
            act.wait_ge(s_neg_a, 2)
            act.wait_ge(s_pool_consts, 2)

            def decay(c, vv):
                for k in range(UG):
                    n, m = c * UPC + vv, c * NG + (UG * vv + k)
                    g = UG * vv + k
                    act.wait_ge(s_delta_spread, m + 1)
                    if k == 0 and above_zero(n - (RING - 1)):
                        act.wait_ge(s_state, n - (RING - 1))
                    src = bank(SPREAD_D + k).rearrange("p (b s) -> p b s", s=SEQ)
                    dst = da[:, vv % RING, k, :].rearrange("p (b s) -> p b s", s=SEQ)
                    a.activation(dst[:, :, 1:], src[:, :, 1:], ACT.Exp, scale=nega[:, g:g + 1]).then_inc(s_decay, 1)

            def post(c, step):
                if step == 0:
                    act.wait_ge(s_summed, c * UPC + UPC)
                    if above_zero(c):
                        act.wait_ge(s_y_turned, c)
                    a.activation(y2[:], bank(YB), ACT.Copy).then_inc(s_y, 1)
                elif step == 1:
                    act.wait_ge(s_x2, c + 1)
                    ch.link(a.activation(sm2[:, 1, :], sm2[:, 0, :], ACT.Ln))
                    a.activation(sm2[:, 2, :], sm2[:, 1, :], ACT.Exp, scale=-0.5).then_inc(s_rough2, 1)
                elif step == 2:
                    act.wait_ge(s_rstd2, c + 1)
                    if above_zero(16 * c):
                        act.wait_ge(s_rows_stored, 16 * c)
                    if above_zero(c):
                        act.wait_ge(s_xn2_turned, c)
                    for j in range(TPC):
                        a.activation(xn[:, j, :], xt[:, TPC * c + j, :], ACT.Identity, bias=sm2[:, 5, j:j + 1],
                                     scale=sm2[:, 4, j:j + 1]).then_inc(s_xn2, 1)
                elif step == 3:
                    act.wait_ge(s_xn2_turned, c + 1)
                    a.activation(x2T[:], bank(TB), ACT.Copy).then_inc(s_xn2T, 1)
                    act.wait_ge(s_logits_product, c + 1)
                    a.activation(lg[:, bass.ts(c, TPC), :], psum[:, RB, 0:TPC * E].rearrange("p (j e) -> p j e", e=E),
                                 ACT.Copy).then_inc(s_logits, 1)

            def chunk(c, first):
                for vv in range(UPC):
                    if not first and vv == LAG:
                        post(c - 1, 0)
                    decay(c, vv)
                    if first:
                        if 1 <= vv < NC:
                            exp_z(vv)
                        if vv + 2 < NC:
                            transposed_rows(vv + 2)
                        if vv + 1 < NC:
                            rank_rows(vv + 1)
                        if vv == NC - 1:
                            ch.after()
                            for k in range(1, NC):
                                log_z(k)
                        if NC <= vv < 2 * NC - 1:
                            c_rows(vv - NC + 1)
                            high(vv - NC + 1)
                    if not first and vv > LAG + 1:
                        post(c - 1, vv - LAG - 1)

            chunk(0, True)
            old = ch.base + ch.n
            with act.Fori(1, NC) as c:
                ch.base, ch.n = old + (c - 1), 0
                chunk(c, False)
            ch.base, ch.n = old + NC - 1, 0

            def exponentials(part, js):
                act.wait_ge(s_router, 2 * part + 1)
                a.activation(rb[:, 1, js.start * E:js.stop * E], rb[:, 0, js.start * E:js.stop * E],
                             ACT.Exp).then_inc(s_exp, 1)

            exponentials(0, slice(0, NT - TPC))
            act.wait_ge(s_summed, NC * UPC)
            act.wait_ge(s_y_turned, NC - 1)
            for h in range(2):
                hs = slice(2 * h * P, 2 * (h + 1) * P)
                a.activation(y2[:, hs], psum[:, YB, hs], ACT.Copy).then_inc(s_y, 1)
            post(NC - 1, 1)
            act.wait_ge(s_rstd2, NC)
            act.wait_ge(s_rows_stored, 16 * (NC - 1))
            act.wait_ge(s_xn2_turned, NC - 1)
            a.activation(xn[:, 0, :], xt[:, NT - TPC, :], ACT.Identity, bias=sm2[:, 5, 0:1],
                         scale=sm2[:, 4, 0:1]).then_inc(s_xn2, 1)
            act.wait_ge(s_last_xn2_turned, 2)
            a.activation(x2T[:, 0:P], bank(0, P), ACT.Copy).then_inc(s_xn2T, 1)
            exponentials(1, slice(NT - TPC, NT))
            act.wait_ge(s_dx_spread, NC * NG)
            for e in range(2):
                act.wait_ge(s_in_weights[e], 32)
                for k in range(2):
                    a.activation(win_p[:, e, 0, k], win_s[:, e, k], ACT.Copy).then_inc(s_in_high, 1)

            act.wait_ge(s_fullest, 1)
            with act.If(act.value_load(fullest[0:1, 0:1]) > CAP):
                act.wait_ge(s_router, 4)
                for k in (1, 3):
                    js = slice(4 * k, 4 * k + 4)
                    a.activation(wmx[:, js], wm[:, js].unsqueeze(3).to_broadcast([P, 4, E, 16]),
                                 ACT.Copy).then_inc(s_copied_act, 1)

            def weights_high(e, b, k):
                a.activation(win_p[:, b, 0, k], win_s[:, b, k], ACT.Copy).then_inc(s_in_high, 1)

            def spread_tokens(e, b):
                if above_zero((e - 1) * 2 * FC):
                    act.wait_ge(s_up, (e - 1) * 2 * FC)
                act.wait_ge(s_rows_turned, 2 * e + 1)
                a.activation(xe_p[:, b, 0, 0:QA * P], bank(4, QA * P), ACT.Copy).then_inc(s_xe, 1)
                act.wait_ge(s_rows_turned, 2 * e + 2)
                a.activation(xe_p[:, b, 0, QA * P:CAP], bank(6, CAP - QA * P), ACT.Copy).then_inc(s_xe, 1)

            def gates(e, b, i, split, first=False, last=False):
                for un in range(2 * FC):
                    g = e * (2 * FC) + un
                    act.wait_ge(s_up, g + 1)
                    if above_zero(g - 1):
                        act.wait_ge(s_hidden, g - 1)
                    a.activation(sg[:, un % 2, :], psum[:, 2 + un % 2, 0:HALF], ACT.Silu).then_inc(s_silu, 1)
                    if not first and un < NQ:
                        weigh(e - 1, 1 - b, un)
                    if last and un == 2 * FC - 2:
                        weigh_last(e, b, range(2))
                    if split and un >= 2 * FC - 2:
                        if un == 2 * FC - 2:
                            act.wait_ge(s_in_weights[1 - b], 32 * (i + b) + 32)
                        weights_high(e + 1, 1 - b, un - 2 * FC + 2)

            def weigh(e, b, q):
                if q == 0:
                    act.wait_ge(s_scatter_ids, 2 * e + 2)
                    act.wait_ge(s_down, e + 1)
                    if above_zero(16 * NQ * (e - 1)):
                        act.wait_ge(s_scattered, 16 * NQ * (e - 1))
                a.activation(ye[:, b, q, :], psum[:, 5 + q // 4, (q % 4) * P:(q % 4 + 1) * P], ACT.Copy,
                             scale=kw[:, b, q:q + 1]).then_inc(s_weighed, 1)

            def weigh_last(e, b, tiles):
                if 0 in tiles:
                    act.wait_ge(s_scatter_ids, 2 * e + 2)
                    act.wait_ge(s_scattered, 16 * NQ * (e - 1))
                for q in tiles:
                    act.wait_ge(s_down_tile, q + 1)
                    a.activation(ye[:, b, q, :], bank(LAST_BANK[q], P), ACT.Copy,
                                 scale=kw[:, b, q:q + 1]).then_inc(s_weighed, 1)

            def expert(i, b, split=True, first=False):
                e = 2 * i + b
                gates(e, b, i, split, first)
                spread_tokens(e + 1, 1 - b)

            spread_tokens(0, 0)
            expert(0, 0, split=False, first=True)
            expert(0, 1)
            with act.Fori(1, E // 2 - 1) as i:
                for b in range(2):
                    expert(i, b)
            expert(E // 2 - 1, 0)
            gates(E - 1, 1, E // 2 - 1, False, last=True)
            weigh_last(E - 1, 1, range(2, NQ))

        @blk.gpsimd
        def _(pool):
            g = nc.gpsimd
            ch = Chain(pool, s_pool)
            g.memset(zero[:], 0.0).then_inc(s_pool_consts, 1)
            g.memset(da.rearrange("p r u (b s) -> p (r u b) s", s=SEQ)[:, :, 0:1], 0.0).then_inc(s_pool_consts, 1)
            g.memset(base[:, 0:1], 0).then_inc(s_pool_consts, 1)
            pool.wait_ge(s_neg_a, 1)
            g.tensor_scalar(nega[:], nega[:], -1.0, 0.0, ALU.mult, ALU.add).then_inc(s_neg_a, 1)
            pool.wait_ge(s_skip, 16)
            skip = drow[:].rearrange("p (o d) -> p o d", o=1).to_broadcast([P, TPC, D])
            for c in range(NC):
                js = slice(TPC * c, TPC * (c + 1))
                pool.wait_ge(s_xn, TPC * (c + 1))
                term = (y2, x2T)[c % 2][:].rearrange("p (j d) -> p j d", d=D)
                ch.link(g.tensor_tensor(term, xn[:, js, :], skip, ALU.mult))
                g.tensor_tensor(xt[:, js, :], xt[:, js, :], term, ALU.add).then_inc(s_residual, 1)

            def low(c, k):
                full = (pre_b, pre_c)[k]
                pool.wait_ge(s_high, 2 * c + k + 1)
                if c >= SPLIT:
                    pool.wait_ge(s_stack, STACKED * (c - SPLIT + 1))
                    pool.wait_ge(s_dx_spread, UG * DIRECT)
                g.tensor_tensor(parts[:, c % SPLIT, 1, k], full[c], parts[:, c % SPLIT, 0, k].bitcast(F32),
                                ALU.subtract).then_inc(s_low, 1)

            def product(c, vv):
                n, s = c * UPC + vv, vv % RING
                pool.wait_ge(s_state, n + 1)
                if above_zero(n - (RING - 1)):
                    pool.wait_ge(s_summed, n - (RING - 1))
                plain(pool)
                cb = cbc[:, bass.ts(c, CH)].rearrange("p (o n) -> p o n", o=1).to_broadcast([P, UG, CH])
                g.tensor_tensor(hc[:, s], hh[:, s], cb, ALU.mult).then_inc(s_product, 1)

            pool.wait_ge(s_low, 2)
            for vv in range(UPC):
                if vv == NC:
                    low(1, 0)
                    low(1, 1)
                elif NC < vv < UPC:
                    low(2 + (vv - NC - 1) // 2, (vv - NC - 1) % 2)
                if vv == 0:
                    pool.wait_ge(s_c, 1)
                product(0, vv)
            low(NC - 1, 1)
            pool.wait_ge(s_c, NC)
            with pool.Fori(1, NC - 1) as c:
                for vv in range(UPC):
                    product(c, vv)
            for vv in range(UPC - 1):
                product(NC - 1, vv)
            n, s = NC * UPC - 1, (UPC - 1) % RING
            pool.wait_ge(s_state, n + 1)
            pool.wait_ge(s_summed, n - (RING - 1))
            for k in range(UG):
                g.tensor_tensor(hc[:, s, k], hh[:, s, k], cbc[:, (NC - 1) * CH:], ALU.mult).then_inc(s_product, 1)

            pool.wait_ge(s_late_consts, 16)
            for dst, src in ((ones_b, "ones"), (tri_b, "tri"), (blk_b, "blk"), (iota_b, "iota")):
                g.tensor_copy(dst[:], cc(src)).then_inc(s_pool_consts, 1)
            g.tensor_tensor(vals[:, 0, :], cc("ones")[:, 0:E * NT], cc("pval").to_broadcast([P, E * NT]),
                            ALU.mult).then_inc(s_pool_consts, 1)
            g.tensor_copy(vals[:, 1, :], cc("jval")).then_inc(s_pool_consts, 1)

            for e in range(2):
                for k in range(2):
                    pool.wait_ge(s_in_high, 2 * e + k + 1)
                    g.tensor_tensor(win_p[:, e, 1, k], win_s[:, e, k], win_p[:, e, 0, k].bitcast(F32),
                                    ALU.subtract).then_inc(s_in_low, 1)

            def gather_ready(e, b):
                pool.wait_ge(s_gather_ids, e + 1)
                if above_zero(2 * (e - 1)):
                    pool.wait_ge(s_rows_turned, 2 * (e - 1))
                plain(pool)

            def gather(b, q):
                g.indirect_dma_start(out=gx[:, b, q, :], out_offset=None, in_=rows,
                                     in_offset=bass.IndirectOffsetOnAxis(ap=gid[:, b, q:q + 1], axis=0)
                                     ).then_inc(s_gathered[b][q], 16)

            def expert(e, b, more=True):
                if more:
                    gather_ready(e + 2, b)
                    for q in range(NQ):
                        gather(b, q)
                pool.wait_ge(s_scatter_ids, 2 * e + 2)
                for q in range(NQ):
                    pool.wait_ge(s_weighed, NQ * e + q + 1)
                    if q == 0 and above_zero(16 * NQ * e):
                        pool.wait_ge(s_scattered, 16 * NQ * e)
                    plain(pool)
                    g.indirect_dma_start(out=out, out_offset=bass.IndirectOffsetOnAxis(ap=sid[:, b, q:q + 1], axis=0),
                                         in_=ye[:, b, q, :], in_offset=None, compute_op=ALU.add
                                         ).then_inc(s_scattered, 16)

            pool.wait_ge(s_rows_stored, 16 * NC)
            pool.wait_ge(s_out_stored, 16 * (NC + 1))
            for b in range(2):
                gather_ready(b, b)
                for q in range(NQ):
                    gather(b, q)
            for e in range(2):
                expert(e, e)
            with pool.Fori(1, E // 2 - 1) as i:
                for b in range(2):
                    expert(2 * i + b, b)
            expert(E - 2, 0, False)
            expert(E - 1, 1, False)

        @blk.tensor
        def _(pe):
            t = nc.tensor
            mm = t.matmul
            pe.wait_ge(s_consts, 16)

            def turn_rows(c):
                if c >= 2:
                    pe.wait_ge(s_xnT, c)
                for j in range(TPC):
                    pe.wait_ge(s_xn, TPC * c + j + 1)
                    ins = t.transpose(psum[:, TURNED[c], j * P:(j + 1) * P], xn[:, TPC * c + j, :], ident)
                ins.then_inc(s_xn_turned, 1)

            def inner(c):
                pe.wait_ge(s_xnT, c + 1)
                if c:
                    pe.wait_ge(s_c, 1)
                    pe.wait_ge(s_xp, c)
                mm(psum[0:RANK, XPB[c], :], wx_s[:, 0:RANK], xnT[:, c * CH:(c + 1) * CH], start=True,
                   stop=True).then_inc(s_xp_product, 1)

            def outer(c):
                pe.wait_ge(s_xp, c + 1)
                if c == 1:
                    pe.wait_ge(s_b, 1)
                elif c:
                    pe.wait_ge(s_positive, c - 1)
                mm(bank(ZB[c]), wdt_s[:], pre_b[c][0:RANK], start=True, stop=True).then_inc(s_z, 1)

            def bc_rows(c):
                if c == 1:
                    pe.wait_ge(s_positive, 3)
                    pe.wait_ge(s_xp, NC)
                elif c:
                    pe.wait_ge(s_b, c)
                    pe.wait_ge(s_c, c)
                for k in range(2):
                    mm(bank((BB, CB)[k][c]), wbc[:, k].rearrange("p s d -> p (s d)"), xnT[:, c * CH:(c + 1) * CH],
                       start=True, stop=True).then_inc(s_bc_product, 1)

            def keep_clock(n):
                z = zero[:].bitcast(BF16)
                for _ in range(n):
                    mm(bank(3, 2 * D), z[:, 0:P], z, start=True, stop=True)

            pe.wait_ge(s_pool_consts, 1)
            keep_clock(WARM["rows"])
            turn_rows(0)
            pe.wait_ge(s_wx, 16)
            pe.wait_ge(s_wdt, 16)
            keep_clock(WARM["turned"])
            inner(0)
            keep_clock(WARM["rank"])
            outer(0)
            pe.wait_ge(s_spreaders, 3)
            pe.wait_ge(s_xp, 1)
            bc_rows(0)
            turn_rows(1)
            keep_clock(WARM["parts"])
            pe.wait_ge(s_late_consts, 16)

            def spread(c, vv, direct=False):
                for k in range(UG):
                    grp, m = UG * vv + k, c * NG + (UG * vv + k)
                    half = grp // 8
                    sel = sel_r[:, grp % 8].rearrange("p s d -> p (s d)")
                    for kind, (to, used, ready) in enumerate(((SPREAD_D, s_decay, s_delta_spread),
                                                              (SPREAD_X, s_input, s_dx_spread))):
                        if above_zero(m - 1):
                            pe.wait_ge(used, m - 1)
                        if direct:
                            mm(bank(to + k), sel[0:P // 2], parts[0:P // 2, 0, 0, kind], start=True, stop=False)
                            ins = mm(bank(to + k), sel[0:P // 2], parts[0:P // 2, 0, 1, kind], start=False, stop=True)
                        else:
                            ins = mm(bank(to + k), sel, stack[:, half, kind, bass.ts(c, CH)], start=True, stop=True)
                        ins.then_inc(ready, 1)

            def reduce(c, vv, by_group=False):
                n, s = c * UPC + vv, vv % RING
                pe.wait_ge(s_product, n + 1)
                if vv == 0:
                    if above_zero(c):
                        pe.wait_ge(s_y, c)
                    else:
                        pe.wait_ge(s_xnT, NC)
                for k in range(UG):
                    if by_group and k:
                        pe.wait_ge(s_product, n + 1 + k)
                    grp = UG * vv + k
                    o = D - GD - GD * grp
                    ins = mm(bank(YB), wred[:, o:o + D], hc[:, s, k, :], start=(grp == 0), stop=(grp == NG - 1))
                ins.then_inc(s_summed, 1)

            def post(c, step):
                if step == 0:
                    pe.wait_ge(s_y, c + 1)
                    if above_zero(c):
                        pe.wait_ge(s_xn2T, c)
                    for j in range(TPC):
                        ins = t.transpose(psum[:, TB, j * P:(j + 1) * P], y2[:, j * P:(j + 1) * P], ident)
                    ins.then_inc(s_y_turned, 1)
                elif step == 1:
                    pe.wait_ge(s_xn2, TPC * c + TPC)
                    for j in range(TPC):
                        ins = t.transpose(psum[:, TB, j * P:(j + 1) * P], xn[:, j, :], ident)
                    ins.then_inc(s_xn2_turned, 1)
                elif step == 2:
                    pe.wait_ge(s_xn2T, c + 1)
                    if above_zero(c):
                        pe.wait_ge(s_logits, c)
                    for j in range(TPC):
                        ins = mm(psum[:, RB, j * E:(j + 1) * E], x2T[:, j * P:(j + 1) * P], wr_s, start=True, stop=True)
                    ins.then_inc(s_logits_product, 1)

            def chunk(c, first):
                for vv in range(UPC):
                    if first and vv == DIRECT:
                        pe.wait_ge(s_stack, STACKED)
                    spread(c, vv, first and vv < DIRECT)
                    if first:
                        if 1 <= vv < NC:
                            outer(vv)
                        if vv + 1 < NC:
                            inner(vv + 1)
                        if vv + 2 < NC:
                            turn_rows(vv + 2)
                        if NC <= vv < 2 * NC - 1:
                            bc_rows(vv - NC + 1)
                    if not first and vv == LAG:
                        post(c - 1, 0)
                    if not first and vv == UPC - 1:
                        post(c - 1, 1)
                    if vv >= LAG:
                        reduce(c, vv - LAG)
                        if not first and vv == UPC - 1:
                            post(c - 1, 2)
                    elif not first:
                        reduce(c - 1, UPC - LAG + vv)

            pe.wait_ge(s_high, 2)
            pe.wait_ge(s_low, 2)
            chunk(0, True)
            with pe.Fori(1, NC) as c:
                pe.wait_ge(s_stack, STACKED * c + STACKED)
                chunk(c, False)
            for vv in range(LAG):
                reduce(NC - 1, UPC - LAG + vv, vv == LAG - 1)
            for h in range(2):
                pe.wait_ge(s_y, NC + h)
                if h == 0:
                    pe.wait_ge(s_xn2T, NC - 1)
                for j in range(2):
                    ins = t.transpose(psum[:, TB + 2 * h, j * P:(j + 1) * P], y2[:, (2 * h + j) * P:(2 * h + j + 1) * P],
                                      ident)
                ins.then_inc(s_y_turned, 1)
            pe.wait_ge(s_decay, NC * NG)
            pe.wait_ge(s_input, NC * NG)
            keep_clock(WARM["rows2"])
            order = (1, 0, 2, 3)
            for j in order:
                if j:
                    pe.wait_ge(s_last_xn2, j)
                else:
                    pe.wait_ge(s_xn2, TPC * (NC - 1) + 1)
                t.transpose(bank(j, P), xn[:, j, :], ident).then_inc(s_last_xn2_turned, 1)
            pe.wait_ge(s_logits, NC - 1)
            for j in order:
                if j:
                    pe.wait_ge(s_last_xn2T, j)
                else:
                    pe.wait_ge(s_xn2T, NC)
                ins = mm(psum[:, RB, j * E:(j + 1) * E], x2T[:, j * P:(j + 1) * P], wr_s, start=True, stop=True)
            ins.then_inc(s_logits_product, 1)

            def flat(a):
                return a[:].rearrange("p e j -> p (e j)")

            pe.wait_ge(s_pool_consts, 3 + 6)
            pe.wait_ge(s_chosen, 2)
            mm(bank(6, P), ones_b[:], flat(kp_b), start=True, stop=True)
            mm(bank(7, P), tri_b[:], flat(kp_b), start=True, stop=True).then_inc(s_chosen_counted, 1)

            pe.wait_ge(s_fullest, 1)
            with pe.If(pe.value_load(fullest[0:1, 0:1]) > CAP):
                for j in range(NT):
                    if j % 4 == 0:
                        pe.wait_ge((s_copied_dve, s_copied_act)[j // 4 % 2], j // 8 + 1)
                    ins = t.transpose(psum[:, j // 4, (j % 4) * P:(j % 4 + 1) * P],
                                      wmx[:, j].rearrange("p e r -> p (e r)"), ident)
                ins.then_inc(s_weights_turned, 1)
                for r in range(NROUND):
                    pe.wait_ge(s_indicator, r + 1)
                    mm(psum[:, 4, r:r + 1], blk_b[:], ind[:, r:r + 1], start=True, stop=True).then_inc(s_digit, 1)
                pe.wait_ge(s_tau_rows, 1)
                mm(psum[:, 4, 32:32 + E], cc("ones"), taud[:], start=True, stop=True).then_inc(s_tau, 1)
                pe.wait_ge(s_above, 2)
                mm(bank(5, P), ones_b[:], flat(gt_b), start=True, stop=True)
                mm(bank(6, P), ones_b[:], flat(eq_b), start=True, stop=True)
                mm(bank(7, P), tri_b[:], flat(eq_b), start=True, stop=True).then_inc(s_counted, 1)
                pe.wait_ge(s_keep, 1)
                mm(bank(6, P), ones_b[:], flat(kp_b), start=True, stop=True)
                mm(bank(7, P), tri_b[:], flat(kp_b), start=True, stop=True).then_inc(s_keep_counted, 1)

            def table(e, first=False):
                pe.wait_ge(s_columns, e + 1)
                if above_zero(e):
                    pe.wait_ge(s_gather_ids, e)
                for j in range(NT):
                    if first:
                        pe.wait_ge(s_first_one_hot, j + 1)
                    ins = mm(psum[:, 7, 0:5 * NQ], oh[:, j, :], rq[:, :, j, :], start=(j == 0), stop=(j == NT - 1))
                ins.then_inc(s_table, 1)

            def turn(e, b, i, first=False):
                for q in range(NQ):
                    if first:
                        keep_clock(WARM["gathered"])
                    pe.wait_ge(s_gathered[b][q], 16 * i + 16)
                    if q == 0:
                        if above_zero(2 * e):
                            pe.wait_ge(s_xe_low, 2 * e)
                    if q == QA:
                        if above_zero(NQ * (e - 1)):
                            pe.wait_ge(s_weighed, NQ * (e - 1))
                    ins = t.transpose(psum[:, 4 + 2 * (q // QA), (q % QA) * P:(q % QA + 1) * P], gx[:, b, q, :], ident)
                    if q in (QA - 1, NQ - 1):
                        ins.then_inc(s_rows_turned, 1)

            def three(out_, w_col, b, k, cs):
                fs = slice(w_col * P, (w_col + 1) * P)
                mm(out_, win_p[:, b, 0, k, fs], xe_p[:, b, 0, cs], start=True, stop=False)
                mm(out_, win_p[:, b, 0, k, fs], xe_p[:, b, 1, cs], start=False, stop=False)
                return mm(out_, win_p[:, b, 1, k, fs], xe_p[:, b, 0, cs], start=False, stop=True)

            def up(e, b, units):
                if 0 in units:
                    pe.wait_ge(s_in_low, 2 * e + 2)
                for un in units:
                    half, f = un // FC, un % FC
                    g = e * (2 * FC) + un
                    pe.wait_ge(s_xe_low, 2 * e + 1 + half)
                    if above_zero(g - 1):
                        pe.wait_ge(s_silu, g - 1)
                    cs = slice(half * HALF, (half + 1) * HALF)
                    three(psum[:, 2 + un % 2, 0:HALF], f, b, 0, cs)
                    if above_zero(g - 1):
                        pe.wait_ge(s_hidden, g - 1)
                    three(psum[:, un % 2, 0:HALF], f, b, 1, cs).then_inc(s_up, 1)

            def down_tile(b, q, place):
                for f in range(FC):
                    ins = mm(place, hT[:, b, f, q * P:(q + 1) * P], w2_s[:, b, f, :], start=(f == 0), stop=(f == FC - 1))
                return ins

            def down(e, b, i, tiles):
                if 0 in tiles:
                    pe.wait_ge(s_out_weights[b], 16 * i + 16)
                    if above_zero(NQ * e):
                        pe.wait_ge(s_weighed, NQ * e)
                pe.wait_ge(s_hidden, e * 2 * FC + (FC if tiles[-1] < 2 else 2 * FC))
                for q in tiles:
                    ins = down_tile(b, q, psum[:, 5 + q // 4, (q % 4) * P:(q % 4 + 1) * P])
                return ins

            def expert(i, b, more=True):
                e = 2 * i + b
                up(e, b, range(2 * FC))
                down(e, b, i, range(0, 2))
                turn(e + 1, 1 - b, i + b)
                down(e, b, i, range(2, 4))
                if more:
                    table(e + 2)
                pe.wait_ge(s_xe_low, 2 * e + 4)
                down(e, b, i, range(4, NQ)).then_inc(s_down, 1)

            def last_expert(e, b):
                up(e, b, range(FC + 2))
                pe.wait_ge(s_out_weights[b], 16 * (E // 2))
                pe.wait_ge(s_weighed, NQ * e)
                pe.wait_ge(s_hidden, e * 2 * FC + FC)
                for q in range(2):
                    down_tile(b, q, bank(LAST_BANK[q], P)).then_inc(s_down_tile, 1)
                up(e, b, range(FC + 2, 2 * FC))
                pe.wait_ge(s_hidden, (e + 1) * 2 * FC)
                for q in range(2, NQ):
                    down_tile(b, q, bank(LAST_BANK[q], P)).then_inc(s_down_tile, 1)

            keep_clock(WARM["slots"])
            table(0, True)
            keep_clock(WARM["columns"])
            table(1)
            turn(0, 0, 0, True)
            expert(0, 0)
            expert(0, 1)
            with pe.Fori(1, E // 2 - 1) as i:
                for b in range(2):
                    expert(i, b)
            expert(E // 2 - 1, 0, False)
            last_expert(E - 1, 1)


def kernel(L0_attn_x, L0_attn_W_xproj, L0_attn_W_dt, L0_attn_b_dt, L0_attn_A_log, L0_attn_D, L0_ffn_router_weight,
           L0_ffn_ff_pre_act_weight, L0_ffn_gate_weight, L0_ffn_ff_post_act_weight):
    import concourse.bacc as bacc
    from concourse.bass_utils import run_bass_kernel_spmd

    def lay(a):
        return np.ascontiguousarray(a)

    x = np.asarray(L0_attn_x)
    alog = np.asarray(L0_attn_A_log).reshape(NG, GD, NS).transpose(2, 1, 0).reshape(P, NG)
    small = np.concatenate([np.asarray(L0_attn_b_dt)[:, None], alog,
                            np.asarray(L0_ffn_router_weight).T], axis=1)
    arrays = {
        "x": lay(x.reshape(T, D)),
        "wx": lay(np.asarray(L0_attn_W_xproj).T),
        "wdt": lay(np.asarray(L0_attn_W_dt).T),
        "small": lay(small),
        "dskip": lay(np.broadcast_to(np.asarray(L0_attn_D), (P, D))),
        "w1": lay(np.asarray(L0_ffn_ff_pre_act_weight).transpose(0, 2, 1)),
        "wg": lay(np.asarray(L0_ffn_gate_weight).transpose(0, 2, 1)),
        "w2": lay(np.asarray(L0_ffn_ff_post_act_weight).reshape(E, D, FC, P).transpose(0, 3, 2, 1)),
        "consts": shape_constants(),
        "jbits": search_bits(),
    }
    nc = bacc.Bacc("TRN2", target_bir_lowering=False, num_devices=1)
    ap = {k: nc.dram_tensor("in_" + k, a.shape, mybir.dt.from_np(a.dtype), kind="ExternalInput").ap() for k, a in arrays.items()}
    out = nc.dram_tensor("out", [T + CAP, D], F32, kind="ExternalOutput").ap()
    rows = nc.dram_tensor("rows", [T, D], F32, kind="Internal").ap()
    build(nc, ap["x"], ap["wx"], ap["wdt"], ap["small"], ap["dskip"], ap["w1"], ap["wg"], ap["w2"], ap["consts"],
          ap["jbits"], out, rows)
    r = run_bass_kernel_spmd(nc, [{"in_" + k: a for k, a in arrays.items()}], core_ids=[0])
    return r.results[0]["out"][:T].reshape(BATCH, SEQ, D)
```
